# Optimizing a Trainium2 kernel written in Bass

```python
import numpy as np
import jax
import jax.numpy as jnp

def _softmax(x, axis=-1):
    return jax.nn.softmax(x, axis=axis)

def _gelu(x):
    return jax.nn.gelu(x, approximate=True)

def _silu(x):
    return jax.nn.silu(x)

def _sigmoid(x):
    return jax.nn.sigmoid(x)

def _layernorm(x, axis=-1, eps=1e-05):
    m = jnp.mean(x, axis=axis, keepdims=True)
    v = jnp.var(x, axis=axis, keepdims=True)
    return (x - m) / jnp.sqrt(v + eps)

def _scatter_add(tgt, idx, src, axis=0):
    return tgt.at[idx].add(src)

def _segment_sum(src, seg, n):
    return jax.ops.segment_sum(src, seg, n)
kernel_name = 'mk_adj_resnorm_d2_adj_r2_a1091d'

def setup_inputs(seed: int=0):
    np.random.seed(seed)
    _w = jnp.asarray

    def _rec_inputs():
        import jax
        import jax.numpy as jnp
        _gk = jax.random.key(seed)
        x = -0.0004039 + 1 * jax.random.normal(jax.random.fold_in(_gk, 1), (128, 64, 384), jnp.float32)
        _w = (1.0 + jnp.arange(64, dtype=jnp.float32)) ** (-0.5)
        _w = _w / _w.mean()
        _pij = jnp.clip(0.0625 * _w[:, None] * _w[None, :], 0.0, 1.0)
        _a = jax.random.uniform(jax.random.fold_in(_gk, 2), (128, 64, 64)) < _pij
        _af = _a.astype(jnp.float32)
        adj = _af
        return (x, adj)
    x, adj = _rec_inputs()

    def _L0_gnn_setup():
        import jax, jax.numpy as jnp
        import numpy as np
        B, S, H, L = (32, 256, 384, 2)

        def _layer_norm(z, a, b, eps=0.001):
            mu = jnp.mean(z, axis=-1, keepdims=True)
            sigma = jnp.std(z, axis=-1, keepdims=True, ddof=1)
            return (z - mu) / (sigma + eps) * a + b
        key = jax.random.key(seed)
        ks = jax.random.split(key, 6)
        hidden_state = jax.random.normal(ks[0], (B, S, H), dtype=jnp.float32)
        adjacency_matrix = (jax.random.uniform(ks[1], (B, S, S)) < 0.2).astype(jnp.float32)
        W_left = 0.05 * jax.random.normal(ks[2], (L, H, H), dtype=jnp.float32)
        W_right = 0.05 * jax.random.normal(ks[3], (L, H, H), dtype=jnp.float32)
        W_lin = 0.05 * jax.random.normal(ks[4], (L, H, H), dtype=jnp.float32)
        b_lin = jnp.zeros((L, H), dtype=jnp.float32)
        ln_a = jnp.ones((L, H), dtype=jnp.float32)
        ln_b = jnp.zeros((L, H), dtype=jnp.float32)
        return {'hidden_state': hidden_state, 'adjacency_matrix': adjacency_matrix, 'W_left': W_left, 'W_right': W_right, 'W_lin': W_lin, 'b_lin': b_lin, 'ln_a': ln_a, 'ln_b': ln_b}
    _L0_gnn_all = _L0_gnn_setup()
    _L0_gnn_in = {k: v for k, v in _L0_gnn_all.items() if k in ('W_left', 'W_right', 'W_lin', 'b_lin', 'ln_a', 'ln_b')}
    del _L0_gnn_all

    def _L1_gnn_setup():
        import jax, jax.numpy as jnp
        import numpy as np
        LN_EPS = 1e-12

        def _digcn_forward(hidden_state, adjacency_matrix, Wl, bl, Ws, bs, Wr, br, ln_w, ln_b):
            B, S, D = hidden_state.shape
            temper = jnp.asarray(D, jnp.float32) ** 0.5
            i = jnp.arange(S)
            upper = (i[None, :] > i[:, None]).astype(hidden_state.dtype)
            lower = (i[None, :] < i[:, None]).astype(hidden_state.dtype)

            def layer(h, params):
                wl, b_l, ws, b_s, wr, b_r, g, beta = params
                u = jnp.einsum('bid,bjd->bij', h, h) / temper
                a = jax.nn.softmax(u, axis=-1)
                delta = a * adjacency_matrix
                attn = delta / (jnp.sum(delta, axis=-1, keepdims=True) + 1e-10)
                hl = h @ wl.T + b_l
                hs = h @ ws.T + b_s
                hr = h @ wr.T + b_r
                diag_a = jnp.diagonal(attn, axis1=1, axis2=2)
                ctx = jnp.einsum('bij,bjd->bid', attn * upper, hl) + diag_a[..., None] * hs + jnp.einsum('bij,bjd->bid', attn * lower, hr)
                mean = ctx.mean(-1, keepdims=True)
                var = ctx.var(-1, keepdims=True)
                o = (ctx - mean) / jnp.sqrt(var + LN_EPS) * g + beta
                return (jax.nn.relu(o), None)
            out, _ = jax.lax.scan(layer, hidden_state, (Wl, bl, Ws, bs, Wr, br, ln_w, ln_b))
            return out
        key = jax.random.key(seed)
        ks = jax.random.split(key, 6)
        B, S, D, L = (8, 512, 384, 2)
        scale = (1.0 / D) ** 0.5
        hidden_state = jax.random.normal(ks[0], (B, S, D), jnp.float32)
        adjacency_matrix = (jax.random.uniform(ks[1], (B, S, S)) < 0.05).astype(jnp.float32)
        Wl = jax.random.normal(ks[2], (L, D, D), jnp.float32) * scale
        Ws = jax.random.normal(ks[3], (L, D, D), jnp.float32) * scale
        Wr = jax.random.normal(ks[4], (L, D, D), jnp.float32) * scale
        bl = jnp.zeros((L, D), jnp.float32)
        bs = jnp.zeros((L, D), jnp.float32)
        br = jnp.zeros((L, D), jnp.float32)
        ln_w = jnp.ones((L, D), jnp.float32)
        ln_b = jnp.zeros((L, D), jnp.float32)
        return dict(hidden_state=hidden_state, adjacency_matrix=adjacency_matrix, Wl=Wl, bl=bl, Ws=Ws, bs=bs, Wr=Wr, br=br, ln_w=ln_w, ln_b=ln_b)
    _L1_gnn_all = _L1_gnn_setup()
    _L1_gnn_in = {k: v for k, v in _L1_gnn_all.items() if k in ('Wl', 'bl', 'Ws', 'bs', 'Wr', 'br', 'ln_w', 'ln_b')}
    del _L1_gnn_all
    return {'x': x, 'adj': adj, 'L0_gnn_W_left': _L0_gnn_in['W_left'], 'L0_gnn_W_right': _L0_gnn_in['W_right'], 'L0_gnn_W_lin': _L0_gnn_in['W_lin'], 'L0_gnn_b_lin': _L0_gnn_in['b_lin'], 'L0_gnn_ln_a': _L0_gnn_in['ln_a'], 'L0_gnn_ln_b': _L0_gnn_in['ln_b'], 'L1_gnn_Wl': _L1_gnn_in['Wl'], 'L1_gnn_bl': _L1_gnn_in['bl'], 'L1_gnn_Ws': _L1_gnn_in['Ws'], 'L1_gnn_bs': _L1_gnn_in['bs'], 'L1_gnn_Wr': _L1_gnn_in['Wr'], 'L1_gnn_br': _L1_gnn_in['br'], 'L1_gnn_ln_w': _L1_gnn_in['ln_w'], 'L1_gnn_ln_b': _L1_gnn_in['ln_b']}

def reference(x, adj, L0_gnn_W_left, L0_gnn_W_right, L0_gnn_W_lin, L0_gnn_b_lin, L0_gnn_ln_a, L0_gnn_ln_b, L1_gnn_Wl, L1_gnn_bl, L1_gnn_Ws, L1_gnn_bs, L1_gnn_Wr, L1_gnn_br, L1_gnn_ln_w, L1_gnn_ln_b):
    import jax
    import jax.numpy as jnp

    def _L0_gnn_ref(hidden_state, adjacency_matrix, W_left, W_right, W_lin, b_lin, ln_a, ln_b):
        import jax, jax.numpy as jnp
        import numpy as np
        B, S, H, L = (32, 256, 384, 2)

        def _layer_norm(z, a, b, eps=0.001):
            mu = jnp.mean(z, axis=-1, keepdims=True)
            sigma = jnp.std(z, axis=-1, keepdims=True, ddof=1)
            return (z - mu) / (sigma + eps) * a + b
        temper = float(np.sqrt(H))
        adj = adjacency_matrix
        adj_tri = jnp.triu(adj, k=1)
        diag_mask = jnp.triu(adj, k=0) - adj_tri
        h = hidden_state
        for l in range(L):
            m_left = jnp.einsum('bsh,oh->bso', h, W_left[l])
            m_right = jnp.einsum('bsh,oh->bso', h, W_right[l])
            u_left = jnp.einsum('bih,bjh->bij', h, m_left) / temper
            u_right = jnp.einsum('bih,bjh->bij', h, m_right) / temper
            u = u_left * adj_tri + u_left * diag_mask + u_right * jnp.swapaxes(adj_tri, 1, 2)
            delta_exp_u = jnp.exp(u) * adj
            attention = delta_exp_u / (jnp.sum(delta_exp_u, axis=2, keepdims=True) + 1e-10)
            h_lin = jnp.einsum('bsh,oh->bso', h, W_lin[l]) + b_lin[l]
            ctx = jnp.matmul(attention, h_lin)
            h = jax.nn.relu(_layer_norm(ctx, ln_a[l], ln_b[l]))
        return h

    def _L1_gnn_ref(hidden_state, adjacency_matrix, Wl, bl, Ws, bs, Wr, br, ln_w, ln_b):
        import jax, jax.numpy as jnp
        import numpy as np
        LN_EPS = 1e-12

        def _digcn_forward(hidden_state, adjacency_matrix, Wl, bl, Ws, bs, Wr, br, ln_w, ln_b):
            B, S, D = hidden_state.shape
            temper = jnp.asarray(D, jnp.float32) ** 0.5
            i = jnp.arange(S)
            upper = (i[None, :] > i[:, None]).astype(hidden_state.dtype)
            lower = (i[None, :] < i[:, None]).astype(hidden_state.dtype)

            def layer(h, params):
                wl, b_l, ws, b_s, wr, b_r, g, beta = params
                u = jnp.einsum('bid,bjd->bij', h, h) / temper
                a = jax.nn.softmax(u, axis=-1)
                delta = a * adjacency_matrix
                attn = delta / (jnp.sum(delta, axis=-1, keepdims=True) + 1e-10)
                hl = h @ wl.T + b_l
                hs = h @ ws.T + b_s
                hr = h @ wr.T + b_r
                diag_a = jnp.diagonal(attn, axis1=1, axis2=2)
                ctx = jnp.einsum('bij,bjd->bid', attn * upper, hl) + diag_a[..., None] * hs + jnp.einsum('bij,bjd->bid', attn * lower, hr)
                mean = ctx.mean(-1, keepdims=True)
                var = ctx.var(-1, keepdims=True)
                o = (ctx - mean) / jnp.sqrt(var + LN_EPS) * g + beta
                return (jax.nn.relu(o), None)
            out, _ = jax.lax.scan(layer, hidden_state, (Wl, bl, Ws, bs, Wr, br, ln_w, ln_b))
            return out
        return _digcn_forward(hidden_state, adjacency_matrix, Wl, bl, Ws, bs, Wr, br, ln_w, ln_b)
    x = _layernorm(x + _L0_gnn_ref(x, adj, L0_gnn_W_left, L0_gnn_W_right, L0_gnn_W_lin, L0_gnn_b_lin, L0_gnn_ln_a, L0_gnn_ln_b), axis=-1)
    x = _layernorm(x + _L1_gnn_ref(x, adj, L1_gnn_Wl, L1_gnn_bl, L1_gnn_Ws, L1_gnn_bs, L1_gnn_Wr, L1_gnn_br, L1_gnn_ln_w, L1_gnn_ln_b), axis=-1)
    return x

_drawn_inputs = setup_inputs


def setup_inputs(seed=0):
    import zlib

    import numpy as np

    out = dict(_drawn_inputs(seed))
    spreads = {'L0_gnn_b_lin': (0.0, 0.1),
     'L0_gnn_ln_a': (1.0, 0.2),
     'L0_gnn_ln_b': (0.0, 0.1),
     'L1_gnn_bl': (0.0, 0.1),
     'L1_gnn_bs': (0.0, 0.1),
     'L1_gnn_br': (0.0, 0.1),
     'L1_gnn_ln_w': (1.0, 0.2),
     'L1_gnn_ln_b': (0.0, 0.1)}
    factors = {}
    for name, (base, spread) in spreads.items():
        noise = np.random.default_rng([zlib.crc32(name.encode()), seed]).standard_normal(out[name].shape)
        drawn = base * np.exp(spread * noise) if base else spread * noise
        out[name] = jnp.asarray(drawn.astype(out[name].dtype))
    for name, factor in factors.items():
        out[name] = (out[name] * factor).astype(out[name].dtype)
    return out
```

```python
from contextlib import ExitStack

import numpy as np

import concourse.bass as bass
from concourse import mybir

ALU = mybir.AluOpType
ACT = mybir.ActivationFunctionType
AX = mybir.AxisListType
F32 = mybir.dt.float32
F32R = mybir.dt.float32r
BF16 = mybir.dt.bfloat16

P = 128
NT = 4
TOK = NT * P
STREAMS = 2
UNITS = 4
BIG = 1e30

C_EYE, C_LE, C_GT, C_LT, C_SEL, C_ROWS, C_COLS = 0, 128, 256, 384, 512, 1024, 1152
C_ALL = 1664


def constants_table():
    c = np.zeros((P, C_ALL), np.float32)
    j, i = np.arange(P)[:, None], np.arange(P)[None, :]
    c[:, C_EYE:C_EYE + P] = i == j
    c[:, C_LE:C_LE + P] = i <= j
    c[:, C_GT:C_GT + P] = i > j
    c[:, C_LT:C_LT + P] = i < j
    for t in range(NT):
        c[t, C_SEL + t * P:C_SEL + (t + 1) * P] = 1.0
    second = (np.arange(P) >= P // 2).astype(np.float32)
    c[0, C_ROWS:C_ROWS + P] = 1 - second
    c[1, C_ROWS:C_ROWS + P] = second
    c[0, C_COLS:C_COLS + TOK] = np.tile(-BIG * second, NT)
    c[1, C_COLS:C_COLS + TOK] = np.tile(-BIG * (1 - second), NT)
    return c


def nth(i, unit, per, k):
    return i * (UNITS * per) + (unit * per + k + 1)


def wait(eng, sem, value):
    if isinstance(value, int) and value <= 0:
        return
    eng.wait_ge(sem, value)


class Common:

    def __init__(self, H):
        self.H = H
        self.KO = H // P
        self.HC = H + 2


def three_products(H_hi, H_lo, W_hi, W_lo):
    return ((H_hi, W_hi), (H_hi, W_lo), (H_lo, W_hi))


def gated_layers(nc, cm, x, adj, adj_t, w_left, w_right, w_lin_t, b_lin, ln_a, ln_b, table, x1):
    H, KO, HC = cm.H, cm.KO, cm.HC
    LAYERS = w_left.shape[0]
    B = x.shape[0]
    PASSES = B * x.shape[1] // (TOK * STREAMS)
    SCALE = float(H) ** -0.5
    EPS = 1e-3
    QB, VB = 2 * KO, NT
    WN = QB + 2 * NT
    RING = 4
    assert LAYERS == 2 and WN * UNITS % RING == 0 and UNITS * KO % 2 == 0

    x_v = x.rearrange("a n h -> (a n) h").rearrange("(i s t p) h -> i s p t h", s=STREAMS, t=NT, p=P)
    x1_v = x1.rearrange("(i s t p) h -> i s p t h", s=STREAMS, t=NT, p=P)
    adj_v = adj.rearrange("(i s t b) r c -> i s b r t c", s=STREAMS, t=NT, b=2)
    adj_t_v = adj_t.rearrange("(i s t b) r c -> i s b r t c", s=STREAMS, t=NT, b=2)

    with ExitStack() as ctx:
        def sb(name, shape, dt=F32):
            return ctx.enter_context(nc.sbuf_tensor("g_" + name, shape, dt))

        def sem(name):
            return ctx.enter_context(nc.semaphore("g_" + name))

        const = sb("const", [P, C_SEL])
        stage = [sb(f"stage{n}", [P, KO, H]) for n in range(2)]
        wq_hi = sb("wq_hi", [P, LAYERS, 2, KO, H], F32R)
        wq_lo = sb("wq_lo", [P, LAYERS, 2, KO, H], F32R)
        wv_hi = sb("wv_hi", [P, LAYERS, KO, H], F32R)
        wv_lo = sb("wv_lo", [P, LAYERS, KO, H], F32R)
        bias = sb("bias", [P, LAYERS, H])
        gain_f = sb("gain_f", [P, KO])
        shift_f = sb("shift_f", [P, KO])
        gain = sb("gain", [P, H])
        shift = sb("shift", [P, H])
        powers = sb("powers", [P, 2, NT])
        x_in = [sb(f"x_in{s}", [P, NT, H]) for s in range(STREAMS)]
        x_res = [sb(f"x_res{s}", [P, NT, H]) for s in range(STREAMS)]
        z = [sb(f"z{s}", [P, NT, HC]) for s in range(STREAMS)]
        ht_hi = [sb(f"ht_hi{s}", [P, KO, TOK], F32R) for s in range(STREAMS)]
        ht_lo = [sb(f"ht_lo{s}", [P, KO, TOK], F32R) for s in range(STREAMS)]
        a_nat = [sb(f"a_nat{s}", [P, NT, P]) for s in range(STREAMS)]
        a_tr = [sb(f"a_tr{s}", [P, NT, P]) for s in range(STREAMS)]
        keep_l = [sb(f"keep_l{s}", [P, NT, P]) for s in range(STREAMS)]
        ht_full = sb("ht_full", [P, KO, TOK])
        qv_hi = sb("qv_hi", [P, KO * 2 * TOK], F32R)
        qv_lo = sb("qv_lo", [P, KO * 2 * TOK], F32R)
        v_full = sb("v_full", [P, NT, H])
        score_l = sb("score_l", [P, NT, P])
        score_r = sb("score_r", [P, NT, P])
        prob = sb("prob", [P, NT, P])
        prob_hi = sb("prob_hi", [P, NT, P], F32R)
        prob_lo = sb("prob_lo", [P, NT, P], F32R)
        stats = sb("stats", [P, NT, 6])
        mv = sb("mv", [P, NT, 2])
        var = sb("var", [P, NT])
        sigma = sb("sigma", [P, NT])
        denom = sb("denom", [P, NT])
        rstd = sb("rstd", [P, NT])
        fstats = sb("fstats", [P, NT, 6])
        fmv = sb("fmv", [P, NT, 2])
        fvar = sb("fvar", [P, NT])
        frstd = sb("frstd", [P, NT])

        work = [ctx.enter_context(nc.psum_tensor(f"g_work{n}", [P, 512], F32)) for n in range(RING)]
        turn = [ctx.enter_context(nc.psum_tensor(f"g_turn{n}", [P, 512], F32)) for n in range(2)]
        score_ps = ctx.enter_context(nc.psum_tensor("g_score_ps", [P, NT, 2, P], F32))

        eye = const[:, C_EYE:C_EYE + P]
        q_hi = qv_hi[:].rearrange("p (m t d i) -> p m t d i", m=KO, t=NT, d=2)
        q_lo = qv_lo[:].rearrange("p (m t d i) -> p m t d i", m=KO, t=NT, d=2)
        v_hi = qv_hi[:, 0:NT * HC].rearrange("p (t h) -> p t h", t=NT)
        v_lo = qv_lo[:, 0:NT * HC].rearrange("p (t h) -> p t h", t=NT)

        const_in, bias_in = sem("const_in"), sem("bias_in")
        stage_in = [sem(f"stage_in{n}") for n in range(2)]
        stage_split = sem("stage_split")
        stage_half = sem("stage_half")
        x_loaded = [sem(f"x_loaded{s}") for s in range(STREAMS)]
        x_copied = [sem(f"x_copied{s}") for s in range(STREAMS)]
        adj_loaded = [sem(f"adj_loaded{s}") for s in range(STREAMS)]
        stored = [sem(f"stored{s}") for s in range(STREAMS)]
        cleared, powers_set = sem("cleared"), sem("powers_set")
        keep_ready = [sem(f"keep_ready{s}") for s in range(STREAMS)]
        turned, turn_read, ht_ready = sem("turned"), sem("turn_read"), sem("ht_ready")
        work_full, work_free = sem("work_full"), sem("work_free")
        q_hi_ready, score_full, masked, score_ready = sem("q_hi_ready"), sem("score_full"), sem("masked"), sem("score_ready")
        exp_ready, prob_ready, prob_hi_ready, prob_lo_ready = sem("exp_ready"), sem("prob_ready"), sem("prob_hi_ready"), sem("prob_lo_ready")
        v_hi_ready, v_lo_ready, ones_set = sem("v_hi_ready"), sem("v_lo_ready"), sem("ones_set")
        ctx_ready = sem("ctx_ready")
        mean_ready, var_ready, sigma_ready = sem("mean_ready"), sem("var_ready"), sem("sigma_ready")
        denom_ready, rstd_ready, z_ready = sem("denom_ready"), sem("rstd_ready"), sem("z_ready")
        centred, scaled, summed, fstats_ready = sem("centred"), sem("scaled"), sem("summed"), sem("fstats_ready")
        fmean_ready, fvar_ready, frstd_ready, x1_ready = sem("fmean_ready"), sem("fvar_ready"), sem("frstd_ready"), sem("x1_ready")

        block = ctx.enter_context(nc.Block())

        @block.sync
        def _(sp):
            def load_x(i, s):
                sp.dma_start(x_in[s][:], x_v[i, s]).then_inc(x_loaded[s], 16)

            def load_adj(i, s):
                for b in range(2):
                    h = slice(b * 64, b * 64 + 64)
                    sp.dma_start(a_tr[s][h, :, h], adj_t_v[i, s, b]).then_inc(adj_loaded[s], 16)
                    sp.dma_start(a_nat[s][h, :, h], adj_v[i, s, b]).then_inc(adj_loaded[s], 16)

            sp.dma_start(const[:], table[:, 0:C_SEL]).then_inc(const_in, 16)
            load_x(0, 0)
            weights = [w for l in range(LAYERS) for w in (w_left[l], w_right[l], w_lin_t[l])]
            for n, w in enumerate(weights):
                if n >= 2:
                    sp.wait_ge(stage_split, n - 1)
                sp.dma_start(stage[n % 2][:], w.rearrange("(k p) o -> p k o", p=P)).then_inc(stage_in[n % 2], 16)
                if n == 1:
                    sp.wait_ge(cleared, 4)
                    load_adj(0, 0)
                    sp.dma_start(bias[:], b_lin.partition_broadcast(P)).then_inc(bias_in, 16)
                    sp.dma_start(gain_f[:], ln_a[0].rearrange("(k p) -> p k", p=P),
                                 allow_slow_non_contiguous=True).then_inc(bias_in, 16)
                    sp.dma_start(shift_f[:], ln_b[0].rearrange("(k p) -> p k", p=P),
                                 allow_slow_non_contiguous=True).then_inc(bias_in, 16)
                    sp.dma_start(gain[:], ln_a[1].partition_broadcast(P)).then_inc(bias_in, 16)
                    sp.dma_start(shift[:], ln_b[1].partition_broadcast(P)).then_inc(bias_in, 16)
                    load_x(0, 1)
                    load_adj(0, 1)

            def one_pass(i, last):
                for s in range(STREAMS):
                    sp.wait_ge(x_loaded[s], 16 * (i + 1))
                    wait(sp, summed, i * (STREAMS * NT) + (s + 1 - STREAMS) * NT)
                    sp.dma_start(x_res[s][:], x_in[s][:]).then_inc(x_copied[s], 16)
                    if not last:
                        sp.wait_ge(turned, nth(i, s, KO, KO - 1))
                        sp.wait_ge(x_copied[s], 16 * (i + 1))
                        load_x(i + 1, s)
                for s in range(STREAMS):
                    if not last:
                        sp.wait_ge(prob_ready, nth(i, 2 + s, 1, 0))
                        load_adj(i + 1, s)
                    sp.wait_ge(x1_ready, i * (STREAMS * NT) + NT * (s + 1))
                    sp.dma_start(x1_v[i, s], z[s][:, :, 0:H]).then_inc(stored[s], 16)

            one_pass(0, False)
            with sp.Fori(1, PASSES - 1) as i:
                one_pass(i, False)
            one_pass(PASSES - 1, True)
            for s in range(STREAMS):
                sp.wait_ge(stored[s], 16 * (PASSES + 1))

        @block.tensor
        def _(pe):
            def turn_tokens(i, unit):
                layer, s = divmod(unit % UNITS, STREAMS)
                src = x_in[s] if layer == 0 else z[s]
                if layer == 0:
                    pe.wait_ge(x_loaded[s], i * 16 + 16 * (unit // UNITS + 1))
                else:
                    pe.wait_ge(z_ready, i * (STREAMS * NT) + NT * (s + 1))
                for k in range(KO):
                    wait(pe, turn_read, nth(i, unit, KO, k - 2))
                    bank = turn[(unit * KO + k) % 2]
                    for t in range(NT):
                        mm = pe.transpose(bank[:, t * P:(t + 1) * P], src[:, t, k * P:(k + 1) * P], eye)
                    mm.then_inc(turned, 1)

            def work_bank(i, unit, j):
                wait(pe, work_free, nth(i, unit, WN, j - RING))
                return work[(unit * WN + j) % RING]

            def queries(i, unit):
                layer, s = divmod(unit % UNITS, STREAMS)
                pe.wait_ge(ht_ready, nth(i, unit, KO, KO - 1))
                for d in range(2):
                    pe.wait_ge(stage_split, 3 * layer + d + 1)
                    for m in range(KO):
                        bank = work_bank(i, unit, d * KO + m)
                        pairs = [(w[:, layer, d, k, m * P:(m + 1) * P], h[s][:, k, :])
                                 for k in range(KO) for w, h in three_products(wq_hi, wq_lo, ht_hi, ht_lo)]
                        for n, (w, h) in enumerate(pairs):
                            mm = pe.matmul(bank[:], w, h, start=(n == 0), stop=(n == len(pairs) - 1))
                        mm.then_inc(work_full, 1)

            def scores(i, unit):
                s = unit % STREAMS
                pe.wait_ge(work_free, nth(i, unit, WN, QB - 1))
                wait(pe, score_ready, nth(i, unit, 1, -1))
                for t in range(NT):
                    pairs = [(h[s][:, m, t * P:(t + 1) * P], q[:, m, t, :, :])
                             for m in range(KO) for h, q in three_products(ht_hi, ht_lo, q_hi, q_lo)]
                    for n, (h, q) in enumerate(pairs):
                        mm = pe.matmul(score_ps[:, t, :, :], h, q, start=(n == 0), stop=(n == len(pairs) - 1))
                mm.then_inc(score_full, 1)

            def values(i, unit):
                layer, s = divmod(unit, STREAMS)
                pe.wait_ge(stage_split, 3 * layer + 3)
                for t in range(NT):
                    bank = work_bank(i, unit, QB + t)
                    pairs = [(h[s][:, k, t * P:(t + 1) * P], w[:, layer, k, :])
                             for k in range(KO) for h, w in three_products(ht_hi, ht_lo, wv_hi, wv_lo)]
                    for n, (h, w) in enumerate(pairs):
                        mm = pe.matmul(bank[:, 0:H], h, w, start=(n == 0), stop=(n == len(pairs) - 1))
                    mm.then_inc(work_full, 1)

            def contexts(i, unit):
                pe.wait_ge(prob_lo_ready, nth(i, unit, 1, 0))
                pe.wait_ge(ones_set, nth(i, unit, 1, 0))
                for t in range(NT):
                    pe.wait_ge(v_lo_ready, nth(i, unit, NT, t))
                    bank = work_bank(i, unit, QB + VB + t)
                    for n, (p, v) in enumerate(three_products(prob_hi, prob_lo, v_hi, v_lo)):
                        mm = pe.matmul(bank[:, 0:HC], p[:, t, :], v[:, t, :], start=(n == 0), stop=(n == 2))
                    mm.then_inc(work_full, 1)

            def one_pass(i, last):
                for unit in range(UNITS):
                    more = not (last and unit == UNITS - 1)
                    if more:
                        turn_tokens(i, unit + 1)
                    values(i, unit)
                    contexts(i, unit)
                    if more:
                        queries(i, unit + 1)
                        scores(i, unit + 1)

            pe.wait_ge(const_in, 16)
            turn_tokens(0, 0)
            queries(0, 0)
            scores(0, 0)
            with pe.Fori(0, PASSES - 1) as i:
                one_pass(i, False)
            one_pass(PASSES - 1, True)

        @block.scalar
        def _(act):
            def turn_out(i, unit, k):
                layer, s = divmod(unit % UNITS, STREAMS)
                act.wait_ge(turned, nth(i, unit, KO, k))
                wait(act, ht_ready, nth(i, unit, KO, k - KO))
                bank = turn[(unit * KO + k) % 2]
                for out in (ht_full[:, k, :], ht_hi[s][:, k, :]):
                    if layer == 0:
                        op = nc.scalar.activation(out, bank[:], ACT.Copy)
                    else:
                        op = nc.scalar.activation(out, bank[:], ACT.Relu, bias=shift_f[:, k:k + 1],
                                                  scale=gain_f[:, k:k + 1])
                op.then_inc(turn_read, 1)

            def queries_hi(i, unit):
                for j in range(QB):
                    d, m = divmod(j, KO)
                    act.wait_ge(work_full, nth(i, unit, WN, j))
                    nc.scalar.activation(q_hi[:, m, :, d, :], work[(unit * WN + j) % RING][:], ACT.Copy)\
                        .then_inc(q_hi_ready, 1)

            def exponentials(i, unit):
                act.wait_ge(score_ready, nth(i, unit, 1, 0))
                nc.scalar.activation(prob[:], score_l[:], ACT.Exp, scale=SCALE).then_inc(exp_ready, 1)

            def probabilities_hi(i, unit):
                act.wait_ge(prob_ready, nth(i, unit, 1, 0))
                nc.scalar.activation(prob_hi[:], prob[:], ACT.Copy).then_inc(prob_hi_ready, 1)

            def values_hi(i, unit):
                for t in range(NT):
                    act.wait_ge(work_free, nth(i, unit, WN, QB + t))
                    nc.scalar.activation(v_hi[:, t, 0:H], v_full[:, t, :], ACT.Copy).then_inc(v_hi_ready, 1)

            def contexts_out(i, unit):
                layer, s = divmod(unit, STREAMS)
                if layer == 0:
                    act.wait_ge(stored[s], 16 * (i + 1))
                for t in range(NT):
                    j = QB + VB + t
                    act.wait_ge(work_full, nth(i, unit, WN, j))
                    nc.scalar.activation(z[s][:, t, :], work[(unit * WN + j) % RING][:, 0:HC], ACT.Copy)\
                        .then_inc(ctx_ready, 1)

            def one_pass(i, last):
                for unit in range(UNITS):
                    more = not (last and unit == UNITS - 1)
                    if more:
                        turn_out(i, unit + 1, 0)
                    exponentials(i, unit)
                    if more:
                        turn_out(i, unit + 1, 1)
                    probabilities_hi(i, unit)
                    if more:
                        turn_out(i, unit + 1, 2)
                    values_hi(i, unit)
                    contexts_out(i, unit)
                    if more:
                        queries_hi(i, unit + 1)

            for k in range(KO):
                turn_out(0, 0, k)
            queries_hi(0, 0)
            act.wait_ge(bias_in, 16 * 5)
            with act.Fori(0, PASSES - 1) as i:
                one_pass(i, False)
            one_pass(PASSES - 1, True)

        @block.gpsimd
        def _(pool):
            def keep_masks(i, s):
                pool.wait_ge(adj_loaded[s], 64 * (i + 1))
                tri = [const[:, c:c + P].unsqueeze(1).to_broadcast([P, NT, P]) for c in (C_LE, C_GT)]
                nc.gpsimd.tensor_tensor(keep_l[s][:], a_tr[s][:], tri[0], ALU.mult)
                nc.gpsimd.tensor_tensor(a_nat[s][:], a_nat[s][:], tri[1], ALU.mult).then_inc(keep_ready[s], 1)

            def values_lo(i, unit):
                for t in range(NT):
                    pool.wait_ge(v_hi_ready, nth(i, unit, NT, t))
                    nc.gpsimd.tensor_tensor(v_lo[:, t, 0:H], v_full[:, t, :], v_hi[:, t, 0:H].bitcast(F32),
                                            ALU.subtract).then_inc(v_lo_ready, 1)
                    if t == 0:
                        nc.gpsimd.memset(v_hi[:, :, H:HC].bitcast(F32), 1.0)
                        nc.gpsimd.memset(v_lo[:, :, H:HC].bitcast(F32), 0.0).then_inc(ones_set, 1)

            def roots(i, unit):
                pool.wait_ge(var_ready, nth(i, unit, 1, 0))
                nc.gpsimd.tensor_tensor(sigma[:], var[:], powers[:, 0, :], ALU.pow).then_inc(sigma_ready, 1)
                if unit >= STREAMS:
                    pool.wait_ge(fvar_ready, i * STREAMS + unit - 1)
                    nc.gpsimd.tensor_tensor(frstd[:], fvar[:], powers[:, 1, :], ALU.pow).then_inc(frstd_ready, 1)

            def one_pass(i, last):
                for unit in range(UNITS):
                    values_lo(i, unit)
                    if unit == 0:
                        keep_masks(i, 1)
                    if unit == UNITS - 1 and not last:
                        keep_masks(i + 1, 0)
                    roots(i, unit)

            for s in range(STREAMS):
                nc.gpsimd.memset(a_tr[s][:], 0.0).then_inc(cleared, 1)
                nc.gpsimd.memset(z[s][:, 0, 0:1], 0.0).then_inc(stored[s], 16)
                nc.gpsimd.memset(a_nat[s][:], 0.0).then_inc(cleared, 1)
            nc.gpsimd.memset(powers[:, 0, :], 0.5)
            nc.gpsimd.memset(powers[:, 1, :], -0.5).then_inc(powers_set, 1)
            pool.wait_ge(powers_set, 1)
            pool.wait_ge(const_in, 16)
            keep_masks(0, 0)
            with pool.Fori(0, PASSES - 1) as i:
                one_pass(i, False)
            one_pass(PASSES - 1, True)

        @block.vector
        def _(dve):
            def split_weight(n):
                layer, which = divmod(n, 3)
                hi, lo = ((wq_hi[:, layer, which], wq_lo[:, layer, which]) if which < 2
                          else (wv_hi[:, layer], wv_lo[:, layer]))
                dve.wait_ge(stage_in[n % 2], 16 * (n // 2 + 1))
                nc.vector.tensor_copy(hi, stage[n % 2][:]).then_inc(stage_half, 1)
                dve.wait_ge(stage_half, n + 1)
                nc.vector.tensor_tensor(lo, stage[n % 2][:], hi.bitcast(F32), ALU.subtract)\
                    .then_inc(stage_split, 1)

            def turn_lo(i, unit, k):
                s = unit % STREAMS
                dve.wait_ge(turn_read, nth(i, unit, KO, k))
                nc.vector.tensor_tensor(ht_lo[s][:, k, :], ht_full[:, k, :], ht_hi[s][:, k, :].bitcast(F32),
                                        ALU.subtract).then_inc(ht_ready, 1)

            def query_lo(i, unit, j):
                d, m = divmod(j, KO)
                dve.wait_ge(q_hi_ready, nth(i, unit, QB, j))
                bank = work[(unit * WN + j) % RING][:].rearrange("p (t i) -> p t i", t=NT)
                nc.vector.tensor_tensor(q_lo[:, m, :, d, :], bank, q_hi[:, m, :, d, :].bitcast(F32),
                                        ALU.subtract).then_inc(work_free, 1)

            def mask_scores(i, unit):
                s = unit % STREAMS
                dve.wait_ge(score_full, nth(i, unit, 1, 0))
                if unit < STREAMS:
                    dve.wait_ge(keep_ready[s], i + 1)
                nc.vector.tensor_tensor(score_l[:], score_ps[:, :, 0, :], keep_l[s][:], ALU.mult)
                nc.vector.tensor_tensor(score_r[:], score_ps[:, :, 1, :], a_nat[s][:], ALU.mult).then_inc(masked, 1)
                dve.wait_ge(masked, nth(i, unit, 1, 0))
                nc.vector.tensor_tensor(score_l[:], score_l[:], score_r[:], ALU.add).then_inc(score_ready, 1)

            def probabilities(i, unit):
                s = unit % STREAMS
                dve.wait_ge(exp_ready, nth(i, unit, 1, 0))
                nc.vector.tensor_tensor(prob[:], prob[:], a_tr[s][:], ALU.mult).then_inc(prob_ready, 1)

            def probabilities_lo(i, unit):
                dve.wait_ge(prob_hi_ready, nth(i, unit, 1, 0))
                nc.vector.tensor_tensor(prob_lo[:], prob[:], prob_hi[:].bitcast(F32), ALU.subtract)\
                    .then_inc(prob_lo_ready, 1)

            def biased_values(i, unit):
                layer = unit // STREAMS
                for t in range(NT):
                    j = QB + t
                    dve.wait_ge(work_full, nth(i, unit, WN, j))
                    nc.vector.tensor_tensor(v_full[:, t, :], work[(unit * WN + j) % RING][:, 0:H],
                                            bias[:, layer, :], ALU.add).then_inc(work_free, 1)

            def context_stats(i, unit):
                for t in range(NT):
                    dve.wait_ge(ctx_ready, nth(i, unit, NT, t))
                    nc.vector.bn_stats(stats[:, t, :], work[(unit * WN + QB + VB + t) % RING][:, 0:H])\
                        .then_inc(work_free, 1)

            def normalise(i, unit):
                layer, s = divmod(unit, STREAMS)
                dve.wait_ge(work_free, nth(i, unit, WN, WN - 1))
                nc.vector.tensor_scalar(denom[:], z[s][:, :, H], 1e-10, EPS, ALU.add, ALU.mult)
                for t in range(NT):
                    op = nc.vector.bn_aggr(mv[:, t, :], stats[:, t, :])
                op.then_inc(mean_ready, 1)
                dve.wait_ge(mean_ready, nth(i, unit, 1, 0))
                nc.vector.tensor_scalar(var[:], mv[:, :, 1], float(H) / (H - 1), None, ALU.mult)\
                    .then_inc(var_ready, 1)
                dve.wait_ge(sigma_ready, nth(i, unit, 1, 0))
                nc.vector.tensor_tensor(denom[:], denom[:], sigma[:], ALU.add).then_inc(denom_ready, 1)
                dve.wait_ge(denom_ready, nth(i, unit, 1, 0))
                nc.vector.reciprocal(rstd[:], denom[:]).then_inc(rstd_ready, 1)
                dve.wait_ge(rstd_ready, nth(i, unit, 1, 0))
                if layer == 0:
                    for t in range(NT):
                        nc.vector.tensor_scalar(z[s][:, t, 0:H], z[s][:, t, 0:H], mv[:, t, 0:1],
                                                rstd[:, t:t + 1], ALU.subtract, ALU.mult).then_inc(z_ready, 1)

            def centre(i, s):
                for t in range(NT):
                    nc.vector.scalar_tensor_tensor(z[s][:, t, 0:H], z[s][:, t, 0:H], mv[:, t, 0:1], gain[:],
                                                   ALU.subtract, ALU.mult).then_inc(centred, 1)

            def scale_shift(i, s):
                for t in range(NT):
                    dve.wait_ge(centred, i * (STREAMS * NT) + s * NT + t + 1)
                    nc.vector.scalar_tensor_tensor(z[s][:, t, 0:H], z[s][:, t, 0:H], rstd[:, t:t + 1], shift[:],
                                                   ALU.mult, ALU.add).then_inc(scaled, 1)

            def add_residual(i, s):
                dve.wait_ge(x_copied[s], 16 * (i + 1))
                for t in range(NT):
                    dve.wait_ge(scaled, i * (STREAMS * NT) + s * NT + t + 1)
                    nc.vector.scalar_tensor_tensor(z[s][:, t, 0:H], z[s][:, t, 0:H], 0.0, x_res[s][:, t, :],
                                                   ALU.max, ALU.add).then_inc(summed, 1)

            def final_stats(i, s):
                for t in range(NT):
                    dve.wait_ge(summed, i * (STREAMS * NT) + s * NT + t + 1)
                    nc.vector.bn_stats(fstats[:, t, :], z[s][:, t, 0:H]).then_inc(fstats_ready, 1)

            def final_var(i, s):
                dve.wait_ge(fstats_ready, i * (STREAMS * NT) + (s + 1) * NT)
                nc.vector.memset(fvar[:], 1e-5)
                for t in range(NT):
                    op = nc.vector.bn_aggr(fmv[:, t, :], fstats[:, t, :])
                op.then_inc(fmean_ready, 1)
                dve.wait_ge(fmean_ready, i * STREAMS + s + 1)
                nc.vector.tensor_tensor(fvar[:], fvar[:], fmv[:, :, 1], ALU.add).then_inc(fvar_ready, 1)

            def final_scale(i, s):
                dve.wait_ge(frstd_ready, i * STREAMS + s + 1)
                for t in range(NT):
                    nc.vector.tensor_scalar(z[s][:, t, 0:H], z[s][:, t, 0:H], fmv[:, t, 0:1], frstd[:, t:t + 1],
                                            ALU.subtract, ALU.mult).then_inc(x1_ready, 1)

            def one_pass(i, last):
                for unit in range(UNITS):
                    more = not (last and unit == UNITS - 1)
                    layer, s = divmod(unit, STREAMS)
                    mask_scores(i, unit)
                    if more:
                        turn_lo(i, unit + 1, 0)
                    probabilities(i, unit)
                    if more:
                        turn_lo(i, unit + 1, 1)
                    probabilities_lo(i, unit)
                    if more:
                        turn_lo(i, unit + 1, 2)
                    biased_values(i, unit)
                    context_stats(i, unit)
                    normalise(i, unit)
                    steps = [centre, scale_shift, add_residual, final_stats, final_var, final_scale]
                    for j in range(QB):
                        if more:
                            query_lo(i, unit + 1, j)
                        if layer == 1:
                            steps[j](i, s)

            split_weight(0)
            for k in range(KO):
                turn_lo(0, 0, k)
            split_weight(1)
            for j in range(QB):
                query_lo(0, 0, j)
                if j == 1:
                    split_weight(2)
            dve.wait_ge(bias_in, 16 * 5)
            for n in range(3, 6):
                split_weight(n)
            with dve.Fori(0, PASSES - 1) as i:
                one_pass(i, False)
            one_pass(PASSES - 1, True)


def softmax_layers(nc, cm, x1, adj_t, w_nbr_t, b_nbr, ln_w, ln_b, table, out):
    H, KO, HC = cm.H, cm.KO, cm.HC
    LAYERS = w_nbr_t[0].shape[0]
    PASSES = x1.shape[0] // (TOK * STREAMS)
    SCALE = float(H) ** -0.5
    SIDES = 3
    VB = NT * SIDES
    WN = VB + NT
    RING = 4
    VF = 4
    EARLY = 2
    assert LAYERS == 2 and WN * UNITS % RING == 0 and UNITS * KO % 2 == 0

    x_v = x1.rearrange("(i s t p) h -> i s p t h", s=STREAMS, t=NT, p=P)
    out_v = out.rearrange("a n h -> (a n) h").rearrange("(i s t p) h -> i s p t h", s=STREAMS, t=NT, p=P)
    adj_t_v = adj_t.rearrange("(i s t b) r c -> i s b r t c", s=STREAMS, t=NT, b=2)

    with ExitStack() as ctx:
        def sb(name, shape, dt=F32):
            return ctx.enter_context(nc.sbuf_tensor("s_" + name, shape, dt))

        def sem(name):
            return ctx.enter_context(nc.semaphore("s_" + name))

        const = sb("const", [P, C_SEL])
        rows_f = sb("rows_f", [NT, C_ALL - C_SEL])
        pick_row = sb("pick_row", [NT, NT, P], F32R)
        block_rows = sb("block_rows", [2, P], BF16)
        block_cols = sb("block_cols", [2, TOK], BF16)
        one = sb("one", [P, 1])
        power = sb("power", [P, NT])
        w_hi = sb("w_hi", [P, LAYERS, SIDES, KO, H], F32R)
        w_lo = sb("w_lo", [P, LAYERS, SIDES, KO, H], F32R)
        bias = sb("bias", [P, SIDES, LAYERS, H])
        gain_f = sb("gain_f", [P, KO])
        shift_f = sb("shift_f", [P, KO])
        gain = sb("gain", [P, H])
        shift = sb("shift", [P, H])
        x_in = [sb(f"x_in{s}", [P, NT, H]) for s in range(STREAMS)]
        z = [sb(f"z{s}", [P, NT, H]) for s in range(STREAMS)]
        ht_hi = [sb(f"ht_hi{s}", [P, KO, TOK], F32R) for s in range(STREAMS)]
        ht_lo = [sb(f"ht_lo{s}", [P, KO, TOK], F32R) for s in range(STREAMS)]
        a_tr = [sb(f"a_tr{s}", [P, NT, P]) for s in range(STREAMS)]
        x_res = [sb(f"x_res{s}", [P, NT, H]) for s in range(STREAMS)]
        ht_full = sb("ht_full", [P, KO, TOK])
        v_hi = sb("v_hi", [P, NT, 2, HC], F32R)
        v_lo = sb("v_lo", [P, NT, 2, HC], F32R)
        v_full = sb("v_full", [P, VF, H])
        v_own = sb("v_own", [P, NT, H])
        row_max = sb("row_max", [P, NT])
        neg_max = sb("neg_max", [NT, P], F32R)
        expo = sb("expo", [P, NT, P])
        prob = [sb(f"prob{n}", [P, NT, P]) for n in range(2)]
        prob_hi = [sb(f"prob_hi{n}", [P, NT, P], F32R) for n in range(2)]
        prob_lo = [sb(f"prob_lo{n}", [P, NT, P], F32R) for n in range(2)]
        own = sb("own", [P, NT])
        stats = sb("stats", [P, NT, 6])
        mv = sb("mv", [P, NT, 2])
        near = sb("near", [P, NT])
        total = sb("total", [P, NT])
        var = sb("var", [P, NT])
        rstd = sb("rstd", [P, NT])
        fmv = sb("fmv", [P, NT, 2])
        fvar = sb("fvar", [P, NT])
        frstd = sb("frstd", [P, NT])

        work = [ctx.enter_context(nc.psum_tensor(f"s_work{n}", [P, 512], F32)) for n in range(RING)]
        turn = [ctx.enter_context(nc.psum_tensor(f"s_turn{n}", [P, 512], F32)) for n in range(2)]
        score_ps = ctx.enter_context(nc.psum_tensor("s_score_ps", [P, NT, P], F32))
        small_ps = ctx.enter_context(nc.psum_tensor("s_small_ps", [P, 512], F32))
        sum_ps = small_ps[:, P:P + NT]

        eye = const[:, C_EYE:C_EYE + P]

        def over_tiles(c):
            return const[:, c:c + P].unsqueeze(1).to_broadcast([P, NT, P])

        const_in, bias_in = sem("const_in"), sem("bias_in")
        stage_in = [sem(f"stage_in{n}") for n in range(2)]
        stage_split, stage_half = sem("stage_split"), sem("stage_half")
        x_loaded = [sem(f"x_loaded{s}") for s in range(STREAMS)]
        x_copied = [sem(f"x_copied{s}") for s in range(STREAMS)]
        adj_loaded = [sem(f"adj_loaded{s}") for s in range(STREAMS)]
        stored = [sem(f"stored{s}") for s in range(STREAMS)]
        cleared, power_set, ones_set, rows_cast = sem("cleared"), sem("power_set"), sem("ones_set"), sem("rows_cast")
        turned, turn_read, ht_ready = sem("turned"), sem("turn_read"), sem("ht_ready")
        work_full, work_free = sem("work_full"), sem("work_free")
        score_full, max_ready, max_turned = sem("score_full"), sem("max_ready"), sem("max_turned")
        neg_ready, shifted, exp_ready, sums_full = sem("neg_ready"), sem("shifted"), sem("exp_ready"), sem("sums_full")
        prob_ready, prob_hi_ready, prob_lo_ready = sem("prob_ready"), sem("prob_hi_ready"), sem("prob_lo_ready")
        diag_ready, own_ready = sem("diag_ready"), sem("own_ready")
        v_hi_ready, v_lo_ready, ctx_ready, near_ready = sem("v_hi_ready"), sem("v_lo_ready"), sem("ctx_ready"), sem("near_ready")
        stats_ready, mean_ready, total_ready, var_ready, rstd_ready, z_ready = (
            sem("stats_ready"), sem("mean_ready"), sem("total_ready"), sem("var_ready"), sem("rstd_ready"), sem("z_ready"))
        centred, scaled, summed, fstats_ready = sem("centred"), sem("scaled"), sem("summed"), sem("fstats_ready")
        fmean_ready, fvar_ready, frstd_ready, out_ready = sem("fmean_ready"), sem("fvar_ready"), sem("frstd_ready"), sem("out_ready")
        squared = sem("squared")

        def value_job(j):
            return divmod(j, SIDES)

        def freed(i, unit, j):
            return nth(i, unit, WN, j) + RING

        stage = [v_own[:, 0:KO, :], z[1][:, 0:KO, :]]

        block = ctx.enter_context(nc.Block())

        @block.sync
        def _(sp):
            def load_x(i, s):
                sp.dma_start(x_in[s][:], x_v[i, s]).then_inc(x_loaded[s], 16)

            def load_adj(i, s):
                for b in range(2):
                    h = slice(b * 64, b * 64 + 64)
                    sp.dma_start(a_tr[s][h, :, h], adj_t_v[i, s, b]).then_inc(adj_loaded[s], 16)

            sp.dma_start(const[:], table[:, 0:C_SEL]).then_inc(const_in, 16)
            load_x(0, 0)
            sp.dma_start(rows_f[:], table[0:NT, C_SEL:C_ALL]).then_inc(const_in, 16)
            weights = [w_nbr_t[n][l] for l in range(LAYERS) for n in range(SIDES)]
            for n, w in enumerate(weights):
                if n >= 2:
                    sp.wait_ge(stage_split, n - 1)
                sp.dma_start(stage[n % 2], w.rearrange("(k p) o -> p k o", p=P)).then_inc(stage_in[n % 2], 16)
                if n == 1:
                    sp.wait_ge(cleared, 2)
                    load_adj(0, 0)
                    for m in range(SIDES):
                        sp.dma_start(bias[:, m], b_nbr[m].partition_broadcast(P)).then_inc(bias_in, 16)
                    sp.dma_start(gain_f[:], ln_w[0].rearrange("(k p) -> p k", p=P),
                                 allow_slow_non_contiguous=True).then_inc(bias_in, 16)
                    sp.dma_start(shift_f[:], ln_b[0].rearrange("(k p) -> p k", p=P),
                                 allow_slow_non_contiguous=True).then_inc(bias_in, 16)
                    sp.dma_start(gain[:], ln_w[1].partition_broadcast(P)).then_inc(bias_in, 16)
                    sp.dma_start(shift[:], ln_b[1].partition_broadcast(P)).then_inc(bias_in, 16)
                    load_x(0, 1)
                    load_adj(0, 1)

            def one_pass(i, last):
                for s in range(STREAMS):
                    sp.wait_ge(x_loaded[s], 16 * (i + 1))
                    wait(sp, summed, i * (STREAMS * NT) + (s + 1 - STREAMS) * NT)
                    sp.dma_start(x_res[s][:], x_in[s][:]).then_inc(x_copied[s], 16)
                    if not last:
                        sp.wait_ge(turned, nth(i, s, KO, KO - 1))
                        sp.wait_ge(x_copied[s], 16 * (i + 1))
                        load_x(i + 1, s)
                for s in range(STREAMS):
                    if not last:
                        sp.wait_ge(own_ready, nth(i, 2 + s, 1, 0))
                        load_adj(i + 1, s)
                    sp.wait_ge(out_ready, i * (STREAMS * NT) + NT * (s + 1))
                    sp.dma_start(out_v[i, s], z[s][:]).then_inc(stored[s], 16)

            one_pass(0, False)
            with sp.Fori(1, PASSES - 1) as i:
                one_pass(i, False)
            one_pass(PASSES - 1, True)
            for s in range(STREAMS):
                sp.wait_ge(stored[s], 16 * (PASSES + 1))

        @block.tensor
        def _(pe):
            def turn_tokens(i, unit):
                layer, s = divmod(unit % UNITS, STREAMS)
                src = x_in[s] if layer == 0 else z[s]
                if layer == 0:
                    pe.wait_ge(x_loaded[s], i * 16 + 16 * (unit // UNITS + 1))
                else:
                    pe.wait_ge(z_ready, i * (STREAMS * NT) + NT * (s + 1))
                for k in range(KO):
                    wait(pe, turn_read, nth(i, unit, KO, k - 2))
                    bank = turn[(unit * KO + k) % 2]
                    for t in range(NT):
                        mm = pe.transpose(bank[:, t * P:(t + 1) * P], src[:, t, k * P:(k + 1) * P], eye)
                    mm.then_inc(turned, 1)

            def work_bank(i, unit, j):
                pe.wait_ge(work_free, freed(i, unit, j - RING))
                return work[(unit * WN + j) % RING]

            def scores(i, unit):
                s = unit % STREAMS
                pe.wait_ge(ht_ready, nth(i, unit, KO, KO - 1))
                wait(pe, exp_ready, nth(i, unit, 1, -1))
                pe.matmul(score_ps[:], block_rows[:], block_cols[:], start=True, stop=False,
                          skip_group_check=True)
                for t in range(NT):
                    tile = slice(t * P, (t + 1) * P)
                    for k in range(KO):
                        for a, b in three_products(ht_hi[s], ht_lo[s], ht_hi[s], ht_lo[s]):
                            mm = pe.matmul(score_ps[:, t, :], a[:, k, tile], b[:, k, tile], start=False,
                                           stop=False, skip_group_check=True)
                mm.then_inc(score_full, 1)

            def turn_max(i, unit):
                pe.wait_ge(max_ready, nth(i, unit, 1, 0))
                pe.wait_ge(near_ready, nth(i, unit, 1, 0))
                pe.transpose(small_ps[0:NT, 0:P], row_max[:], eye).then_inc(max_turned, 1)

            def subtract_max(i, unit):
                pe.wait_ge(neg_ready, nth(i, unit, 1, 0))
                for t in range(NT):
                    mm = pe.matmul(score_ps[:, t, :], pick_row[:, t, :], neg_max[:], start=False,
                                   stop=(t == NT - 1), skip_group_check=True)
                mm.then_inc(shifted, 1)

            def row_sums(i, unit):
                pe.wait_ge(exp_ready, nth(i, unit, 1, 0))
                for t in range(NT):
                    mm = pe.matmul(sum_ps[:, t:t + 1], expo[:, t, :], one[:], start=True, stop=True)
                mm.then_inc(sums_full, 1)

            def values(i, unit, j):
                layer, s = divmod(unit, STREAMS)
                t, side = value_job(j)
                pe.wait_ge(stage_split, SIDES * layer + side + 1)
                bank = work_bank(i, unit, j)
                pairs = [(h[s][:, k, t * P:(t + 1) * P], w[:, layer, side, k, :])
                         for k in range(KO) for h, w in three_products(ht_hi, ht_lo, w_hi, w_lo)]
                for n, (h, w) in enumerate(pairs):
                    mm = pe.matmul(bank[:, 0:H], h, w, start=(n == 0), stop=(n == len(pairs) - 1))
                mm.then_inc(work_full, 1)

            def contexts(i, unit):
                pe.wait_ge(prob_lo_ready, nth(i, unit, 2, 1))
                for t in range(NT):
                    pe.wait_ge(v_lo_ready, nth(i, unit, 2 * NT, 2 * t + 1))
                    bank = work_bank(i, unit, VB + t)
                    pairs = [(p[n][:, t, :], v[:, t, n, :])
                             for n in range(2) for p, v in three_products(prob_hi, prob_lo, v_hi, v_lo)]
                    for n, (p, v) in enumerate(pairs):
                        mm = pe.matmul(bank[:, 0:HC], p, v, start=(n == 0), stop=(n == len(pairs) - 1))
                    mm.then_inc(work_full, 1)

            def one_pass(i, last):
                for unit in range(UNITS):
                    more = not (last and unit == UNITS - 1)
                    values(i, unit, 0)
                    turn_max(i, unit)
                    values(i, unit, 1)
                    values(i, unit, 2)
                    subtract_max(i, unit)
                    for j in range(3, 6):
                        values(i, unit, j)
                    row_sums(i, unit)
                    for j in range(6, 9):
                        values(i, unit, j)
                    if more:
                        turn_tokens(i, unit + 1)
                    for j in range(9, VB):
                        values(i, unit, j)
                    contexts(i, unit)
                    if more:
                        scores(i, unit + 1)

            pe.wait_ge(const_in, 32)
            turn_tokens(0, 0)
            pe.wait_ge(rows_cast, 3)
            pe.wait_ge(ones_set, 1)
            scores(0, 0)
            with pe.Fori(0, PASSES - 1) as i:
                one_pass(i, False)
            one_pass(PASSES - 1, True)

        @block.scalar
        def _(act):
            def turn_out(i, unit, k):
                layer, s = divmod(unit % UNITS, STREAMS)
                act.wait_ge(turned, nth(i, unit, KO, k))
                wait(act, ht_ready, nth(i, unit, KO, k - KO))
                bank = turn[(unit * KO + k) % 2]
                for out_ in (ht_full[:, k, :], ht_hi[s][:, k, :]):
                    if layer == 0:
                        op = nc.scalar.activation(out_, bank[:], ACT.Copy)
                    else:
                        op = nc.scalar.activation(out_, bank[:], ACT.Relu, bias=shift_f[:, k:k + 1],
                                                  scale=gain_f[:, k:k + 1])
                op.then_inc(turn_read, 1)

            def negate_max(i, unit):
                act.wait_ge(max_turned, nth(i, unit, 1, 0))
                nc.scalar.activation(neg_max[:], small_ps[0:NT, 0:P], ACT.Copy, scale=-1.0).then_inc(neg_ready, 1)

            def exponentials(i, unit):
                act.wait_ge(shifted, nth(i, unit, 1, 0))
                nc.scalar.activation(expo[:], score_ps[:], ACT.Exp, scale=SCALE).then_inc(exp_ready, 1)

            def probabilities_hi(i, unit):
                for n in range(2):
                    act.wait_ge(prob_ready, nth(i, unit, 2, n))
                    nc.scalar.activation(prob_hi[n][:], prob[n][:], ACT.Copy).then_inc(prob_hi_ready, 1)

            def values_hi(i, unit, t):
                for n in range(2):
                    act.wait_ge(work_free, freed(i, unit, t * SIDES + n))
                    nc.scalar.activation(v_hi[:, t, n, 0:H], v_full[:, (2 * t + n) % VF, :], ACT.Copy)\
                        .then_inc(v_hi_ready, 1)

            def one_pass(i, last):
                for unit in range(UNITS):
                    more = not (last and unit == UNITS - 1)
                    negate_max(i, unit)
                    values_hi(i, unit, 0)
                    exponentials(i, unit)
                    values_hi(i, unit, 1)
                    probabilities_hi(i, unit)
                    values_hi(i, unit, 2)
                    if more:
                        for k in range(KO):
                            turn_out(i, unit + 1, k)
                    values_hi(i, unit, 3)

            act.wait_ge(const_in, 32)
            nc.scalar.activation(pick_row[:].rearrange("r t i -> r (t i)"), rows_f[:, 0:TOK], ACT.Copy)\
                .then_inc(rows_cast, 1)
            nc.scalar.activation(block_rows[:], rows_f[0:2, C_ROWS - C_SEL:C_COLS - C_SEL], ACT.Copy)\
                .then_inc(rows_cast, 1)
            nc.scalar.activation(block_cols[:], rows_f[0:2, C_COLS - C_SEL:C_ALL - C_SEL], ACT.Copy)\
                .then_inc(rows_cast, 1)
            for k in range(KO):
                turn_out(0, 0, k)
            act.wait_ge(bias_in, 16 * (SIDES + 4))
            with act.Fori(0, PASSES - 1) as i:
                one_pass(i, False)
            one_pass(PASSES - 1, True)

        @block.gpsimd
        def _(pool):
            def values_lo(i, unit, t):
                for n in range(2):
                    pool.wait_ge(v_hi_ready, nth(i, unit, 2 * NT, 2 * t + n))
                    nc.gpsimd.tensor_tensor(v_lo[:, t, n, 0:H], v_full[:, (2 * t + n) % VF, :],
                                            v_hi[:, t, n, 0:H].bitcast(F32), ALU.subtract).then_inc(v_lo_ready, 1)

            def roots(i, unit):
                pool.wait_ge(var_ready, nth(i, unit, 1, 0))
                nc.gpsimd.tensor_tensor(rstd[:], var[:], power[:], ALU.pow).then_inc(rstd_ready, 1)

            def final_roots(i, s):
                pool.wait_ge(fvar_ready, i * STREAMS + s + 1)
                nc.gpsimd.tensor_tensor(frstd[:], fvar[:], power[:], ALU.pow).then_inc(frstd_ready, 1)

            def one_pass(i, last):
                for unit in range(UNITS):
                    for t in range(EARLY, NT):
                        values_lo(i, unit, t)
                    roots(i, unit)
                    if not (last and unit == UNITS - 1):
                        for t in range(EARLY):
                            values_lo(i, unit + 1, t)
                    if unit >= STREAMS:
                        final_roots(i, unit - STREAMS)

            for s in range(STREAMS):
                nc.gpsimd.memset(a_tr[s][:], 0.0).then_inc(cleared, 1)
            nc.gpsimd.memset(v_hi[:, :, :, H:HC].bitcast(F32), 1.0).then_inc(stored[0], 16)
            nc.gpsimd.memset(v_lo[:, :, :, H:HC].bitcast(F32), 0.0).then_inc(stored[1], 16)
            nc.gpsimd.memset(one[:], 1.0).then_inc(ones_set, 1)
            nc.gpsimd.memset(power[:], -0.5).then_inc(power_set, 1)
            pool.wait_ge(power_set, 1)
            for t in range(EARLY):
                values_lo(0, 0, t)
            with pool.Fori(0, PASSES - 1) as i:
                one_pass(i, False)
            one_pass(PASSES - 1, True)

        @block.vector
        def _(dve):
            def split_weight(n):
                layer, side = divmod(n, SIDES)
                hi, lo = w_hi[:, layer, side], w_lo[:, layer, side]
                dve.wait_ge(stage_in[n % 2], 16 * (n // 2 + 1))
                nc.vector.tensor_copy(hi, stage[n % 2]).then_inc(stage_half, 1)
                dve.wait_ge(stage_half, n + 1)
                nc.vector.tensor_tensor(lo, stage[n % 2], hi.bitcast(F32), ALU.subtract)\
                    .then_inc(stage_split, 1)

            def turn_lo(i, unit, k):
                s = unit % STREAMS
                dve.wait_ge(turn_read, nth(i, unit, KO, k))
                nc.vector.tensor_tensor(ht_lo[s][:, k, :], ht_full[:, k, :], ht_hi[s][:, k, :].bitcast(F32),
                                        ALU.subtract).then_inc(ht_ready, 1)

            def maximum(i, unit):
                dve.wait_ge(score_full, nth(i, unit, 1, 0))
                nc.vector.tensor_reduce(row_max[:], score_ps[:], AX.X, ALU.max).then_inc(max_ready, 1)

            def biased_value(i, unit, j):
                layer = unit // STREAMS % LAYERS
                t, side = value_job(j)
                dve.wait_ge(work_full, nth(i, unit, WN, j))
                if side < 2:
                    if 2 * t >= VF:
                        dve.wait_ge(v_lo_ready, nth(i, unit, 2 * NT, 2 * t + side - VF))
                    dst = v_full[:, (2 * t + side) % VF, :]
                else:
                    dst = v_own[:, t, :]
                nc.vector.tensor_tensor(dst, work[(unit * WN + j) % RING][:, 0:H], bias[:, side, layer, :],
                                        ALU.add).then_inc(work_free, 1)

            def biased_values(i, unit, t):
                for side in range(SIDES):
                    biased_value(i, unit, t * SIDES + side)

            def probabilities(i, unit):
                s = unit % STREAMS
                dve.wait_ge(exp_ready, nth(i, unit, 1, 0))
                if unit < STREAMS:
                    dve.wait_ge(adj_loaded[s], 32 * (i + 1))
                wait(dve, sums_full, nth(i, unit, 1, 0))
                nc.vector.tensor_tensor(expo[:], expo[:], a_tr[s][:], ALU.mult).then_inc(squared, 1)
                dve.wait_ge(squared, nth(i, unit, 1, 0))
                for n, c in enumerate((C_LT, C_GT)):
                    nc.vector.tensor_tensor(prob[n][:], expo[:], over_tiles(c), ALU.mult).then_inc(prob_ready, 1)
                nc.vector.tensor_tensor(expo[:], expo[:], over_tiles(C_EYE), ALU.mult).then_inc(diag_ready, 1)
                dve.wait_ge(diag_ready, nth(i, unit, 1, 0))
                nc.vector.tensor_reduce(own[:], expo[:], AX.X, ALU.add).then_inc(own_ready, 1)

            def probabilities_lo(i, unit):
                for n in range(2):
                    dve.wait_ge(prob_hi_ready, nth(i, unit, 2, n))
                    nc.vector.tensor_tensor(prob_lo[n][:], prob[n][:], prob_hi[n][:].bitcast(F32), ALU.subtract)\
                        .then_inc(prob_lo_ready, 1)

            def contexts_out(i, unit):
                layer, s = divmod(unit, STREAMS)
                if layer == 0:
                    dve.wait_ge(stored[s], 16 * (i + 1))
                dve.wait_ge(own_ready, nth(i, unit, 1, 0))
                for t in range(NT):
                    j = VB + t
                    bank = work[(unit * WN + j) % RING]
                    dve.wait_ge(work_full, nth(i, unit, WN, j))
                    nc.vector.tensor_copy(near[:, t:t + 1], bank[:, H:H + 1])
                    nc.vector.scalar_tensor_tensor(z[s][:, t, :], v_own[:, t, :], own[:, t:t + 1], bank[:, 0:H],
                                                   ALU.mult, ALU.add).then_inc(work_free, 1)
                    dve.wait_ge(work_free, freed(i, unit, j))
                    nc.vector.bn_stats(stats[:, t, :], z[s][:, t, :]).then_inc(stats_ready, 1)

            def normalise(i, unit):
                layer, s = divmod(unit, STREAMS)
                dve.wait_ge(sums_full, nth(i, unit, 1, 0))
                dve.wait_ge(stats_ready, nth(i, unit, NT, NT - 1))
                nc.vector.scalar_tensor_tensor(total[:], sum_ps, 1e-10, near[:], ALU.mult, ALU.add)\
                    .then_inc(near_ready, 1)
                for t in range(NT):
                    op = nc.vector.bn_aggr(mv[:, t, :], stats[:, t, :])
                op.then_inc(mean_ready, 1)
                dve.wait_ge(near_ready, nth(i, unit, 1, 1))
                nc.vector.tensor_tensor(total[:], total[:], own[:], ALU.add).then_inc(total_ready, 1)
                dve.wait_ge(total_ready, nth(i, unit, 2, 0))
                nc.vector.scalar_tensor_tensor(total[:], total[:], 1e-12, total[:], ALU.mult, ALU.mult)\
                    .then_inc(total_ready, 1)
                dve.wait_ge(total_ready, nth(i, unit, 2, 1))
                dve.wait_ge(mean_ready, nth(i, unit, 1, 0))
                nc.vector.tensor_tensor(var[:], mv[:, :, 1], total[:], ALU.add).then_inc(var_ready, 1)
                if layer == 0:
                    dve.wait_ge(rstd_ready, nth(i, unit, 1, 0))
                    for t in range(NT):
                        nc.vector.tensor_scalar(z[s][:, t, :], z[s][:, t, :], mv[:, t, 0:1],
                                                rstd[:, t:t + 1], ALU.subtract, ALU.mult).then_inc(z_ready, 1)

            def centre(i, s):
                for t in range(NT):
                    nc.vector.scalar_tensor_tensor(z[s][:, t, :], z[s][:, t, :], mv[:, t, 0:1], gain[:],
                                                   ALU.subtract, ALU.mult).then_inc(centred, 1)

            def scale_shift(i, s):
                dve.wait_ge(rstd_ready, nth(i, STREAMS + s, 1, 0))
                for t in range(NT):
                    dve.wait_ge(centred, i * (STREAMS * NT) + s * NT + t + 1)
                    nc.vector.scalar_tensor_tensor(z[s][:, t, :], z[s][:, t, :], rstd[:, t:t + 1], shift[:],
                                                   ALU.mult, ALU.add).then_inc(scaled, 1)

            def add_residual(i, s):
                dve.wait_ge(x_copied[s], 16 * (i + 1))
                for t in range(NT):
                    dve.wait_ge(scaled, i * (STREAMS * NT) + s * NT + t + 1)
                    nc.vector.scalar_tensor_tensor(z[s][:, t, :], z[s][:, t, :], 0.0, x_res[s][:, t, :],
                                                   ALU.max, ALU.add).then_inc(summed, 1)

            def final_stats(i, s):
                for t in range(NT):
                    dve.wait_ge(summed, i * (STREAMS * NT) + s * NT + t + 1)
                    nc.vector.bn_stats(stats[:, t, :], z[s][:, t, :]).then_inc(fstats_ready, 1)

            def final_var(i, s):
                dve.wait_ge(fstats_ready, i * (STREAMS * NT) + (s + 1) * NT)
                nc.vector.memset(fvar[:], 1e-5)
                for t in range(NT):
                    op = nc.vector.bn_aggr(fmv[:, t, :], stats[:, t, :])
                op.then_inc(fmean_ready, 1)
                dve.wait_ge(fmean_ready, i * STREAMS + s + 1)
                nc.vector.tensor_tensor(fvar[:], fvar[:], fmv[:, :, 1], ALU.add).then_inc(fvar_ready, 1)

            def final_scale(i, s):
                dve.wait_ge(frstd_ready, i * STREAMS + s + 1)
                for t in range(NT):
                    nc.vector.tensor_scalar(z[s][:, t, :], z[s][:, t, :], fmv[:, t, 0:1], frstd[:, t:t + 1],
                                            ALU.subtract, ALU.mult).then_inc(out_ready, 1)

            def one_pass(i, last):
                for unit in range(UNITS):
                    more = not (last and unit == UNITS - 1)
                    layer, s = divmod(unit, STREAMS)
                    probabilities(i, unit)
                    biased_values(i, unit, 2)
                    probabilities_lo(i, unit)
                    if more:
                        for k in range(KO):
                            turn_lo(i, unit + 1, k)
                    biased_values(i, unit, 3)
                    contexts_out(i, unit)
                    normalise(i, unit)
                    steps = [centre, scale_shift, add_residual, final_stats, final_var, final_scale]
                    if more:
                        maximum(i, unit + 1)
                    for n in range(EARLY * SIDES):
                        if more:
                            biased_value(i, unit + 1, n)
                        if layer == 1:
                            steps[n](i, s)

            nc.vector.memset(near[:], 0.0).then_inc(work_free, RING)
            nc.vector.memset(total[:], 0.0).then_inc(near_ready, 1)
            split_weight(0)
            for k in range(KO):
                turn_lo(0, 0, k)
            for n in range(1, 6):
                split_weight(n)
            dve.wait_ge(bias_in, 16 * (SIDES + 4))
            maximum(0, 0)
            biased_values(0, 0, 0)
            biased_values(0, 0, 1)
            with dve.Fori(0, PASSES - 1) as i:
                one_pass(i, False)
            one_pass(PASSES - 1, True)


def resnorm_graph_blocks(nc, x, adj, adj_t, w, table, out):
    B, S, H = x.shape
    assert S == P // 2 and H % P == 0 and B * S % (TOK * STREAMS) == 0
    x1 = nc.dram_tensor("x1", (B * S, H), F32).ap()
    cm = Common(H)
    gated_layers(nc, cm, x, adj, adj_t, w["L0_gnn_W_left"], w["L0_gnn_W_right"], w["L0_gnn_W_lin"],
                 w["L0_gnn_b_lin"], w["L0_gnn_ln_a"], w["L0_gnn_ln_b"], table, x1)
    softmax_layers(nc, cm, x1, adj_t, [w["L1_gnn_Wl"], w["L1_gnn_Wr"], w["L1_gnn_Ws"]],
                   [w["L1_gnn_bl"], w["L1_gnn_br"], w["L1_gnn_bs"]], w["L1_gnn_ln_w"], w["L1_gnn_ln_b"], table, out)


_TURNED = ["L0_gnn_W_lin", "L1_gnn_Wl", "L1_gnn_Wr", "L1_gnn_Ws"]
_STRAIGHT = ["L0_gnn_W_left", "L0_gnn_W_right", "L0_gnn_b_lin", "L0_gnn_ln_a", "L0_gnn_ln_b",
             "L1_gnn_bl", "L1_gnn_bs", "L1_gnn_br", "L1_gnn_ln_w", "L1_gnn_ln_b"]


def kernel(**inputs):
    import numpy as _np
    import concourse.bacc as _bacc
    from concourse import mybir as _mybir
    from concourse.bass_utils import run_bass_kernel_spmd as _run

    host = {n: _np.ascontiguousarray(inputs[n]) for n in ["x", "adj"] + _STRAIGHT}
    host["adj_t"] = _np.ascontiguousarray(_np.transpose(_np.asarray(inputs["adj"]), (0, 2, 1)))
    for n in _TURNED:
        host[n] = _np.ascontiguousarray(_np.transpose(_np.asarray(inputs[n]), (0, 2, 1)))
    host["table"] = constants_table()

    nc = _bacc.Bacc("TRN2", target_bir_lowering=False, num_devices=1)
    ap = {n: nc.dram_tensor(f"in_{n}", a.shape, _mybir.dt.from_np(a.dtype), kind="ExternalInput").ap()
          for n, a in host.items()}
    out = nc.dram_tensor("out_0", host["x"].shape, F32, kind="ExternalOutput").ap()
    resnorm_graph_blocks(nc, ap["x"], ap["adj"], ap["adj_t"], ap, ap["table"], out)
    r = _run(nc, [{f"in_{n}": a for n, a in host.items()}], core_ids=[0])
    return r.results[0]["out_0"]
```

```python
from contextlib import ExitStack

import numpy as np

import concourse.bass as bass
from concourse import mybir

ALU = mybir.AluOpType
ACT = mybir.ActivationFunctionType
AX = mybir.AxisListType
F32 = mybir.dt.float32
F32R = mybir.dt.float32r
BF16 = mybir.dt.bfloat16

P = 128
NT = 4
TOK = NT * P
STREAMS = 2
UNITS = 4
BIG = 1e30

C_EYE, C_LE, C_GT, C_LT, C_SEL, C_ROWS, C_COLS = 0, 128, 256, 384, 512, 1024, 1152
C_ALL = 1664


def constants_table():
    c = np.zeros((P, C_ALL), np.float32)
    j, i = np.arange(P)[:, None], np.arange(P)[None, :]
    c[:, C_EYE:C_EYE + P] = i == j
    c[:, C_LE:C_LE + P] = i <= j
    c[:, C_GT:C_GT + P] = i > j
    c[:, C_LT:C_LT + P] = i < j
    for t in range(NT):
        c[t, C_SEL + t * P:C_SEL + (t + 1) * P] = 1.0
    second = (np.arange(P) >= P // 2).astype(np.float32)
    c[0, C_ROWS:C_ROWS + P] = 1 - second
    c[1, C_ROWS:C_ROWS + P] = second
    zero = np.zeros(P)
    c[0, C_COLS:C_COLS + 4 * P] = np.concatenate([-BIG * second, zero] * 2)
    c[1, C_COLS:C_COLS + 4 * P] = np.concatenate([-BIG * (1 - second), zero] * 2)
    return c


def nth(i, unit, per, k):
    return i * (UNITS * per) + (unit * per + k + 1)


def wait(eng, sem, value):
    if isinstance(value, int) and value <= 0:
        return
    eng.wait_ge(sem, value)


class Common:

    def __init__(self, H):
        self.H = H
        self.KO = H // P
        self.HC = H + 2


def three_products(H_hi, H_lo, W_hi, W_lo):
    return ((H_hi, W_hi), (H_hi, W_lo), (H_lo, W_hi))


def gated_layers(nc, cm, x, adj, adj_t, w_left, w_right, w_lin_t, b_lin, ln_a, ln_b, table, x1):
    H, KO, HC = cm.H, cm.KO, cm.HC
    LAYERS = w_left.shape[0]
    B = x.shape[0]
    PASSES = B * x.shape[1] // (TOK * STREAMS)
    SCALE = float(H) ** -0.5
    EPS = 1e-3
    QB, VB = 2 * KO, NT
    WN = QB + 2 * NT
    RING = 4
    assert LAYERS == 2 and WN * UNITS % RING == 0 and UNITS * KO % 2 == 0

    x_v = x.rearrange("a n h -> (a n) h").rearrange("(i s t p) h -> i s p t h", s=STREAMS, t=NT, p=P)
    x1_v = x1.rearrange("(i s t p) h -> i s p t h", s=STREAMS, t=NT, p=P)
    adj_v = adj.rearrange("(i s t b) r c -> i s b r t c", s=STREAMS, t=NT, b=2)
    adj_t_v = adj_t.rearrange("(i s t b) r c -> i s b r t c", s=STREAMS, t=NT, b=2)

    with ExitStack() as ctx:
        def sb(name, shape, dt=F32):
            return ctx.enter_context(nc.sbuf_tensor("g_" + name, shape, dt))

        def sem(name):
            return ctx.enter_context(nc.semaphore("g_" + name))

        const = sb("const", [P, C_SEL])
        wq_hi = sb("wq_hi", [P, LAYERS, 2, KO, H], F32R)
        wq_lo = sb("wq_lo", [P, LAYERS, 2, KO, H], F32R)
        wv_hi = sb("wv_hi", [P, LAYERS, KO, H], F32R)
        wv_lo = sb("wv_lo", [P, LAYERS, KO, H], F32R)
        bias = sb("bias", [P, LAYERS, H])
        gain_f = sb("gain_f", [P, KO])
        shift_f = sb("shift_f", [P, KO])
        gain = sb("gain", [P, H])
        shift = sb("shift", [P, H])
        powers = sb("powers", [P, 2, NT])
        x_in = [sb(f"x_in{s}", [P, NT, H]) for s in range(STREAMS)]
        x_res = [sb(f"x_res{s}", [P, NT, H]) for s in range(STREAMS)]
        z = [sb(f"z{s}", [P, NT, HC]) for s in range(STREAMS)]
        ht_hi = [sb(f"ht_hi{s}", [P, KO, TOK], F32R) for s in range(STREAMS)]
        ht_lo = [sb(f"ht_lo{s}", [P, KO, TOK], F32R) for s in range(STREAMS)]
        a_nat = [sb(f"a_nat{s}", [P, NT, P]) for s in range(STREAMS)]
        a_tr = [sb(f"a_tr{s}", [P, NT, P]) for s in range(STREAMS)]
        keep_l = [sb(f"keep_l{s}", [P, NT, P]) for s in range(STREAMS)]
        ht_full = sb("ht_full", [P, KO, TOK])
        qv_hi = sb("qv_hi", [P, KO * 2 * TOK], F32R)
        qv_lo = sb("qv_lo", [P, KO * 2 * TOK], F32R)
        v_full = sb("v_full", [P, NT, H])
        score_l = sb("score_l", [P, NT, P])
        score_r = sb("score_r", [P, NT, P])
        prob = sb("prob", [P, NT, P])
        prob_hi = sb("prob_hi", [P, NT, P], F32R)
        prob_lo = sb("prob_lo", [P, NT, P], F32R)
        stats = sb("stats", [P, NT, 6])
        mv = sb("mv", [P, NT, 2])
        var = sb("var", [P, NT])
        sigma = sb("sigma", [P, NT])
        denom = sb("denom", [P, NT])
        rstd = sb("rstd", [P, NT])
        fstats = sb("fstats", [P, NT, 6])
        fmv = sb("fmv", [P, NT, 2])
        offset = sb("offset", [P, NT])
        foffset = [sb(f"foffset{s}", [P, NT]) for s in range(STREAMS)]
        fvar = sb("fvar", [P, NT])
        frstd = [sb(f"frstd{s}", [P, NT]) for s in range(STREAMS)]

        work = [ctx.enter_context(nc.psum_tensor(f"g_work{n}", [P, 512], F32)) for n in range(RING)]
        turn = [ctx.enter_context(nc.psum_tensor(f"g_turn{n}", [P, 512], F32)) for n in range(2)]
        score_ps = ctx.enter_context(nc.psum_tensor("g_score_ps", [P, NT, 2, P], F32))

        eye = const[:, C_EYE:C_EYE + P]
        q_hi = qv_hi[:].rearrange("p (m t d i) -> p m t d i", m=KO, t=NT, d=2)
        q_lo = qv_lo[:].rearrange("p (m t d i) -> p m t d i", m=KO, t=NT, d=2)
        V0 = KO * 2 * TOK - NT * HC
        assert V0 >= 2 * TOK
        v_hi = qv_hi[:, V0:].rearrange("p (t h) -> p t h", t=NT)
        v_lo = qv_lo[:, V0:].rearrange("p (t h) -> p t h", t=NT)

        stage = [b[:, 0:KO, 0:H] for b in (v_full, z[0], z[1], x_res[0], x_res[1], z[0])]
        weight_halves = [(wq_hi[:, l, n], wq_lo[:, l, n]) if n < 2 else (wv_hi[:, l], wv_lo[:, l])
                         for l in range(LAYERS) for n in range(3)]

        const_in, bias_in = sem("const_in"), sem("bias_in")
        stage_in = [sem(f"stage_in{n}") for n in range(2 * 3)]
        upper_split, first_split, second_split = sem("upper_split"), sem("first_split"), sem("second_split")
        x_loaded = [sem(f"x_loaded{s}") for s in range(STREAMS)]
        x_copied = [sem(f"x_copied{s}") for s in range(STREAMS)]
        adj_loaded = [sem(f"adj_loaded{s}") for s in range(STREAMS)]
        stored = [sem(f"stored{s}") for s in range(STREAMS)]
        cleared, powers_set = sem("cleared"), sem("powers_set")
        keep_ready = [sem(f"keep_ready{s}") for s in range(STREAMS)]
        turned, turn_read, ht_ready = sem("turned"), sem("turn_read"), sem("ht_ready")
        work_full, work_free = sem("work_full"), sem("work_free")
        q_hi_ready, score_full, masked, score_ready = sem("q_hi_ready"), sem("score_full"), sem("masked"), sem("score_ready")
        exp_ready, prob_ready, prob_hi_ready, prob_lo_ready = sem("exp_ready"), sem("prob_ready"), sem("prob_hi_ready"), sem("prob_lo_ready")
        v_hi_ready, v_lo_ready, ones_set = sem("v_hi_ready"), sem("v_lo_ready"), sem("ones_set")
        ctx_ready = sem("ctx_ready")
        mean_ready, var_ready, sigma_ready = sem("mean_ready"), sem("var_ready"), sem("sigma_ready")
        denom_ready, rstd_ready, z_ready = sem("denom_ready"), sem("rstd_ready"), sem("z_ready")
        offset_ready, foffset_ready = sem("offset_ready"), sem("foffset_ready")
        gained, scaled, summed, fstats_ready = sem("gained"), sem("scaled"), sem("summed"), sem("fstats_ready")
        fmean_ready, fvar_ready, frstd_ready, x1_ready = sem("fmean_ready"), sem("fvar_ready"), sem("frstd_ready"), sem("x1_ready")

        def query_use(unit, j):
            return unit * WN + (0 if j == 0 else NT + j)

        def value_use(unit, t):
            return unit * WN + NT + QB + t

        def context_use(unit, t):
            return (unit + 1) * WN + 1 + t

        def used(i, use):
            return i * (UNITS * WN) + (use + 1)

        block = ctx.enter_context(nc.Block())

        @block.sync
        def _(sp):
            def load_x(i, s):
                sp.dma_start(x_in[s][:], x_v[i, s]).then_inc(x_loaded[s], 16)

            def load_adj(i, s):
                for b in range(2):
                    h = slice(b * 64, b * 64 + 64)
                    sp.dma_start(a_tr[s][h, :, h], adj_t_v[i, s, b]).then_inc(adj_loaded[s], 16)
                    sp.dma_start(a_nat[s][h, :, h], adj_v[i, s, b]).then_inc(adj_loaded[s], 16)

            def small_loads():
                sp.wait_ge(cleared, 4)
                load_adj(0, 0)
                sp.dma_start(bias[:], b_lin.partition_broadcast(P)).then_inc(bias_in, 16)
                sp.dma_start(gain_f[:], ln_a[0].rearrange("(k p) -> p k", p=P),
                             allow_slow_non_contiguous=True).then_inc(bias_in, 16)
                sp.dma_start(shift_f[:], ln_b[0].rearrange("(k p) -> p k", p=P),
                             allow_slow_non_contiguous=True).then_inc(bias_in, 16)
                sp.dma_start(gain[:], ln_a[1].partition_broadcast(P)).then_inc(bias_in, 16)
                sp.dma_start(shift[:], ln_b[1].partition_broadcast(P)).then_inc(bias_in, 16)
                load_x(0, 1)
                load_adj(0, 1)

            sp.dma_start(const[:], table[:, 0:C_SEL]).then_inc(const_in, 16)
            load_x(0, 0)
            weights = [w for l in range(LAYERS) for w in (w_left[l], w_right[l], w_lin_t[l])]
            for n, w in enumerate(weights):
                if n == 3:
                    small_loads()
                if n == 5:
                    sp.wait_ge(first_split, 2)
                sp.dma_start(stage[n], w.rearrange("(k p) o -> p k o", p=P)).then_inc(stage_in[n], 16)
            sp.wait_ge(second_split, 3)

            def one_pass(i, last):
                for s in range(STREAMS):
                    sp.wait_ge(x_loaded[s], 16 * (i + 1))
                    wait(sp, summed, i * (STREAMS * NT) + (s + 1 - STREAMS) * NT)
                    sp.dma_start(x_res[s][:], x_in[s][:]).then_inc(x_copied[s], 16)
                    if not last:
                        sp.wait_ge(turned, nth(i, s, KO, KO - 1))
                        sp.wait_ge(x_copied[s], 16 * (i + 1))
                        load_x(i + 1, s)
                for s in range(STREAMS):
                    if not last:
                        sp.wait_ge(prob_ready, nth(i, 2 + s, 1, 0))
                        load_adj(i + 1, s)
                    sp.wait_ge(x1_ready, i * (STREAMS * NT) + NT * (s + 1))
                    sp.dma_start(x1_v[i, s], z[s][:, :, 0:H]).then_inc(stored[s], 16)

            one_pass(0, False)
            with sp.Fori(1, PASSES - 1) as i:
                one_pass(i, False)
            one_pass(PASSES - 1, True)
            for s in range(STREAMS):
                sp.wait_ge(stored[s], 16 * (PASSES + 1))

        @block.tensor
        def _(pe):
            def turn_block(i, unit, k):
                layer, s = divmod(unit % UNITS, STREAMS)
                src = x_in[s] if layer == 0 else z[s]
                if layer == 0:
                    pe.wait_ge(x_loaded[s], i * 16 + 16 * (unit // UNITS + 1))
                else:
                    pe.wait_ge(z_ready, i * (STREAMS * NT) + NT * (s + 1))
                wait(pe, turn_read, nth(i, unit, KO, k - 2))
                bank = turn[(unit * KO + k) % 2]
                for t in range(NT):
                    mm = pe.transpose(bank[:, t * P:(t + 1) * P], src[:, t, k * P:(k + 1) * P], eye)
                mm.then_inc(turned, 1)

            def work_bank(i, use):
                wait(pe, work_free, used(i, use - RING))
                return work[use % RING]

            def query(i, unit, j):
                layer, s = divmod(unit % UNITS, STREAMS)
                d, m = divmod(j, KO)
                pe.wait_ge(ht_ready, nth(i, unit, KO, KO - 1))
                pe.wait_ge((first_split, second_split)[layer], d + 1)
                bank = work_bank(i, query_use(unit, j))
                pairs = [(w[:, layer, d, k, m * P:(m + 1) * P], h[s][:, k, :])
                         for k in range(KO) for w, h in three_products(wq_hi, wq_lo, ht_hi, ht_lo)]
                for n, (w, h) in enumerate(pairs):
                    mm = pe.matmul(bank[:], w, h, start=(n == 0), stop=(n == len(pairs) - 1))
                return mm

            def scores(i, unit, turn_next):
                s = unit % STREAMS
                pe.wait_ge(work_free, used(i, query_use(unit, QB - 1)))
                wait(pe, score_ready, nth(i, unit, 1, -1))
                for t in range(NT):
                    if t == NT // 2 and turn_next:
                        turn_block(i, unit + 1, 2)
                    pairs = [(h[s][:, m, t * P:(t + 1) * P], q[:, m, t, :, :])
                             for m in range(KO) for h, q in three_products(ht_hi, ht_lo, q_hi, q_lo)]
                    for n, (h, q) in enumerate(pairs):
                        mm = pe.matmul(score_ps[:, t, :, :], h, q, start=(n == 0), stop=(n == len(pairs) - 1))
                mm.then_inc(score_full, 1)

            def value(i, unit, t, uses=1):
                layer, s = divmod(unit % UNITS, STREAMS)
                pe.wait_ge((first_split, second_split)[layer], 3)
                bank = work_bank(i, value_use(unit, t))
                pairs = [(h[s][:, k, t * P:(t + 1) * P], w[:, layer, k, :])
                         for k in range(KO) for h, w in three_products(ht_hi, ht_lo, wv_hi, wv_lo)]
                for n, (h, w) in enumerate(pairs):
                    mm = pe.matmul(bank[:, 0:H], h, w, start=(n == 0), stop=(n == len(pairs) - 1))
                mm.then_inc(work_full, uses)

            def contexts(i, unit):
                pe.wait_ge(prob_lo_ready, nth(i, unit, 1, 0))
                pe.wait_ge(ones_set, nth(i, unit, 1, 0))
                for t in range(NT):
                    pe.wait_ge(v_lo_ready, nth(i, unit, NT, t))
                    bank = work_bank(i, context_use(unit, t))
                    for n, (p, v) in enumerate(three_products(prob_hi, prob_lo, v_hi, v_lo)):
                        mm = pe.matmul(bank[:, 0:HC], p[:, t, :], v[:, t, :], start=(n == 0), stop=(n == 2))
                    mm.then_inc(work_full, 1)

            def one_pass(i, last):
                for unit in range(UNITS):
                    more = not (last and unit == UNITS - 1)
                    more_turns = not (last and unit >= UNITS - 2)
                    for t in range(1, NT):
                        value(i, unit, t, uses=1 if more or t < NT - 1 else 2)
                    if more:
                        query(i, unit + 1, 0).then_inc(work_full, 1)
                    contexts(i, unit)
                    if more:
                        for j in range(1, QB):
                            query(i, unit + 1, j).then_inc(work_full, 1)
                        value(i, unit + 1, 0)
                    if more_turns:
                        turn_block(i, unit + 2, 0)
                        turn_block(i, unit + 2, 1)
                    if more:
                        scores(i, unit + 1, more_turns)

            pe.wait_ge(const_in, 16)
            for k in range(KO):
                turn_block(0, 0, k)
            query(0, 0, 0).then_inc(work_full, 1 + NT)
            for j in range(1, QB):
                query(0, 0, j).then_inc(work_full, 1)
            value(0, 0, 0)
            turn_block(0, 1, 0)
            turn_block(0, 1, 1)
            scores(0, 0, True)
            with pe.Fori(0, PASSES - 1) as i:
                one_pass(i, False)
            one_pass(PASSES - 1, True)

        @block.scalar
        def _(act):
            def weight_hi(n):
                act.wait_ge(stage_in[n], 16)
                nc.scalar.activation(weight_halves[n][0], stage[n], ACT.Copy).then_inc(upper_split, 1)

            def turn_out(i, unit, k):
                layer, s = divmod(unit % UNITS, STREAMS)
                act.wait_ge(turned, nth(i, unit, KO, k))
                wait(act, ht_ready, nth(i, unit, KO, k - KO))
                bank = turn[(unit * KO + k) % 2]
                for out in (ht_full[:, k, :], ht_hi[s][:, k, :]):
                    if layer == 0:
                        op = nc.scalar.activation(out, bank[:], ACT.Copy)
                    else:
                        op = nc.scalar.activation(out, bank[:], ACT.Relu, bias=shift_f[:, k:k + 1],
                                                  scale=gain_f[:, k:k + 1])
                op.then_inc(turn_read, 1)

            def query_hi(i, unit, j):
                d, m = divmod(j, KO)
                use = query_use(unit, j)
                act.wait_ge(work_full, used(i, use))
                nc.scalar.activation(q_hi[:, m, :, d, :], work[use % RING][:], ACT.Copy).then_inc(q_hi_ready, 1)

            def exponentials(i, unit):
                act.wait_ge(score_ready, nth(i, unit, 1, 0))
                nc.scalar.activation(prob[:], score_l[:], ACT.Exp, scale=SCALE).then_inc(exp_ready, 1)

            def probabilities_hi(i, unit):
                act.wait_ge(prob_ready, nth(i, unit, 1, 0))
                nc.scalar.activation(prob_hi[:], prob[:], ACT.Copy).then_inc(prob_hi_ready, 1)

            def value_hi(i, unit, t):
                act.wait_ge(work_free, used(i, value_use(unit, t)))
                nc.scalar.activation(v_hi[:, t, 0:H], v_full[:, t, :], ACT.Copy).then_inc(v_hi_ready, 1)

            def contexts_out(i, unit):
                layer, s = divmod(unit % UNITS, STREAMS)
                if layer == 0:
                    act.wait_ge(stored[s], 16 * (i + unit // UNITS + 1))
                for t in range(NT):
                    use = context_use(unit, t)
                    act.wait_ge(work_full, used(i, use))
                    nc.scalar.activation(z[s][:, t, :], work[use % RING][:, 0:HC], ACT.Copy).then_inc(ctx_ready, 1)

            def final_normalise(i, s):
                act.wait_ge(foffset_ready, i * STREAMS + s + 1)
                for t in range(NT):
                    nc.scalar.activation(z[s][:, t, 0:H], z[s][:, t, 0:H], ACT.Identity, scale=frstd[s][:, t:t + 1],
                                         bias=foffset[s][:, t:t + 1]).then_inc(x1_ready, 1)

            def normalise(i, s):
                act.wait_ge(offset_ready, i * STREAMS + s + 1)
                for t in range(NT):
                    nc.scalar.activation(z[s][:, t, 0:H], z[s][:, t, 0:H], ACT.Identity, scale=rstd[:, t:t + 1],
                                         bias=offset[:, t:t + 1]).then_inc(z_ready, 1)

            def up_to_contexts(i, unit, last):
                more = not (last and unit == UNITS - 1)
                if more:
                    for k in range(KO):
                        turn_out(i, unit + 1, k)
                exponentials(i, unit)
                value_hi(i, unit, 0)
                value_hi(i, unit, 1)
                probabilities_hi(i, unit)
                value_hi(i, unit, 2)
                value_hi(i, unit, 3)
                if more:
                    query_hi(i, unit + 1, 0)
                contexts_out(i, unit)

            def one_pass(i, last):
                for unit in range(UNITS):
                    more = not (last and unit == UNITS - 1)
                    if more:
                        query_hi(i, unit + 1, 1)
                        query_hi(i, unit + 1, 2)
                    if unit < STREAMS:
                        normalise(i, unit)
                    if more:
                        for j in range(3, QB):
                            query_hi(i, unit + 1, j)
                        up_to_contexts(i, unit + 1, last)
                    if unit >= STREAMS:
                        final_normalise(i, unit - STREAMS)

            weight_hi(0)
            for k in range(KO):
                turn_out(0, 0, k)
            weight_hi(1)
            weight_hi(2)
            query_hi(0, 0, 0)
            for j in range(1, QB):
                query_hi(0, 0, j)
                if j < 4:
                    weight_hi(j + 2)
            act.wait_ge(bias_in, 16 * 5)
            up_to_contexts(0, 0, False)
            with act.Fori(0, PASSES - 1) as i:
                one_pass(i, False)
            one_pass(PASSES - 1, True)

        @block.gpsimd
        def _(pool):
            def weight_lo(n):
                pool.wait_ge(upper_split, n + 1)
                hi, lo = weight_halves[n]
                nc.gpsimd.tensor_tensor(lo, stage[n], hi.bitcast(F32), ALU.subtract).then_inc(second_split, 1)

            def keep_masks(i, s):
                pool.wait_ge(adj_loaded[s], 64 * (i + 1))
                tri = [const[:, c:c + P].unsqueeze(1).to_broadcast([P, NT, P]) for c in (C_LE, C_GT)]
                nc.gpsimd.tensor_tensor(keep_l[s][:], a_tr[s][:], tri[0], ALU.mult)
                nc.gpsimd.tensor_tensor(a_nat[s][:], a_nat[s][:], tri[1], ALU.mult).then_inc(keep_ready[s], 1)

            def value_lo(i, unit, t):
                pool.wait_ge(v_hi_ready, nth(i, unit, NT, t))
                nc.gpsimd.tensor_tensor(v_lo[:, t, 0:H], v_full[:, t, :], v_hi[:, t, 0:H].bitcast(F32),
                                        ALU.subtract).then_inc(v_lo_ready, 1)
                if t == 0:
                    nc.gpsimd.memset(v_hi[:, :, H:HC].bitcast(F32), 1.0)
                    nc.gpsimd.memset(v_lo[:, :, H:HC].bitcast(F32), 0.0).then_inc(ones_set, 1)

            def roots(i, unit):
                pool.wait_ge(var_ready, nth(i, unit, 1, 0))
                nc.gpsimd.tensor_tensor(sigma[:], var[:], powers[:, 0, :], ALU.pow).then_inc(sigma_ready, 1)

            def final_roots(i, s):
                pool.wait_ge(fvar_ready, i * STREAMS + s + 1)
                nc.gpsimd.tensor_tensor(frstd[s][:], fvar[:], powers[:, 1, :], ALU.pow).then_inc(frstd_ready, 1)

            def one_pass(i, last):
                for unit in range(UNITS):
                    layer, s = divmod(unit, STREAMS)
                    more = not (last and unit == UNITS - 1)
                    if unit == 0:
                        keep_masks(i, 1)
                    if unit == UNITS - 1 and more:
                        keep_masks(i + 1, 0)
                    if more:
                        for t in range(NT):
                            value_lo(i, unit + 1, t)
                    if layer == 1:
                        final_roots(i, s)
                    if more:
                        roots(i, unit + 1)

            for s in range(STREAMS):
                nc.gpsimd.memset(a_tr[s][:], 0.0).then_inc(cleared, 1)
                nc.gpsimd.memset(a_nat[s][:], 0.0).then_inc(cleared, 1)
            nc.gpsimd.memset(powers[:, 0, 0:2], 0.5).then_inc(stored[0], 16)
            nc.gpsimd.memset(powers[:, 0, 2:NT], 0.5).then_inc(stored[1], 16)
            nc.gpsimd.memset(powers[:, 1, :], -0.5).then_inc(powers_set, 1)
            pool.wait_ge(powers_set, 1)
            pool.wait_ge(const_in, 16)
            keep_masks(0, 0)
            for n in range(3, 6):
                weight_lo(n)
            for t in range(NT):
                value_lo(0, 0, t)
            roots(0, 0)
            with pool.Fori(0, PASSES - 1) as i:
                one_pass(i, False)
            one_pass(PASSES - 1, True)

        @block.vector
        def _(dve):
            def weight_lo(n):
                dve.wait_ge(upper_split, n + 1)
                hi, lo = weight_halves[n]
                nc.vector.tensor_tensor(lo, stage[n], hi.bitcast(F32), ALU.subtract).then_inc(first_split, 1)

            def turn_lo(i, unit, k):
                s = unit % STREAMS
                dve.wait_ge(turn_read, nth(i, unit, KO, k))
                nc.vector.tensor_tensor(ht_lo[s][:, k, :], ht_full[:, k, :], ht_hi[s][:, k, :].bitcast(F32),
                                        ALU.subtract).then_inc(ht_ready, 1)

            def query_lo(i, unit, j):
                d, m = divmod(j, KO)
                dve.wait_ge(q_hi_ready, nth(i, unit, QB, j))
                bank = work[query_use(unit, j) % RING][:].rearrange("p (t i) -> p t i", t=NT)
                op = nc.vector.tensor_tensor(q_lo[:, m, :, d, :], bank, q_hi[:, m, :, d, :].bitcast(F32),
                                             ALU.subtract)
                first = isinstance(i, int) and i == 0 and unit == 0 and j == 0
                op.then_inc(work_free, 1 + NT if first else 1)

            def mask_scores(i, unit):
                s = unit % STREAMS
                dve.wait_ge(score_full, nth(i, unit, 1, 0))
                if unit % UNITS < STREAMS:
                    dve.wait_ge(keep_ready[s], i + unit // UNITS + 1)
                nc.vector.tensor_tensor(score_l[:], score_ps[:, :, 0, :], keep_l[s][:], ALU.mult)
                nc.vector.tensor_tensor(score_r[:], score_ps[:, :, 1, :], a_nat[s][:], ALU.mult).then_inc(masked, 1)
                dve.wait_ge(masked, nth(i, unit, 1, 0))
                nc.vector.tensor_tensor(score_l[:], score_l[:], score_r[:], ALU.add).then_inc(score_ready, 1)

            def probabilities(i, unit):
                s = unit % STREAMS
                dve.wait_ge(exp_ready, nth(i, unit, 1, 0))
                nc.vector.tensor_tensor(prob[:], prob[:], a_tr[s][:], ALU.mult).then_inc(prob_ready, 1)

            def probabilities_lo(i, unit):
                dve.wait_ge(prob_hi_ready, nth(i, unit, 1, 0))
                nc.vector.tensor_tensor(prob_lo[:], prob[:], prob_hi[:].bitcast(F32), ALU.subtract)\
                    .then_inc(prob_lo_ready, 1)

            def biased_value(i, unit, t, uses=1):
                layer = unit % UNITS // STREAMS
                use = value_use(unit, t)
                dve.wait_ge(work_full, used(i, use))
                nc.vector.tensor_tensor(v_full[:, t, :], work[use % RING][:, 0:H],
                                        bias[:, layer, :], ALU.add).then_inc(work_free, uses)

            def context_stats(i, unit, t):
                dve.wait_ge(ctx_ready, nth(i, unit, NT, t))
                nc.vector.bn_stats(stats[:, t, :], work[context_use(unit, t) % RING][:, 0:H])\
                    .then_inc(work_free, 1)

            def normalise(i, unit):
                layer, s = divmod(unit, STREAMS)
                dve.wait_ge(work_free, used(i, context_use(unit, NT - 1)))
                nc.vector.tensor_scalar(denom[:], z[s][:, :, H], 1e-10, EPS, ALU.add, ALU.mult)
                for t in range(NT):
                    op = nc.vector.bn_aggr(mv[:, t, :], stats[:, t, :])
                op.then_inc(mean_ready, 1)
                dve.wait_ge(mean_ready, nth(i, unit, 1, 0))
                nc.vector.tensor_scalar(var[:], mv[:, :, 1], float(H) / (H - 1), None, ALU.mult)\
                    .then_inc(var_ready, 1)
                dve.wait_ge(sigma_ready, nth(i, unit, 1, 0))
                nc.vector.tensor_tensor(denom[:], denom[:], sigma[:], ALU.add).then_inc(denom_ready, 1)
                dve.wait_ge(denom_ready, nth(i, unit, 1, 0))
                nc.vector.reciprocal(rstd[:], denom[:]).then_inc(rstd_ready, 1)
                dve.wait_ge(rstd_ready, nth(i, unit, 1, 0))
                if layer == 0:
                    nc.vector.scalar_tensor_tensor(offset[:], mv[:, :, 0], -1.0, rstd[:], ALU.mult, ALU.mult)\
                        .then_inc(offset_ready, 1)

            def gain_and_shift(i, s, t):
                nc.vector.scalar_tensor_tensor(z[s][:, t, 0:H], z[s][:, t, 0:H], mv[:, t, 0:1], gain[:],
                                               ALU.subtract, ALU.mult).then_inc(gained, 1)
                dve.wait_ge(gained, i * (STREAMS * NT) + s * NT + t + 1)
                nc.vector.scalar_tensor_tensor(z[s][:, t, 0:H], z[s][:, t, 0:H], rstd[:, t:t + 1], shift[:],
                                               ALU.mult, ALU.add).then_inc(scaled, 1)

            def add_residual(i, s):
                dve.wait_ge(x_copied[s], 16 * (i + 1))
                for t in range(NT):
                    dve.wait_ge(scaled, i * (STREAMS * NT) + s * NT + t + 1)
                    nc.vector.scalar_tensor_tensor(z[s][:, t, 0:H], z[s][:, t, 0:H], 0.0, x_res[s][:, t, :],
                                                   ALU.max, ALU.add).then_inc(summed, 1)

            def final_stats(i, s, t):
                dve.wait_ge(summed, i * (STREAMS * NT) + s * NT + t + 1)
                nc.vector.bn_stats(fstats[:, t, :], z[s][:, t, 0:H]).then_inc(fstats_ready, 1)

            def final_var(i, s):
                dve.wait_ge(fstats_ready, i * (STREAMS * NT) + (s + 1) * NT)
                nc.vector.memset(fvar[:], 1e-5)
                for t in range(NT):
                    op = nc.vector.bn_aggr(fmv[:, t, :], fstats[:, t, :])
                op.then_inc(fmean_ready, 1)
                dve.wait_ge(fmean_ready, i * STREAMS + s + 1)
                nc.vector.tensor_tensor(fvar[:], fvar[:], fmv[:, :, 1], ALU.add).then_inc(fvar_ready, 1)

            def final_offset(i, s):
                dve.wait_ge(frstd_ready, i * STREAMS + s + 1)
                nc.vector.scalar_tensor_tensor(foffset[s][:], fmv[:, :, 0], -1.0, frstd[s][:], ALU.mult, ALU.mult)\
                    .then_inc(foffset_ready, 1)

            def one_pass(i, last):
                for unit in range(UNITS):
                    more = not (last and unit == UNITS - 1)
                    layer, s = divmod(unit, STREAMS)
                    normalise(i, unit)
                    if more:
                        for j in range(1, QB):
                            query_lo(i, unit + 1, j)
                            if layer == 1 and j > 1:
                                gain_and_shift(i, s, j - 2)
                        up_to_contexts(i, unit + 1, last, s if layer == 1 else None)
                    else:
                        for t in range(NT):
                            gain_and_shift(i, s, t)
                        add_residual(i, s)
                        for t in range(NT):
                            final_stats(i, s, t)
                        final_var(i, s)
                        final_offset(i, s)

            def up_to_contexts(i, unit, last, s):
                more = not (last and unit == UNITS - 1)
                if more:
                    turn_lo(i, unit + 1, 0)
                biased_value(i, unit, 0)
                if more:
                    turn_lo(i, unit + 1, 1)
                if s is not None:
                    add_residual(i, s)
                if more:
                    turn_lo(i, unit + 1, 2)
                mask_scores(i, unit)
                biased_value(i, unit, 1)
                probabilities(i, unit)
                biased_value(i, unit, 2)
                probabilities_lo(i, unit)
                biased_value(i, unit, 3, uses=1 if more else 2)
                for t in range(NT):
                    if t == 3 and more:
                        query_lo(i, unit + 1, 0)
                    if s is not None:
                        final_stats(i, s, t)
                for t in range(NT):
                    if t == 2 and s is not None:
                        final_var(i, s)
                    context_stats(i, unit, t)
                if s is not None:
                    final_offset(i, s)

            weight_lo(0)
            for k in range(KO):
                turn_lo(0, 0, k)
            weight_lo(1)
            query_lo(0, 0, 0)
            weight_lo(2)
            for j in range(1, QB):
                query_lo(0, 0, j)
            dve.wait_ge(bias_in, 16 * 5)
            up_to_contexts(0, 0, False, None)
            with dve.Fori(0, PASSES - 1) as i:
                one_pass(i, False)
            one_pass(PASSES - 1, True)


def softmax_layers(nc, cm, x1, adj_t, w_nbr_t, b_nbr, ln_w, ln_b, table, out):
    H, KO, HC = cm.H, cm.KO, cm.HC
    LAYERS = w_nbr_t[0].shape[0]
    PASSES = x1.shape[0] // (TOK * STREAMS)
    SCALE = float(H) ** -0.5
    SIDES = 3
    VB = NT * SIDES
    WN = VB + NT
    RING = 4
    VF = 4
    assert LAYERS == 2 and WN * UNITS % RING == 0 and UNITS * KO % 2 == 0

    x_v = x1.rearrange("(i s t p) h -> i s p t h", s=STREAMS, t=NT, p=P)
    out_v = out.rearrange("a n h -> (a n) h").rearrange("(i s t p) h -> i s p t h", s=STREAMS, t=NT, p=P)
    adj_t_v = adj_t.rearrange("(i s t b) r c -> i s b r t c", s=STREAMS, t=NT, b=2)

    with ExitStack() as ctx:
        def sb(name, shape, dt=F32):
            return ctx.enter_context(nc.sbuf_tensor("s_" + name, shape, dt))

        def sem(name):
            return ctx.enter_context(nc.semaphore("s_" + name))

        const = sb("const", [P, C_SEL])
        rows_f = sb("rows_f", [NT, C_ALL - C_SEL])
        pick_row = sb("pick_row", [NT, NT, P], F32R)
        block_rows = sb("block_rows", [2, P], BF16)
        block_cols = sb("block_cols", [2, 4 * P], BF16)
        one = sb("one", [P, 1])
        power = sb("power", [P, NT])
        w_hi = sb("w_hi", [P, LAYERS, SIDES, KO, H], F32R)
        w_lo = sb("w_lo", [P, LAYERS, SIDES, KO, H], F32R)
        bias = sb("bias", [P, SIDES, LAYERS, H])
        gain_f = sb("gain_f", [P, KO])
        shift_f = sb("shift_f", [P, KO])
        gain = sb("gain", [P, H])
        shift = sb("shift", [P, H])
        x_in = [sb(f"x_in{s}", [P, NT, H]) for s in range(STREAMS)]
        z = [sb(f"z{s}", [P, NT, H]) for s in range(STREAMS)]
        ht = [sb(f"ht{s}", [P, KO, 2, TOK], F32R) for s in range(STREAMS)]
        ht_hi = [h[:, :, 0, :] for h in ht]
        ht_lo = [h[:, :, 1, :] for h in ht]
        a_tr = [sb(f"a_tr{s}", [P, NT, P]) for s in range(STREAMS)]
        x_res = [sb(f"x_res{s}", [P, NT, H]) for s in range(STREAMS)]
        ht_full = sb("ht_full", [P, KO, TOK])
        v_hi = sb("v_hi", [P, NT, 2, HC], F32R)
        v_lo = sb("v_lo", [P, NT, 2, HC], F32R)
        v_full = sb("v_full", [P, VF, H])
        v_own = sb("v_own", [P, NT, H])
        row_max = sb("row_max", [P, NT])
        neg_max = sb("neg_max", [NT, P], F32R)
        score = sb("score", [P, NT, P])
        part = sb("part", [P, NT, P])
        expo = sb("expo", [P, NT, P])
        prob = [sb(f"prob{n}", [P, NT, P]) for n in range(2)]
        prob_hi = [sb(f"prob_hi{n}", [P, NT, P], F32R) for n in range(2)]
        prob_lo = [sb(f"prob_lo{n}", [P, NT, P], F32R) for n in range(2)]
        own = sb("own", [P, NT])
        stats = sb("stats", [P, NT, 6])
        mv = sb("mv", [P, NT, 2])
        total = sb("total", [P, NT])
        var = sb("var", [P, NT])
        rstd = sb("rstd", [P, NT])
        fmv = sb("fmv", [P, NT, 2])
        offset = sb("offset", [P, NT])
        foffset = [sb(f"foffset{s}", [P, NT]) for s in range(STREAMS)]
        fvar = sb("fvar", [P, NT])
        frstd = [sb(f"frstd{s}", [P, NT]) for s in range(STREAMS)]

        work = [ctx.enter_context(nc.psum_tensor(f"s_work{n}", [P, 512], F32)) for n in range(RING)]
        turn = [ctx.enter_context(nc.psum_tensor(f"s_turn{n}", [P, 512], F32)) for n in range(2)]
        score_ps = ctx.enter_context(nc.psum_tensor("s_score_ps", [P, NT, 2, P], F32))
        max_ps = turn[0][0:NT, 0:P]
        sum_ps = score_ps[:, 0, 0, 0:NT]

        eye = const[:, C_EYE:C_EYE + P]

        def over_tiles(c):
            return const[:, c:c + P].unsqueeze(1).to_broadcast([P, NT, P])

        const_in, bias_in = sem("const_in"), sem("bias_in")
        stage_in = [sem(f"stage_in{n}") for n in range(2 * SIDES)]
        upper_split, first_split, second_split = sem("upper_split"), sem("first_split"), sem("second_split")
        x_loaded = [sem(f"x_loaded{s}") for s in range(STREAMS)]
        x_copied = [sem(f"x_copied{s}") for s in range(STREAMS)]
        adj_loaded = [sem(f"adj_loaded{s}") for s in range(STREAMS)]
        stored = [sem(f"stored{s}") for s in range(STREAMS)]
        cleared, power_set, ones_set, rows_cast = sem("cleared"), sem("power_set"), sem("ones_set"), sem("rows_cast")
        turned, turn_read, ht_ready = sem("turned"), sem("turn_read"), sem("ht_ready")
        work_full, work_free = sem("work_full"), sem("work_free")
        score_full, max_ready, max_turned = sem("score_full"), sem("max_ready"), sem("max_turned")
        neg_ready, shifted, exp_ready, sums_full = sem("neg_ready"), sem("shifted"), sem("exp_ready"), sem("sums_full")
        prob_ready, prob_hi_ready, prob_lo_ready = sem("prob_ready"), sem("prob_hi_ready"), sem("prob_lo_ready")
        diag_ready, own_ready = sem("diag_ready"), sem("own_ready")
        v_hi_ready, v_lo_ready, ctx_ready, sums_read = sem("v_hi_ready"), sem("v_lo_ready"), sem("ctx_ready"), sem("sums_read")
        stats_ready, mean_ready, total_ready, var_ready, rstd_ready, z_ready = (
            sem("stats_ready"), sem("mean_ready"), sem("total_ready"), sem("var_ready"), sem("rstd_ready"), sem("z_ready"))
        offset_ready, foffset_ready = sem("offset_ready"), sem("foffset_ready")
        normed, gained, scaled, summed, fstats_ready = sem("normed"), sem("gained"), sem("scaled"), sem("summed"), sem("fstats_ready")
        fmean_ready, fvar_ready, frstd_ready, out_ready = sem("fmean_ready"), sem("fvar_ready"), sem("frstd_ready"), sem("out_ready")
        squared, part_copied, joined = sem("squared"), sem("part_copied"), sem("joined")

        def value_job(j):
            return divmod(j, SIDES)

        def freed(i, unit, j):
            return nth(i, unit, WN, j) + RING

        stage = [b[:, 0:KO, :] for b in (v_own, z[0], z[1], x_res[0], x_res[1], z[0])]
        weight_halves = [(w_hi[:, l, n], w_lo[:, l, n]) for l in range(LAYERS) for n in range(SIDES)]

        block = ctx.enter_context(nc.Block())

        @block.sync
        def _(sp):
            def load_x(i, s):
                sp.dma_start(x_in[s][:], x_v[i, s]).then_inc(x_loaded[s], 16)

            def load_adj(i, s):
                for b in range(2):
                    h = slice(b * 64, b * 64 + 64)
                    sp.dma_start(a_tr[s][h, :, h], adj_t_v[i, s, b]).then_inc(adj_loaded[s], 16)

            def small_loads():
                sp.wait_ge(cleared, 2)
                load_adj(0, 0)
                for m in range(SIDES):
                    sp.dma_start(bias[:, m], b_nbr[m].partition_broadcast(P)).then_inc(bias_in, 16)
                sp.dma_start(gain_f[:], ln_w[0].rearrange("(k p) -> p k", p=P),
                             allow_slow_non_contiguous=True).then_inc(bias_in, 16)
                sp.dma_start(shift_f[:], ln_b[0].rearrange("(k p) -> p k", p=P),
                             allow_slow_non_contiguous=True).then_inc(bias_in, 16)
                sp.dma_start(gain[:], ln_w[1].partition_broadcast(P)).then_inc(bias_in, 16)
                sp.dma_start(shift[:], ln_b[1].partition_broadcast(P)).then_inc(bias_in, 16)
                load_x(0, 1)
                load_adj(0, 1)

            sp.dma_start(const[:], table[:, 0:C_SEL]).then_inc(const_in, 16)
            load_x(0, 0)
            sp.dma_start(rows_f[:], table[0:NT, C_SEL:C_ALL]).then_inc(const_in, 16)
            weights = [w_nbr_t[n][l] for l in range(LAYERS) for n in range(SIDES)]
            for n, w in enumerate(weights):
                if n == 3:
                    small_loads()
                if n == 5:
                    sp.wait_ge(first_split, 2)
                sp.dma_start(stage[n], w.rearrange("(k p) o -> p k o", p=P)).then_inc(stage_in[n], 16)
            sp.wait_ge(second_split, 3)

            def one_pass(i, last):
                for s in range(STREAMS):
                    sp.wait_ge(x_loaded[s], 16 * (i + 1))
                    wait(sp, summed, i * (STREAMS * NT) + (s + 1 - STREAMS) * NT)
                    sp.dma_start(x_res[s][:], x_in[s][:]).then_inc(x_copied[s], 16)
                    if not last:
                        sp.wait_ge(turned, nth(i, s, KO, KO - 1))
                        sp.wait_ge(x_copied[s], 16 * (i + 1))
                        load_x(i + 1, s)
                for s in range(STREAMS):
                    if not last:
                        sp.wait_ge(own_ready, nth(i, 2 + s, 1, 0))
                        load_adj(i + 1, s)
                    sp.wait_ge(out_ready, i * (STREAMS * NT) + NT * (s + 1))
                    sp.dma_start(out_v[i, s], z[s][:]).then_inc(stored[s], 16)

            one_pass(0, False)
            with sp.Fori(1, PASSES - 1) as i:
                one_pass(i, False)
            one_pass(PASSES - 1, True)
            for s in range(STREAMS):
                sp.wait_ge(stored[s], 16 * (PASSES + 1))

        @block.tensor
        def _(pe):
            def turn_block(i, unit, k):
                layer, s = divmod(unit % UNITS, STREAMS)
                src = x_in[s] if layer == 0 else z[s]
                if layer == 0:
                    pe.wait_ge(x_loaded[s], i * 16 + 16 * (unit // UNITS + 1))
                else:
                    pe.wait_ge(z_ready, i * (STREAMS * NT) + NT * (s + 1))
                wait(pe, turn_read, nth(i, unit, KO, k - 2))
                bank = turn[(unit * KO + k) % 2]
                for t in range(NT):
                    mm = pe.transpose(bank[:, t * P:(t + 1) * P], src[:, t, k * P:(k + 1) * P], eye)
                mm.then_inc(turned, 1)

            def work_bank(i, unit, j):
                pe.wait_ge(work_free, freed(i, unit, j - RING))
                return work[(unit * WN + j) % RING]

            def scores(i, unit):
                s = unit % STREAMS
                pe.wait_ge(ht_ready, nth(i, unit, KO, KO - 1))
                pe.wait_ge(sums_read, nth(i, unit, 1, 0))
                for bank in (0, 2):
                    pe.matmul(score_ps[:, bank:bank + 2, :, :], block_rows[:], block_cols[:], start=True,
                              stop=False, skip_group_check=True)
                for t in range(NT):
                    tile = slice(t * P, (t + 1) * P)
                    for k in range(KO):
                        pe.matmul(score_ps[:, t, :, :], ht_hi[s][:, k, tile], ht[s][:, k, :, tile],
                                  start=False, stop=False, skip_group_check=True)
                        mm = pe.matmul(score_ps[:, t, 0, :], ht_lo[s][:, k, tile], ht_hi[s][:, k, tile],
                                       start=False, stop=False, skip_group_check=True)
                mm.then_inc(score_full, 1)

            def turn_max(i, unit):
                pe.wait_ge(max_ready, nth(i, unit, 1, 0))
                pe.transpose(max_ps, row_max[:], eye).then_inc(max_turned, 1)

            def subtract_max(i, unit):
                pe.wait_ge(neg_ready, nth(i, unit, 1, 0))
                for t in range(NT):
                    mm = pe.matmul(score_ps[:, t, 0, :], pick_row[:, t, :], neg_max[:], start=False,
                                   stop=(t == NT - 1), skip_group_check=True)
                mm.then_inc(shifted, 1)

            def row_sums(i, unit):
                pe.wait_ge(exp_ready, nth(i, unit, 1, 0))
                for t in range(NT):
                    mm = pe.matmul(sum_ps[:, t:t + 1], expo[:, t, :], one[:], start=True, stop=True)
                mm.then_inc(sums_full, 1)

            def values(i, unit, j):
                layer, s = divmod(unit, STREAMS)
                t, side = value_job(j)
                pe.wait_ge((first_split, second_split)[layer], side + 1)
                bank = work_bank(i, unit, j)
                pairs = [(h[s][:, k, t * P:(t + 1) * P], w[:, layer, side, k, :])
                         for k in range(KO) for h, w in three_products(ht_hi, ht_lo, w_hi, w_lo)]
                for n, (h, w) in enumerate(pairs):
                    mm = pe.matmul(bank[:, 0:H], h, w, start=(n == 0), stop=(n == len(pairs) - 1))
                mm.then_inc(work_full, 1)

            def contexts(i, unit):
                pe.wait_ge(prob_lo_ready, nth(i, unit, 2, 1))
                for t in range(NT):
                    pe.wait_ge(v_lo_ready, nth(i, unit, 2 * NT, 2 * t + 1))
                    bank = work_bank(i, unit, VB + t)
                    pairs = [(p[n][:, t, :], v[:, t, n, :])
                             for n in range(2) for p, v in three_products(prob_hi, prob_lo, v_hi, v_lo)]
                    for n, (p, v) in enumerate(pairs):
                        mm = pe.matmul(bank[:, 0:HC], p, v, start=(n == 0), stop=(n == len(pairs) - 1))
                    mm.then_inc(work_full, 1)

            def one_pass(i, last):
                for unit in range(UNITS):
                    more = not (last and unit == UNITS - 1)
                    turn_max(i, unit)
                    for j in range(3):
                        values(i, unit, j)
                    subtract_max(i, unit)
                    values(i, unit, 3)
                    values(i, unit, 4)
                    row_sums(i, unit)
                    values(i, unit, 5)
                    if more:
                        turn_block(i, unit + 1, 0)
                        turn_block(i, unit + 1, 1)
                    values(i, unit, 6)
                    values(i, unit, 7)
                    if more:
                        turn_block(i, unit + 1, 2)
                    for j in range(8, VB):
                        values(i, unit, j)
                    if more:
                        scores(i, unit + 1)
                    contexts(i, unit)

            pe.wait_ge(const_in, 32)
            for k in range(KO):
                turn_block(0, 0, k)
            pe.wait_ge(rows_cast, 3)
            pe.wait_ge(ones_set, 1)
            scores(0, 0)
            with pe.Fori(0, PASSES - 1) as i:
                one_pass(i, False)
            one_pass(PASSES - 1, True)

        @block.scalar
        def _(act):
            def weight_hi(n):
                act.wait_ge(stage_in[n], 16)
                nc.scalar.activation(weight_halves[n][0], stage[n], ACT.Copy).then_inc(upper_split, 1)

            def turn_out(i, unit, k):
                layer, s = divmod(unit % UNITS, STREAMS)
                act.wait_ge(turned, nth(i, unit, KO, k))
                wait(act, ht_ready, nth(i, unit, KO, k - KO))
                bank = turn[(unit * KO + k) % 2]
                for out_ in (ht_full[:, k, :], ht_hi[s][:, k, :]):
                    if layer == 0:
                        op = nc.scalar.activation(out_, bank[:], ACT.Copy)
                    else:
                        op = nc.scalar.activation(out_, bank[:], ACT.Relu, bias=shift_f[:, k:k + 1],
                                                  scale=gain_f[:, k:k + 1])
                op.then_inc(turn_read, 1)

            def copy_part(i, unit):
                act.wait_ge(score_full, nth(i, unit, 1, 0))
                nc.scalar.activation(part[:], score_ps[:, :, 1, :], ACT.Copy).then_inc(part_copied, 1)

            def negate_max(i, unit):
                act.wait_ge(max_turned, nth(i, unit, 1, 0))
                nc.scalar.activation(neg_max[:], max_ps, ACT.Copy, scale=-1.0).then_inc(neg_ready, 1)

            def exponentials(i, unit):
                act.wait_ge(joined, nth(i, unit, 2, 1))
                nc.scalar.activation(expo[:], score[:], ACT.Exp, scale=SCALE).then_inc(exp_ready, 1)

            def probabilities_hi(i, unit):
                for n in range(2):
                    act.wait_ge(prob_ready, nth(i, unit, 2, n))
                    nc.scalar.activation(prob_hi[n][:], prob[n][:], ACT.Copy).then_inc(prob_hi_ready, 1)

            def values_hi(i, unit, t):
                for n in range(2):
                    act.wait_ge(work_free, freed(i, unit, t * SIDES + n))
                    nc.scalar.activation(v_hi[:, t, n, 0:H], v_full[:, (2 * t + n) % VF, :], ACT.Copy)\
                        .then_inc(v_hi_ready, 1)

            def final_normalise(i, s):
                act.wait_ge(foffset_ready, i * STREAMS + s + 1)
                for t in range(NT):
                    nc.scalar.activation(z[s][:, t, :], z[s][:, t, :], ACT.Identity, scale=frstd[s][:, t:t + 1],
                                         bias=foffset[s][:, t:t + 1]).then_inc(out_ready, 1)

            def normalise(i, unit):
                layer, s = divmod(unit, STREAMS)
                act.wait_ge(offset_ready, nth(i, unit, 1, 0))
                for t in range(NT):
                    nc.scalar.activation(z[s][:, t, :], z[s][:, t, :], ACT.Identity, scale=rstd[:, t:t + 1],
                                         bias=offset[:, t:t + 1]).then_inc((z_ready, normed)[layer], 1)

            def first_half(i, unit):
                negate_max(i, unit)
                values_hi(i, unit, 0)
                exponentials(i, unit)

            def second_half(i, unit, more):
                values_hi(i, unit, 1)
                if more:
                    turn_out(i, unit + 1, 0)
                probabilities_hi(i, unit)
                if more:
                    turn_out(i, unit + 1, 1)
                values_hi(i, unit, 2)
                if more:
                    turn_out(i, unit + 1, 2)
                values_hi(i, unit, 3)
                if more:
                    copy_part(i, unit + 1)

            def one_pass(i, last):
                for unit in range(UNITS):
                    more = not (last and unit == UNITS - 1)
                    if more:
                        first_half(i, unit + 1)
                    normalise(i, unit)
                    if more:
                        second_half(i, unit + 1, not (last and unit == UNITS - 2))
                    if unit >= STREAMS:
                        final_normalise(i, unit - STREAMS)

            act.wait_ge(const_in, 32)
            nc.scalar.activation(pick_row[:].rearrange("r t i -> r (t i)"), rows_f[:, 0:TOK], ACT.Copy)\
                .then_inc(rows_cast, 1)
            nc.scalar.activation(block_rows[:], rows_f[0:2, C_ROWS - C_SEL:C_COLS - C_SEL], ACT.Copy)\
                .then_inc(rows_cast, 1)
            nc.scalar.activation(block_cols[:], rows_f[0:2, C_COLS - C_SEL:C_ALL - C_SEL], ACT.Copy)\
                .then_inc(rows_cast, 1)
            for k in range(KO):
                turn_out(0, 0, k)
            for n in range(SIDES):
                weight_hi(n)
            copy_part(0, 0)
            first_half(0, 0)
            for n in range(SIDES, 2 * SIDES):
                weight_hi(n)
            act.wait_ge(bias_in, 16 * (SIDES + 4))
            second_half(0, 0, True)
            with act.Fori(0, PASSES - 1) as i:
                one_pass(i, False)
            one_pass(PASSES - 1, True)

        @block.gpsimd
        def _(pool):
            def weight_lo(n):
                pool.wait_ge(upper_split, n + 1)
                hi, lo = weight_halves[n]
                nc.gpsimd.tensor_tensor(lo, stage[n], hi.bitcast(F32), ALU.subtract).then_inc(second_split, 1)

            def values_lo(i, unit, t):
                for n in range(2):
                    pool.wait_ge(v_hi_ready, nth(i, unit, 2 * NT, 2 * t + n))
                    nc.gpsimd.tensor_tensor(v_lo[:, t, n, 0:H], v_full[:, (2 * t + n) % VF, :],
                                            v_hi[:, t, n, 0:H].bitcast(F32), ALU.subtract).then_inc(v_lo_ready, 1)

            def roots(i, unit):
                pool.wait_ge(var_ready, nth(i, unit, 1, 0))
                nc.gpsimd.tensor_tensor(rstd[:], var[:], power[:], ALU.pow).then_inc(rstd_ready, 1)

            def final_roots(i, s):
                pool.wait_ge(fvar_ready, i * STREAMS + s + 1)
                nc.gpsimd.tensor_tensor(frstd[s][:], fvar[:], power[:], ALU.pow).then_inc(frstd_ready, 1)

            def gain_and_shift(i, s, t):
                done = i * (STREAMS * NT) + s * NT + t + 1
                pool.wait_ge(normed, done)
                nc.gpsimd.tensor_tensor(z[s][:, t, :], z[s][:, t, :], gain[:], ALU.mult).then_inc(gained, 1)
                pool.wait_ge(gained, done)
                nc.gpsimd.tensor_tensor(z[s][:, t, :], z[s][:, t, :], shift[:], ALU.add).then_inc(scaled, 1)

            def one_pass(i, last):
                for unit in range(UNITS):
                    layer, s = divmod(unit, STREAMS)
                    more = not (last and unit == UNITS - 1)
                    if more:
                        values_lo(i, unit + 1, 0)
                    if layer == 1:
                        gain_and_shift(i, s, 0)
                        gain_and_shift(i, s, 1)
                    if more:
                        values_lo(i, unit + 1, 1)
                    if layer == 1:
                        gain_and_shift(i, s, 2)
                        gain_and_shift(i, s, 3)
                    if more:
                        values_lo(i, unit + 1, 2)
                    if layer == 1:
                        final_roots(i, s)
                    if more:
                        values_lo(i, unit + 1, 3)
                        roots(i, unit + 1)

            for s in range(STREAMS):
                nc.gpsimd.memset(a_tr[s][:], 0.0).then_inc(cleared, 1)
            nc.gpsimd.memset(v_hi[:, :, :, H:HC].bitcast(F32), 1.0).then_inc(stored[0], 16)
            nc.gpsimd.memset(v_lo[:, :, :, H:HC].bitcast(F32), 0.0).then_inc(stored[1], 16)
            nc.gpsimd.memset(one[:], 1.0).then_inc(ones_set, 1)
            nc.gpsimd.memset(power[:], -0.5).then_inc(power_set, 1)
            pool.wait_ge(power_set, 1)
            for n in range(3, 6):
                weight_lo(n)
            for t in range(NT):
                values_lo(0, 0, t)
            roots(0, 0)
            with pool.Fori(0, PASSES - 1) as i:
                one_pass(i, False)
            one_pass(PASSES - 1, True)

        @block.vector
        def _(dve):
            def weight_lo(n):
                dve.wait_ge(upper_split, n + 1)
                hi, lo = weight_halves[n]
                nc.vector.tensor_tensor(lo, stage[n], hi.bitcast(F32), ALU.subtract).then_inc(first_split, 1)

            def turn_lo(i, unit, k):
                s = unit % STREAMS
                dve.wait_ge(turn_read, nth(i, unit, KO, k))
                nc.vector.tensor_tensor(ht_lo[s][:, k, :], ht_full[:, k, :], ht_hi[s][:, k, :].bitcast(F32),
                                        ALU.subtract).then_inc(ht_ready, 1)

            def join(i, unit, n):
                nc.vector.tensor_tensor(score[:], score_ps[:, :, 0, :], part[:], ALU.add)\
                    .then_inc(joined, 1)

            def maximum(i, unit):
                dve.wait_ge(part_copied, nth(i, unit, 1, 0))
                join(i, unit, 0)
                dve.wait_ge(joined, nth(i, unit, 2, 0))
                nc.vector.tensor_reduce(row_max[:], score[:], AX.X, ALU.max).then_inc(max_ready, 1)

            def biased_value(i, unit, j):
                layer = unit % UNITS // STREAMS
                t, side = value_job(j)
                dve.wait_ge(work_full, nth(i, unit, WN, j))
                if side < 2:
                    if 2 * t >= VF:
                        dve.wait_ge(v_lo_ready, nth(i, unit, 2 * NT, 2 * t + side - VF))
                    dst = v_full[:, (2 * t + side) % VF, :]
                else:
                    dst = v_own[:, t, :]
                nc.vector.tensor_tensor(dst, work[(unit * WN + j) % RING][:, 0:H], bias[:, side, layer, :],
                                        ALU.add).then_inc(work_free, 1)

            def probabilities(i, unit):
                s = unit % STREAMS
                dve.wait_ge(exp_ready, nth(i, unit, 1, 0))
                if unit % UNITS < STREAMS:
                    dve.wait_ge(adj_loaded[s], 32 * (i + unit // UNITS + 1))
                wait(dve, sums_full, nth(i, unit, 1, 0))
                nc.vector.tensor_tensor(expo[:], expo[:], a_tr[s][:], ALU.mult).then_inc(squared, 1)
                dve.wait_ge(squared, nth(i, unit, 1, 0))
                for n, c in enumerate((C_LT, C_GT)):
                    nc.vector.tensor_tensor(prob[n][:], expo[:], over_tiles(c), ALU.mult).then_inc(prob_ready, 1)
                nc.vector.tensor_tensor(expo[:], expo[:], over_tiles(C_EYE), ALU.mult).then_inc(diag_ready, 1)
                dve.wait_ge(diag_ready, nth(i, unit, 1, 0))
                nc.vector.tensor_reduce(own[:], expo[:], AX.X, ALU.add).then_inc(own_ready, 1)
                dve.wait_ge(own_ready, nth(i, unit, 1, 0))
                nc.vector.scalar_tensor_tensor(total[:], sum_ps, 1e-10, own[:], ALU.mult, ALU.add)\
                    .then_inc(sums_read, 1)

            def probabilities_lo(i, unit):
                for n in range(2):
                    dve.wait_ge(prob_hi_ready, nth(i, unit, 2, n))
                    nc.vector.tensor_tensor(prob_lo[n][:], prob[n][:], prob_hi[n][:].bitcast(F32), ALU.subtract)\
                        .then_inc(prob_lo_ready, 1)

            def contexts_out(i, unit):
                layer, s = divmod(unit % UNITS, STREAMS)
                if layer == 0:
                    dve.wait_ge(stored[s], 16 * (i + unit // UNITS + 1))
                for t in range(NT):
                    j = VB + t
                    bank = work[(unit * WN + j) % RING]
                    dve.wait_ge(work_full, nth(i, unit, WN, j))
                    nc.vector.tensor_tensor(total[:, t:t + 1], total[:, t:t + 1], bank[:, H:H + 1], ALU.add)
                    nc.vector.scalar_tensor_tensor(z[s][:, t, :], v_own[:, t, :], own[:, t:t + 1], bank[:, 0:H],
                                                   ALU.mult, ALU.add).then_inc(work_free, 1)
                    dve.wait_ge(work_free, freed(i, unit, j))
                    nc.vector.bn_stats(stats[:, t, :], z[s][:, t, :]).then_inc(stats_ready, 1)

            def normalise(i, unit):
                layer, s = divmod(unit, STREAMS)
                dve.wait_ge(stats_ready, nth(i, unit, NT, NT - 1))
                nc.vector.scalar_tensor_tensor(total[:], total[:], 1e-12, total[:], ALU.mult, ALU.mult)\
                    .then_inc(total_ready, 1)
                for t in range(NT):
                    op = nc.vector.bn_aggr(mv[:, t, :], stats[:, t, :])
                op.then_inc(mean_ready, 1)
                dve.wait_ge(total_ready, nth(i, unit, 1, 0))
                dve.wait_ge(mean_ready, nth(i, unit, 1, 0))
                nc.vector.tensor_tensor(var[:], mv[:, :, 1], total[:], ALU.add).then_inc(var_ready, 1)
                dve.wait_ge(rstd_ready, nth(i, unit, 1, 0))
                nc.vector.scalar_tensor_tensor(offset[:], mv[:, :, 0], -1.0, rstd[:], ALU.mult, ALU.mult)\
                    .then_inc(offset_ready, 1)

            def add_residual(i, s):
                dve.wait_ge(x_copied[s], 16 * (i + 1))
                for t in range(NT):
                    dve.wait_ge(scaled, i * (STREAMS * NT) + s * NT + t + 1)
                    nc.vector.scalar_tensor_tensor(z[s][:, t, :], z[s][:, t, :], 0.0, x_res[s][:, t, :],
                                                   ALU.max, ALU.add).then_inc(summed, 1)

            def final_stats(i, s):
                for t in range(NT):
                    dve.wait_ge(summed, i * (STREAMS * NT) + s * NT + t + 1)
                    nc.vector.bn_stats(stats[:, t, :], z[s][:, t, :]).then_inc(fstats_ready, 1)

            def final_var(i, s):
                dve.wait_ge(fstats_ready, i * (STREAMS * NT) + (s + 1) * NT)
                nc.vector.memset(fvar[:], 1e-5)
                for t in range(NT):
                    op = nc.vector.bn_aggr(fmv[:, t, :], stats[:, t, :])
                op.then_inc(fmean_ready, 1)
                dve.wait_ge(fmean_ready, i * STREAMS + s + 1)
                nc.vector.tensor_tensor(fvar[:], fvar[:], fmv[:, :, 1], ALU.add).then_inc(fvar_ready, 1)

            def final_offset(i, s):
                dve.wait_ge(frstd_ready, i * STREAMS + s + 1)
                nc.vector.scalar_tensor_tensor(foffset[s][:], fmv[:, :, 0], -1.0, frstd[s][:], ALU.mult, ALU.mult)\
                    .then_inc(foffset_ready, 1)

            def up_to_contexts(i, unit, last, s):
                more = not (last and unit == UNITS - 1)
                for j in range(3):
                    biased_value(i, unit, j)
                dve.wait_ge(shifted, nth(i, unit, 1, 0))
                join(i, unit, 1)
                biased_value(i, unit, 3)
                biased_value(i, unit, 4)
                probabilities(i, unit)
                biased_value(i, unit, 5)
                if more:
                    turn_lo(i, unit + 1, 0)
                biased_value(i, unit, 6)
                if more:
                    turn_lo(i, unit + 1, 1)
                biased_value(i, unit, 7)
                probabilities_lo(i, unit)
                if more:
                    turn_lo(i, unit + 1, 2)
                biased_value(i, unit, 8)
                if s is not None:
                    add_residual(i, s)
                biased_value(i, unit, 9)
                biased_value(i, unit, 10)
                if s is not None:
                    final_stats(i, s)
                    final_var(i, s)
                biased_value(i, unit, 11)
                if s is not None:
                    final_offset(i, s)
                if more:
                    maximum(i, unit + 1)
                contexts_out(i, unit)

            def one_pass(i, last):
                for unit in range(UNITS):
                    layer, s = divmod(unit, STREAMS)
                    normalise(i, unit)
                    if not (last and unit == UNITS - 1):
                        up_to_contexts(i, unit + 1, last, s if layer == 1 else None)
                    else:
                        add_residual(i, s)
                        final_stats(i, s)
                        final_var(i, s)
                        final_offset(i, s)

            nc.vector.memset(own[:], 0.0).then_inc(work_free, RING)
            nc.vector.memset(total[:], 0.0).then_inc(sums_read, 1)
            for k in range(KO):
                turn_lo(0, 0, k)
            for n in range(3):
                weight_lo(n)
            dve.wait_ge(bias_in, 16 * (SIDES + 4))
            maximum(0, 0)
            up_to_contexts(0, 0, False, None)
            with dve.Fori(0, PASSES - 1) as i:
                one_pass(i, False)
            one_pass(PASSES - 1, True)


def resnorm_graph_blocks(nc, x, adj, adj_t, w, table, out):
    B, S, H = x.shape
    assert S == P // 2 and H % P == 0 and B * S % (TOK * STREAMS) == 0
    x1 = nc.dram_tensor("x1", (B * S, H), F32).ap()
    cm = Common(H)
    gated_layers(nc, cm, x, adj, adj_t, w["L0_gnn_W_left"], w["L0_gnn_W_right"], w["L0_gnn_W_lin"],
                 w["L0_gnn_b_lin"], w["L0_gnn_ln_a"], w["L0_gnn_ln_b"], table, x1)
    softmax_layers(nc, cm, x1, adj_t, [w["L1_gnn_Wl"], w["L1_gnn_Wr"], w["L1_gnn_Ws"]],
                   [w["L1_gnn_bl"], w["L1_gnn_br"], w["L1_gnn_bs"]], w["L1_gnn_ln_w"], w["L1_gnn_ln_b"], table, out)


_TURNED = ["L0_gnn_W_lin", "L1_gnn_Wl", "L1_gnn_Wr", "L1_gnn_Ws"]
_STRAIGHT = ["L0_gnn_W_left", "L0_gnn_W_right", "L0_gnn_b_lin", "L0_gnn_ln_a", "L0_gnn_ln_b",
             "L1_gnn_bl", "L1_gnn_bs", "L1_gnn_br", "L1_gnn_ln_w", "L1_gnn_ln_b"]


def kernel(**inputs):
    import numpy as _np
    import concourse.bacc as _bacc
    from concourse import mybir as _mybir
    from concourse.bass_utils import run_bass_kernel_spmd as _run

    host = {n: _np.ascontiguousarray(inputs[n]) for n in ["x", "adj"] + _STRAIGHT}
    host["adj_t"] = _np.ascontiguousarray(_np.transpose(_np.asarray(inputs["adj"]), (0, 2, 1)))
    for n in _TURNED:
        host[n] = _np.ascontiguousarray(_np.transpose(_np.asarray(inputs[n]), (0, 2, 1)))
    host["table"] = constants_table()

    nc = _bacc.Bacc("TRN2", target_bir_lowering=False, num_devices=1)
    ap = {n: nc.dram_tensor(f"in_{n}", a.shape, _mybir.dt.from_np(a.dtype), kind="ExternalInput").ap()
          for n, a in host.items()}
    out = nc.dram_tensor("out_0", host["x"].shape, F32, kind="ExternalOutput").ap()
    resnorm_graph_blocks(nc, ap["x"], ap["adj"], ap["adj_t"], ap, ap["table"], out)
    r = _run(nc, [{f"in_{n}": a for n, a in host.items()}], core_ids=[0])
    return r.results[0]["out_0"]
```

```python
from contextlib import ExitStack

import numpy as np

import concourse.bass as bass
from concourse import mybir

ALU = mybir.AluOpType
ACT = mybir.ActivationFunctionType
AX = mybir.AxisListType
F32 = mybir.dt.float32
F32R = mybir.dt.float32r
BF16 = mybir.dt.bfloat16

P = 128
NT = 4
TOK = NT * P
STREAMS = 2
UNITS = 4
BIG = 1e30

C_EYE, C_LE, C_GT, C_LT, C_SEL, C_ROWS, C_COLS = 0, 128, 256, 384, 512, 1024, 1152
C_ALL = 1664


def constants_table():
    c = np.zeros((P, C_ALL), np.float32)
    j, i = np.arange(P)[:, None], np.arange(P)[None, :]
    c[:, C_EYE:C_EYE + P] = i == j
    c[:, C_LE:C_LE + P] = i <= j
    c[:, C_GT:C_GT + P] = i > j
    c[:, C_LT:C_LT + P] = i < j
    for t in range(NT):
        c[t, C_SEL + t * P:C_SEL + (t + 1) * P] = 1.0
    second = (np.arange(P) >= P // 2).astype(np.float32)
    c[0, C_ROWS:C_ROWS + P] = 1 - second
    c[1, C_ROWS:C_ROWS + P] = second
    zero = np.zeros(P)
    c[0, C_COLS:C_COLS + 4 * P] = np.concatenate([-BIG * second, zero] * 2)
    c[1, C_COLS:C_COLS + 4 * P] = np.concatenate([-BIG * (1 - second), zero] * 2)
    return c


def nth(i, unit, per, k):
    return i * (UNITS * per) + (unit * per + k + 1)


def wait(eng, sem, value):
    if isinstance(value, int) and value <= 0:
        return
    eng.wait_ge(sem, value)


class Shared:

    def __init__(self, nc, ctx, H, layers):
        self.H = H
        self.KO = KO = H // P
        self.HC = H + 2

        def sb(name, shape, dt=F32):
            return ctx.enter_context(nc.sbuf_tensor("b_" + name, shape, dt))

        self.const = sb("const", [P, C_SEL])
        self.w_hi = sb("w_hi", [P, layers, 3, KO, H], F32R)
        self.w_lo = sb("w_lo", [P, layers, 3, KO, H], F32R)
        self.x_in = [sb(f"x_in{s}", [P, NT, H]) for s in range(STREAMS)]
        self.a_tr = [sb(f"a_tr{s}", [P, NT, P]) for s in range(STREAMS)]
        self.ht = [sb(f"ht{s}", [P, KO, 2, TOK], F32R) for s in range(STREAMS)]
        self.z = [sb(f"z{s}", [P, NT, self.HC]) for s in range(STREAMS)]
        self.ht_full = sb("ht_full", [P, KO, TOK])
        self.bias = sb("bias", [P, 3, layers, H])
        self.gain_f = sb("gain_f", [P, KO])
        self.shift_f = sb("shift_f", [P, KO])
        self.gain = sb("gain", [P, H])
        self.shift = sb("shift", [P, H])
        self.pick_row = sb("pick_row", [NT, NT, P], F32R)
        self.block_rows = sb("block_rows", [2, P], BF16)
        self.block_cols = sb("block_cols", [2, 4 * P], BF16)
        self.turn = [ctx.enter_context(nc.psum_tensor(f"b_turn{n}", [P, 512], F32)) for n in range(2)]
        self.score_ps = ctx.enter_context(nc.psum_tensor("b_score_ps", [P, NT, 2, P], F32))
        self.stored = [ctx.enter_context(nc.semaphore(f"b_stored{s}")) for s in range(STREAMS)]
        self.turned, self.turn_read, self.ht_ready, self.score_full = (
            ctx.enter_context(nc.semaphore("b_" + n)) for n in ("turned", "turn_read", "ht_ready", "score_full"))
        self.x_loaded = [ctx.enter_context(nc.semaphore(f"b_x_loaded{s}")) for s in range(STREAMS)]
        self.adj_loaded = [ctx.enter_context(nc.semaphore(f"b_adj_loaded{s}")) for s in range(STREAMS)]


def three_products(H_hi, H_lo, W_hi, W_lo):
    return ((H_hi, W_hi), (H_hi, W_lo), (H_lo, W_hi))


def symmetric_scores(pe, sh, s):
    ht, score_ps = sh.ht[s], sh.score_ps
    for bank in (0, 2):
        pe.matmul(score_ps[:, bank:bank + 2, :, :], sh.block_rows[:], sh.block_cols[:], start=True,
                  stop=False, skip_group_check=True)
    for t in range(NT):
        tile = slice(t * P, (t + 1) * P)
        for k in range(sh.KO):
            pe.matmul(score_ps[:, t, :, :], ht[:, k, 0, tile], ht[:, k, :, tile],
                      start=False, stop=False, skip_group_check=True)
            mm = pe.matmul(score_ps[:, t, 0, :], ht[:, k, 1, tile], ht[:, k, 0, tile],
                           start=False, stop=False, skip_group_check=True)
    mm.then_inc(sh.score_full, 1)


def gated_layers(nc, sh, x, x_t, adj, adj_t, w_left, w_right, w_lin_t, b_lin, ln_a, ln_b, table, x1,
                 next_w, next_b, next_ln_w, next_ln_b):
    H, KO, HC = sh.H, sh.KO, sh.HC
    const, w_hi, w_lo, x_in, a_tr = sh.const, sh.w_hi, sh.w_lo, sh.x_in, sh.a_tr
    z, ht_full, turn, score_ps, stored = sh.z, sh.ht_full, sh.turn, sh.score_ps, sh.stored
    ht_hi, ht_lo = ([h[:, :, half, :] for h in sh.ht] for half in range(2))
    LAYERS = w_left.shape[0]
    B = x.shape[0]
    PASSES = B * x.shape[1] // (TOK * STREAMS)
    SCALE = float(H) ** -0.5
    EPS = 1e-3
    QB, VB = 2 * KO, NT
    WN = QB + 2 * NT
    RING = 4
    assert LAYERS == 2 and WN * UNITS % RING == 0 and UNITS * KO % 2 == 0

    x_v = x.rearrange("a n h -> (a n) h").rearrange("(i s t p) h -> i s p t h", s=STREAMS, t=NT, p=P)
    x_t_v = x_t.rearrange("(k p) (i s t) -> i s p k t", p=P, s=STREAMS, t=TOK)
    x1_v = x1.rearrange("(i s t p) h -> i s p t h", s=STREAMS, t=NT, p=P)
    adj_v = adj.rearrange("(i s t b) r c -> i s b r t c", s=STREAMS, t=NT, b=2)
    adj_t_v = adj_t.rearrange("(i s t b) r c -> i s b r t c", s=STREAMS, t=NT, b=2)

    with ExitStack() as ctx:
        def sb(name, shape, dt=F32):
            return ctx.enter_context(nc.sbuf_tensor("g_" + name, shape, dt))

        def sem(name):
            return ctx.enter_context(nc.semaphore("g_" + name))

        bias = sb("bias", [P, LAYERS, H])
        gain_f = sb("gain_f", [P, KO])
        shift_f = sb("shift_f", [P, KO])
        gain = sb("gain", [P, H])
        shift = sb("shift", [P, H])
        powers = sb("powers", [P, 2, NT])
        x_res = [sb(f"x_res{s}", [P, NT, H]) for s in range(STREAMS)]
        a_nat = [sb(f"a_nat{s}", [P, NT, P]) for s in range(STREAMS)]
        keep_l = [sb(f"keep_l{s}", [P, NT, P]) for s in range(STREAMS)]
        next_stage = [sb(f"next_stage{n}", [P, KO, H]) for n in range(2)]
        qv_hi = sb("qv_hi", [P, KO * 2 * TOK], F32R)
        qv_lo = sb("qv_lo", [P, KO * 2 * TOK], F32R)
        v_full = sb("v_full", [P, NT, H])
        score_l = sb("score_l", [P, NT, P])
        score_r = sb("score_r", [P, NT, P])
        prob = sb("prob", [P, NT, P])
        prob_hi = sb("prob_hi", [P, NT, P], F32R)
        prob_lo = sb("prob_lo", [P, NT, P], F32R)
        stats = sb("stats", [P, NT, 6])
        mv = sb("mv", [P, NT, 2])
        var = sb("var", [P, NT])
        sigma = sb("sigma", [P, NT])
        denom = sb("denom", [P, NT])
        rstd = sb("rstd", [P, NT])
        fstats = sb("fstats", [P, NT, 6])
        fmv = sb("fmv", [P, NT, 2])
        offset = sb("offset", [P, NT])
        foffset = [sb(f"foffset{s}", [P, NT]) for s in range(STREAMS)]
        fvar = sb("fvar", [P, NT])
        frstd = [sb(f"frstd{s}", [P, NT]) for s in range(STREAMS)]

        work = [ctx.enter_context(nc.psum_tensor(f"g_work{n}", [P, 512], F32)) for n in range(RING)]

        eye = const[:, C_EYE:C_EYE + P]
        xt_in = [b[:].rearrange("p t h -> p (t h)").rearrange("p (k i) -> p k i", k=KO) for b in x_in]
        q_hi = qv_hi[:].rearrange("p (m t d i) -> p m t d i", m=KO, t=NT, d=2)
        q_lo = qv_lo[:].rearrange("p (m t d i) -> p m t d i", m=KO, t=NT, d=2)
        V0 = KO * 2 * TOK - NT * HC
        assert V0 >= 2 * TOK
        v_hi = qv_hi[:, V0:].rearrange("p (t h) -> p t h", t=NT)
        v_lo = qv_lo[:, V0:].rearrange("p (t h) -> p t h", t=NT)

        stage = [b[:, 0:KO, 0:H] for b in (v_full, z[0], z[1], x_res[0], x_res[1], z[0])]
        weight_halves = [(w_hi[:, l, n], w_lo[:, l, n]) for l in range(LAYERS) for n in range(3)]

        const_in, bias_in = sem("const_in"), sem("bias_in")
        stage_in = [sem(f"stage_in{n}") for n in range(2 * 3)]
        upper_split, first_split, second_split = sem("upper_split"), sem("first_split"), sem("second_split")
        next_stage_in = [sem(f"next_stage_in{n}") for n in range(3)]
        x_split = sem("x_split")
        rows_in, rows_cast = sem("rows_in"), sem("rows_cast")
        next_upper, next_split, next_small = sem("next_upper"), sem("next_split"), sem("next_small")
        x_loaded = [sem(f"x_loaded{s}") for s in range(STREAMS)]
        res_loaded = [sem(f"res_loaded{s}") for s in range(STREAMS)]
        adj_loaded = [sem(f"adj_loaded{s}") for s in range(STREAMS)]
        cleared, powers_set = sem("cleared"), sem("powers_set")
        keep_ready = [sem(f"keep_ready{s}") for s in range(STREAMS)]
        turned, turn_read, ht_ready = sem("turned"), sem("turn_read"), sem("ht_ready")
        work_full, work_free = sem("work_full"), sem("work_free")
        q_hi_ready, score_full, masked, score_ready = sem("q_hi_ready"), sem("score_full"), sem("masked"), sem("score_ready")
        exp_ready, prob_ready, prob_hi_ready, prob_lo_ready = sem("exp_ready"), sem("prob_ready"), sem("prob_hi_ready"), sem("prob_lo_ready")
        v_hi_ready, v_lo_ready, ones_set = sem("v_hi_ready"), sem("v_lo_ready"), sem("ones_set")
        ctx_ready = sem("ctx_ready")
        mean_ready, var_ready, sigma_ready = sem("mean_ready"), sem("var_ready"), sem("sigma_ready")
        denom_ready, rstd_ready, z_ready = sem("denom_ready"), sem("rstd_ready"), sem("z_ready")
        offset_ready, foffset_ready = sem("offset_ready"), sem("foffset_ready")
        gained, scaled, summed, fstats_ready = sem("gained"), sem("scaled"), sem("summed"), sem("fstats_ready")
        fmean_ready, fvar_ready, frstd_ready, x1_ready = sem("fmean_ready"), sem("fvar_ready"), sem("frstd_ready"), sem("x1_ready")
        last_ready = sem("last_ready")

        def query_use(unit, j):
            return unit * WN + (0 if j == 0 else NT + j)

        def value_use(unit, t):
            return unit * WN + NT + QB + t

        def context_use(unit, t):
            return (unit + 1) * WN + 1 + t

        def layer_of(unit):
            return unit % UNITS // STREAMS

        def used(i, use):
            return i * (UNITS * WN) + (use + 1)

        next_rows = next_stage[0][0:NT, :, :].rearrange("r k h -> r (k h)")
        assert C_ALL - C_SEL == KO * H

        block = ctx.enter_context(nc.Block())

        @block.sync
        def _(sp):
            def load_x(i, s):
                sp.dma_start(xt_in[s], x_t_v[i, s]).then_inc(x_loaded[s], 16)

            def load_adj(i, s):
                for b in range(2):
                    h = slice(b * 64, b * 64 + 64)
                    sp.dma_start(a_tr[s][h, :, h], adj_t_v[i, s, b]).then_inc(adj_loaded[s], 16)
                    sp.dma_start(a_nat[s][h, :, h], adj_v[i, s, b]).then_inc(adj_loaded[s], 16)

            def small_loads():
                sp.wait_ge(cleared, 4)
                load_adj(0, 0)
                sp.dma_start(bias[:], b_lin.partition_broadcast(P)).then_inc(bias_in, 16)
                sp.dma_start(gain_f[:], ln_a[0].rearrange("(k p) -> p k", p=P),
                             allow_slow_non_contiguous=True).then_inc(bias_in, 16)
                sp.dma_start(shift_f[:], ln_b[0].rearrange("(k p) -> p k", p=P),
                             allow_slow_non_contiguous=True).then_inc(bias_in, 16)
                sp.dma_start(gain[:], ln_a[1].partition_broadcast(P)).then_inc(bias_in, 16)
                sp.dma_start(shift[:], ln_b[1].partition_broadcast(P)).then_inc(bias_in, 16)
                load_x(0, 1)
                load_adj(0, 1)

            load_x(0, 0)
            weights = [w for l in range(LAYERS) for w in (w_left[l], w_right[l], w_lin_t[l])]
            for n, w in enumerate(weights):
                if n == 1:
                    sp.dma_start(const[:], table[:, 0:C_SEL]).then_inc(const_in, 16)
                if n == 3:
                    small_loads()
                    sp.dma_start(next_rows, table[0:NT, C_SEL:C_ALL]).then_inc(rows_in, 16)
                if n == 5:
                    sp.wait_ge(first_split, 2)
                sp.dma_start(stage[n], w.rearrange("(k p) o -> p k o", p=P)).then_inc(stage_in[n], 16)
            sp.wait_ge(second_split, 3)

            def one_pass(i, last):
                for s in range(STREAMS):
                    wait(sp, summed, i * (STREAMS * NT) + (s + 1 - STREAMS) * NT)
                    sp.dma_start(x_res[s][:], x_v[i, s]).then_inc(res_loaded[s], 16)
                    sp.wait_ge(x_split, (i * STREAMS + s + 1) * KO)
                    if not last:
                        load_x(i + 1, s)
                    else:
                        sp.wait_ge(stored[s], 16 * 2)
                        sp.dma_start(x_in[s][:], x1_v[0, s]).then_inc(sh.x_loaded[s], 16)
                for s in range(STREAMS):
                    sp.wait_ge(prob_ready, nth(i, 2 + s, 1, 0))
                    if not last:
                        load_adj(i + 1, s)
                    else:
                        next_adj(s)
                    if last and s == 0:
                        sp.wait_ge(next_split, 1)
                        next_weights(2)
                    if last and s == STREAMS - 1:
                        half = NT // 2
                        sp.wait_ge(x1_ready, i * (STREAMS * NT) + NT * s + half)
                        sp.dma_start(x1_v[i, s][:, 0:half], z[s][:, 0:half, 0:H]).then_inc(stored[s], 16)
                        sp.wait_ge(last_ready, half)
                        sp.dma_start(x1_v[i, s][:, half:], z[s][:, half:, 0:H]).then_inc(stored[s], 16)
                    else:
                        sp.wait_ge(x1_ready, i * (STREAMS * NT) + NT * (s + 1))
                        sp.dma_start(x1_v[i, s], z[s][:, :, 0:H]).then_inc(stored[s], 16)

            def next_weights(n):
                sp.dma_start(next_stage[n % 2][:], next_w[n][0].rearrange("(k p) o -> p k o", p=P))\
                    .then_inc(next_stage_in[n], 16)

            def next_adj(s):
                for b in range(2):
                    h = slice(b * 64, b * 64 + 64)
                    sp.dma_start(a_tr[s][h, :, h], adj_t_v[0, s, b]).then_inc(sh.adj_loaded[s], 16)

            def next_tables():
                for m in range(3):
                    sp.dma_start(sh.bias[:, m], next_b[m].partition_broadcast(P)).then_inc(next_small, 16)
                sp.dma_start(sh.gain_f[:], next_ln_w[0].rearrange("(k p) -> p k", p=P),
                             allow_slow_non_contiguous=True).then_inc(next_small, 16)
                sp.dma_start(sh.shift_f[:], next_ln_b[0].rearrange("(k p) -> p k", p=P),
                             allow_slow_non_contiguous=True).then_inc(next_small, 16)
                sp.dma_start(sh.gain[:], next_ln_w[1].partition_broadcast(P)).then_inc(next_small, 16)
                sp.dma_start(sh.shift[:], next_ln_b[1].partition_broadcast(P)).then_inc(next_small, 16)

            one_pass(0, False)
            sp.wait_ge(rows_cast, 3)
            next_weights(0)
            next_weights(1)
            next_tables()
            with sp.Fori(1, PASSES - 1) as i:
                one_pass(i, False)
            one_pass(PASSES - 1, True)
            sp.wait_ge(next_small, 16 * 7)
            for s in range(STREAMS):
                sp.wait_ge(sh.x_loaded[s], 16)
                sp.wait_ge(sh.adj_loaded[s], 16 * 2)

        @block.tensor
        def _(pe):
            def turn_block(i, unit, k):
                s = unit - STREAMS
                pe.wait_ge(z_ready, i * (STREAMS * NT) + NT * (s + 1))
                pe.wait_ge(turn_read, nth(i, unit, KO, k - 2))
                bank = turn[(s * KO + k) % 2]
                for t in range(NT):
                    mm = pe.transpose(bank[:, t * P:(t + 1) * P], z[s][:, t, k * P:(k + 1) * P], eye)
                mm.then_inc(turned, 1)

            def work_bank(i, use):
                wait(pe, work_free, used(i, use - RING))
                return work[use % RING]

            def query(i, unit, j):
                layer, s = divmod(unit % UNITS, STREAMS)
                d, m = divmod(j, KO)
                pe.wait_ge((x_split, ht_ready)[layer], (i * STREAMS + unit // UNITS * STREAMS + s + 1) * KO)
                pe.wait_ge((first_split, second_split)[layer], d + 1)
                bank = work_bank(i, query_use(unit, j))
                pairs = [(w[:, layer, d, k, m * P:(m + 1) * P], h[s][:, k, :])
                         for k in range(KO) for w, h in three_products(w_hi, w_lo, ht_hi, ht_lo)]
                for n, (w, h) in enumerate(pairs):
                    mm = pe.matmul(bank[:], w, h, start=(n == 0), stop=(n == len(pairs) - 1))
                return mm

            def scores(i, unit, turn_next):
                s = unit % STREAMS
                pe.wait_ge(work_free, used(i, query_use(unit, QB - 1)))
                wait(pe, score_ready, nth(i, unit, 1, -1))
                for t in range(NT):
                    if t == NT // 2 and turn_next:
                        turn_block(i, unit + 1, 2)
                    pairs = [(h[s][:, m, t * P:(t + 1) * P], q[:, m, t, :, :])
                             for m in range(KO) for h, q in three_products(ht_hi, ht_lo, q_hi, q_lo)]
                    for n, (h, q) in enumerate(pairs):
                        mm = pe.matmul(score_ps[:, t, :, :], h, q, start=(n == 0), stop=(n == len(pairs) - 1))
                mm.then_inc(score_full, 1)

            def value(i, unit, t, uses=1):
                layer, s = divmod(unit % UNITS, STREAMS)
                pe.wait_ge((first_split, second_split)[layer], 3)
                bank = work_bank(i, value_use(unit, t))
                pairs = [(h[s][:, k, t * P:(t + 1) * P], w[:, layer, 2, k, :])
                         for k in range(KO) for h, w in three_products(ht_hi, ht_lo, w_hi, w_lo)]
                for n, (h, w) in enumerate(pairs):
                    mm = pe.matmul(bank[:, 0:H], h, w, start=(n == 0), stop=(n == len(pairs) - 1))
                mm.then_inc(work_full, uses)

            def contexts(i, unit):
                pe.wait_ge(prob_lo_ready, nth(i, unit, 1, 0))
                pe.wait_ge(ones_set, nth(i, unit, 1, 0))
                for t in range(NT):
                    pe.wait_ge(v_lo_ready, nth(i, unit, NT, t))
                    bank = work_bank(i, context_use(unit, t))
                    for n, (p, v) in enumerate(three_products(prob_hi, prob_lo, v_hi, v_lo)):
                        mm = pe.matmul(bank[:, 0:HC], p[:, t, :], v[:, t, :], start=(n == 0), stop=(n == 2))
                    mm.then_inc(work_full, 1)

            def next_turn(k):
                pe.wait_ge(sh.x_loaded[0], 16)
                if k < 2:
                    pe.wait_ge(turn_read, nth(PASSES - 1, UNITS - 1, KO, KO - 1))
                else:
                    pe.wait_ge(sh.turn_read, k - 1)
                for t in range(NT):
                    mm = pe.transpose(turn[k % 2][:, t * P:(t + 1) * P], x_in[0][:, t, k * P:(k + 1) * P], eye)
                mm.then_inc(sh.turned, 1)

            def next_scores():
                pe.wait_ge(rows_cast, 3)
                pe.wait_ge(sh.ht_ready, KO)
                pe.wait_ge(score_ready, nth(PASSES - 1, UNITS - 1, 1, 0))
                symmetric_scores(pe, sh, 0)

            def one_pass(i, last):
                for unit in range(UNITS):
                    more = not (last and unit == UNITS - 1)
                    turn_next = unit < STREAMS
                    for t in range(1, NT):
                        value(i, unit, t, uses=1 if more or t < NT - 1 else 2)
                    if more:
                        query(i, unit + 1, 0).then_inc(work_full, 1)
                    else:
                        next_turn(0)
                        next_turn(1)
                    contexts(i, unit)
                    if more:
                        for j in range(1, QB):
                            query(i, unit + 1, j).then_inc(work_full, 1)
                        value(i, unit + 1, 0)
                    if turn_next:
                        turn_block(i, unit + 2, 0)
                        turn_block(i, unit + 2, 1)
                    if more:
                        scores(i, unit + 1, turn_next)

            pe.wait_ge(const_in, 16)
            query(0, 0, 0).then_inc(work_full, 1 + NT)
            for j in range(1, QB):
                query(0, 0, j).then_inc(work_full, 1)
            value(0, 0, 0)
            scores(0, 0, False)
            with pe.Fori(0, PASSES - 1) as i:
                one_pass(i, False)
            one_pass(PASSES - 1, True)
            next_turn(2)
            next_scores()

        @block.scalar
        def _(act):
            def weight_hi(n):
                act.wait_ge(stage_in[n], 16)
                nc.scalar.activation(weight_halves[n][0], stage[n], ACT.Copy).then_inc(upper_split, 1)

            def next_weight_hi(n):
                act.wait_ge(next_stage_in[n], 16)
                act.wait_ge(work_full, used(PASSES - 1, value_use(STREAMS - 1, NT - 1)))
                nc.scalar.activation(w_hi[:, 0, n], next_stage[n % 2][:], ACT.Copy).then_inc(next_upper, 1)

            def next_turn_out(k):
                act.wait_ge(sh.turned, k + 1)
                act.wait_ge(ht_ready, PASSES * STREAMS * KO)
                nc.scalar.activation(ht_full[:, k, :], turn[k % 2][:], ACT.Copy)
                nc.scalar.activation(ht_hi[0][:, k, :], turn[k % 2][:], ACT.Copy).then_inc(sh.turn_read, 1)

            def turn_out(i, unit, k):
                layer, s = divmod(unit % UNITS, STREAMS)
                if layer == 0:
                    act.wait_ge(x_loaded[s], 16 * (i + unit // UNITS + 1))
                    nc.scalar.activation(ht_hi[s][:, k, :], xt_in[s][:, k, :], ACT.Copy).then_inc(turn_read, 1)
                else:
                    act.wait_ge(turned, (i * STREAMS + s) * KO + k + 1)
                    for out in (ht_full[:, k, :], ht_hi[s][:, k, :]):
                        op = nc.scalar.activation(out, turn[(s * KO + k) % 2][:], ACT.Relu,
                                                  bias=shift_f[:, k:k + 1], scale=gain_f[:, k:k + 1])
                    op.then_inc(turn_read, 1)

            def query_hi(i, unit, j):
                d, m = divmod(j, KO)
                use = query_use(unit, j)
                act.wait_ge(work_full, used(i, use))
                nc.scalar.activation(q_hi[:, m, :, d, :], work[use % RING][:], ACT.Copy).then_inc(q_hi_ready, 1)

            def exponentials(i, unit):
                act.wait_ge(score_ready, nth(i, unit, 1, 0))
                nc.scalar.activation(prob[:], score_l[:], ACT.Exp, scale=SCALE).then_inc(exp_ready, 1)

            def probabilities_hi(i, unit):
                act.wait_ge(prob_ready, nth(i, unit, 1, 0))
                nc.scalar.activation(prob_hi[:], prob[:], ACT.Copy).then_inc(prob_hi_ready, 1)

            def value_hi(i, unit, t):
                act.wait_ge(work_free, used(i, value_use(unit, t)))
                nc.scalar.activation(v_hi[:, t, 0:H], v_full[:, t, :], ACT.Copy).then_inc(v_hi_ready, 1)

            def contexts_out(i, unit):
                layer, s = divmod(unit % UNITS, STREAMS)
                if layer == 0:
                    act.wait_ge(stored[s], 16 * (i + unit // UNITS + 1))
                for t in range(NT):
                    use = context_use(unit, t)
                    act.wait_ge(work_full, used(i, use))
                    nc.scalar.activation(z[s][:, t, :], work[use % RING][:, 0:HC], ACT.Copy).then_inc(ctx_ready, 1)

            def final_normalise(i, s, tiles=NT):
                act.wait_ge(foffset_ready, i * STREAMS + s + 1)
                for t in range(tiles):
                    nc.scalar.activation(z[s][:, t, 0:H], z[s][:, t, 0:H], ACT.Identity, scale=frstd[s][:, t:t + 1],
                                         bias=foffset[s][:, t:t + 1]).then_inc(x1_ready, 1)

            def normalise(i, s):
                act.wait_ge(offset_ready, i * STREAMS + s + 1)
                for t in range(NT):
                    nc.scalar.activation(z[s][:, t, 0:H], z[s][:, t, 0:H], ACT.Identity, scale=rstd[:, t:t + 1],
                                         bias=offset[:, t:t + 1]).then_inc(z_ready, 1)

            def up_to_contexts(i, unit, last):
                more = not (last and unit == UNITS - 1)
                if more and layer_of(unit + 1) == 1:
                    for k in range(KO):
                        turn_out(i, unit + 1, k)
                exponentials(i, unit)
                value_hi(i, unit, 0)
                value_hi(i, unit, 1)
                probabilities_hi(i, unit)
                value_hi(i, unit, 2)
                value_hi(i, unit, 3)
                if more:
                    query_hi(i, unit + 1, 0)
                else:
                    next_turn_out(0)
                    next_turn_out(1)
                contexts_out(i, unit)
                if not more:
                    next_turn_out(2)

            def one_pass(i, last):
                for unit in range(UNITS):
                    more = not (last and unit == UNITS - 1)
                    if more:
                        query_hi(i, unit + 1, 1)
                        query_hi(i, unit + 1, 2)
                    if unit < STREAMS:
                        normalise(i, unit)
                    if more:
                        for j in range(3, QB):
                            query_hi(i, unit + 1, j)
                            if not last and layer_of(unit + 2) == 0:
                                turn_out(i, unit + 2, j - 3)
                        up_to_contexts(i, unit + 1, last)
                    if last:
                        for n in {1: (0,), 2: (1, 2)}.get(unit, ()):
                            next_weight_hi(n)
                    if unit >= STREAMS:
                        final_normalise(i, unit - STREAMS, tiles=NT if more else NT // 2)

            for k in range(KO):
                turn_out(0, 0, k)
            weight_hi(0)
            weight_hi(1)
            weight_hi(2)
            query_hi(0, 0, 0)
            for j in range(1, QB):
                query_hi(0, 0, j)
                if j < 4:
                    weight_hi(j + 2)
            act.wait_ge(bias_in, 16 * 5)
            for k in range(KO):
                turn_out(0, 1, k)
            up_to_contexts(0, 0, False)
            act.wait_ge(rows_in, 16)
            nc.scalar.activation(sh.pick_row[:].rearrange("r t i -> r (t i)"), next_rows[:, 0:TOK], ACT.Copy)\
                .then_inc(rows_cast, 1)
            nc.scalar.activation(sh.block_rows[:], next_rows[0:2, C_ROWS - C_SEL:C_COLS - C_SEL], ACT.Copy)\
                .then_inc(rows_cast, 1)
            nc.scalar.activation(sh.block_cols[:], next_rows[0:2, C_COLS - C_SEL:C_ALL - C_SEL], ACT.Copy)\
                .then_inc(rows_cast, 1)
            with act.Fori(0, PASSES - 1) as i:
                one_pass(i, False)
            one_pass(PASSES - 1, True)

        @block.gpsimd
        def _(pool):
            def weight_lo(n):
                pool.wait_ge(upper_split, n + 1)
                hi, lo = weight_halves[n]
                nc.gpsimd.tensor_tensor(lo, stage[n], hi.bitcast(F32), ALU.subtract).then_inc(second_split, 1)

            def x_lo(i, unit):
                s = unit % UNITS
                for k in range(KO):
                    pool.wait_ge(turn_read, nth(i, unit, KO, k))
                    nc.gpsimd.tensor_tensor(ht_lo[s][:, k, :], xt_in[s][:, k, :], ht_hi[s][:, k, :].bitcast(F32),
                                            ALU.subtract).then_inc(x_split, 1)

            def next_weight_lo(n):
                pool.wait_ge(next_upper, n + 1)
                nc.gpsimd.tensor_tensor(w_lo[:, 0, n], next_stage[n % 2][:], w_hi[:, 0, n].bitcast(F32),
                                        ALU.subtract).then_inc(next_split, 1)

            def keep_masks(i, s):
                pool.wait_ge(adj_loaded[s], 64 * (i + 1))
                tri = [const[:, c:c + P].unsqueeze(1).to_broadcast([P, NT, P]) for c in (C_LE, C_GT)]
                nc.gpsimd.tensor_tensor(keep_l[s][:], a_tr[s][:], tri[0], ALU.mult)
                nc.gpsimd.tensor_tensor(a_nat[s][:], a_nat[s][:], tri[1], ALU.mult).then_inc(keep_ready[s], 1)

            def value_lo(i, unit, t):
                pool.wait_ge(v_hi_ready, nth(i, unit, NT, t))
                nc.gpsimd.tensor_tensor(v_lo[:, t, 0:H], v_full[:, t, :], v_hi[:, t, 0:H].bitcast(F32),
                                        ALU.subtract).then_inc(v_lo_ready, 1)
                if t == 0:
                    nc.gpsimd.memset(v_hi[:, :, H:HC].bitcast(F32), 1.0)
                    nc.gpsimd.memset(v_lo[:, :, H:HC].bitcast(F32), 0.0).then_inc(ones_set, 1)

            def roots(i, unit):
                pool.wait_ge(var_ready, nth(i, unit, 1, 0))
                nc.gpsimd.tensor_tensor(sigma[:], var[:], powers[:, 0, :], ALU.pow).then_inc(sigma_ready, 1)

            def final_roots(i, s):
                pool.wait_ge(fvar_ready, i * STREAMS + s + 1)
                nc.gpsimd.tensor_tensor(frstd[s][:], fvar[:], powers[:, 1, :], ALU.pow).then_inc(frstd_ready, 1)

            def one_pass(i, last):
                for unit in range(UNITS):
                    layer, s = divmod(unit, STREAMS)
                    more = not (last and unit == UNITS - 1)
                    if unit == 0:
                        keep_masks(i, 1)
                    if unit == UNITS - 1 and more:
                        keep_masks(i + 1, 0)
                    if not last and layer_of(unit + 2) == 0:
                        x_lo(i, unit + 2)
                    if more:
                        for t in range(NT):
                            value_lo(i, unit + 1, t)
                    if layer == 1:
                        final_roots(i, s)
                    if more:
                        roots(i, unit + 1)
                    if last:
                        for n in {1: (0,), 2: (1, 2)}.get(unit, ()):
                            next_weight_lo(n)

            for s in range(STREAMS):
                nc.gpsimd.memset(a_tr[s][:], 0.0).then_inc(cleared, 1)
                nc.gpsimd.memset(a_nat[s][:], 0.0).then_inc(cleared, 1)
            nc.gpsimd.memset(powers[:, 0, 0:2], 0.5).then_inc(stored[0], 16)
            nc.gpsimd.memset(powers[:, 0, 2:NT], 0.5).then_inc(stored[1], 16)
            nc.gpsimd.memset(powers[:, 1, 0:2], -0.5).then_inc(work_free, NT)
            nc.gpsimd.memset(powers[:, 1, 2:NT], -0.5).then_inc(powers_set, 1)
            pool.wait_ge(powers_set, 1)
            pool.wait_ge(const_in, 16)
            keep_masks(0, 0)
            for n in range(3, 6):
                weight_lo(n)
            pool.wait_ge(x_split, KO)
            x_lo(0, 1)
            for t in range(NT):
                value_lo(0, 0, t)
            roots(0, 0)
            with pool.Fori(0, PASSES - 1) as i:
                one_pass(i, False)
            one_pass(PASSES - 1, True)

        @block.vector
        def _(dve):
            def weight_lo(n):
                dve.wait_ge(upper_split, n + 1)
                hi, lo = weight_halves[n]
                nc.vector.tensor_tensor(lo, stage[n], hi.bitcast(F32), ALU.subtract).then_inc(first_split, 1)

            def first_x_lo(k):
                dve.wait_ge(turn_read, k + 1)
                nc.vector.tensor_tensor(ht_lo[0][:, k, :], xt_in[0][:, k, :], ht_hi[0][:, k, :].bitcast(F32),
                                        ALU.subtract).then_inc(x_split, 1)

            def turn_lo(i, unit, k):
                s = unit - STREAMS
                dve.wait_ge(turn_read, nth(i, unit, KO, k))
                nc.vector.tensor_tensor(ht_lo[s][:, k, :], ht_full[:, k, :], ht_hi[s][:, k, :].bitcast(F32),
                                        ALU.subtract).then_inc(ht_ready, 1)

            def next_turn_lo(k):
                dve.wait_ge(sh.turn_read, k + 1)
                nc.vector.tensor_tensor(ht_lo[0][:, k, :], ht_full[:, k, :], ht_hi[0][:, k, :].bitcast(F32),
                                        ALU.subtract).then_inc(sh.ht_ready, 1)

            def query_lo(i, unit, j):
                d, m = divmod(j, KO)
                dve.wait_ge(q_hi_ready, nth(i, unit, QB, j))
                bank = work[query_use(unit, j) % RING][:].rearrange("p (t i) -> p t i", t=NT)
                op = nc.vector.tensor_tensor(q_lo[:, m, :, d, :], bank, q_hi[:, m, :, d, :].bitcast(F32),
                                             ALU.subtract)
                op.then_inc(work_free, 1)

            def mask_scores(i, unit):
                s = unit % STREAMS
                dve.wait_ge(score_full, nth(i, unit, 1, 0))
                if unit % UNITS < STREAMS:
                    dve.wait_ge(keep_ready[s], i + unit // UNITS + 1)
                nc.vector.tensor_tensor(score_l[:], score_ps[:, :, 0, :], keep_l[s][:], ALU.mult)
                nc.vector.tensor_tensor(score_r[:], score_ps[:, :, 1, :], a_nat[s][:], ALU.mult).then_inc(masked, 1)
                dve.wait_ge(masked, nth(i, unit, 1, 0))
                nc.vector.tensor_tensor(score_l[:], score_l[:], score_r[:], ALU.add).then_inc(score_ready, 1)

            def probabilities(i, unit):
                s = unit % STREAMS
                dve.wait_ge(exp_ready, nth(i, unit, 1, 0))
                nc.vector.tensor_tensor(prob[:], prob[:], a_tr[s][:], ALU.mult).then_inc(prob_ready, 1)

            def probabilities_lo(i, unit):
                dve.wait_ge(prob_hi_ready, nth(i, unit, 1, 0))
                nc.vector.tensor_tensor(prob_lo[:], prob[:], prob_hi[:].bitcast(F32), ALU.subtract)\
                    .then_inc(prob_lo_ready, 1)

            def biased_value(i, unit, t, uses=1):
                layer = unit % UNITS // STREAMS
                use = value_use(unit, t)
                dve.wait_ge(work_full, used(i, use))
                nc.vector.tensor_tensor(v_full[:, t, :], work[use % RING][:, 0:H],
                                        bias[:, layer, :], ALU.add).then_inc(work_free, uses)

            def context_stats(i, unit, t):
                dve.wait_ge(ctx_ready, nth(i, unit, NT, t))
                nc.vector.bn_stats(stats[:, t, :], work[context_use(unit, t) % RING][:, 0:H])\
                    .then_inc(work_free, 1)

            def variances(i, unit):
                layer, s = divmod(unit, STREAMS)
                dve.wait_ge(work_free, used(i, context_use(unit, NT - 1)))
                nc.vector.tensor_scalar(denom[:], z[s][:, :, H], 1e-10, EPS, ALU.add, ALU.mult)
                for t in range(NT):
                    op = nc.vector.bn_aggr(mv[:, t, :], stats[:, t, :])
                op.then_inc(mean_ready, 1)
                dve.wait_ge(mean_ready, nth(i, unit, 1, 0))
                nc.vector.tensor_scalar(var[:], mv[:, :, 1], float(H) / (H - 1), None, ALU.mult)\
                    .then_inc(var_ready, 1)

            def deviations(i, unit):
                layer = unit // STREAMS
                dve.wait_ge(sigma_ready, nth(i, unit, 1, 0))
                nc.vector.tensor_tensor(denom[:], denom[:], sigma[:], ALU.add).then_inc(denom_ready, 1)
                dve.wait_ge(denom_ready, nth(i, unit, 1, 0))
                nc.vector.reciprocal(rstd[:], denom[:]).then_inc(rstd_ready, 1)
                dve.wait_ge(rstd_ready, nth(i, unit, 1, 0))
                if layer == 0:
                    nc.vector.scalar_tensor_tensor(offset[:], mv[:, :, 0], -1.0, rstd[:], ALU.mult, ALU.mult)\
                        .then_inc(offset_ready, 1)

            def gain_and_shift(i, s, t):
                nc.vector.scalar_tensor_tensor(z[s][:, t, 0:H], z[s][:, t, 0:H], mv[:, t, 0:1], gain[:],
                                               ALU.subtract, ALU.mult).then_inc(gained, 1)
                dve.wait_ge(gained, i * (STREAMS * NT) + s * NT + t + 1)
                nc.vector.scalar_tensor_tensor(z[s][:, t, 0:H], z[s][:, t, 0:H], rstd[:, t:t + 1], shift[:],
                                               ALU.mult, ALU.add).then_inc(scaled, 1)

            def add_residual(i, s):
                dve.wait_ge(res_loaded[s], 16 * (i + 1))
                for t in range(NT):
                    dve.wait_ge(scaled, i * (STREAMS * NT) + s * NT + t + 1)
                    nc.vector.scalar_tensor_tensor(z[s][:, t, 0:H], z[s][:, t, 0:H], 0.0, x_res[s][:, t, :],
                                                   ALU.max, ALU.add).then_inc(summed, 1)

            def final_stats(i, s, t):
                dve.wait_ge(summed, i * (STREAMS * NT) + s * NT + t + 1)
                nc.vector.bn_stats(fstats[:, t, :], z[s][:, t, 0:H]).then_inc(fstats_ready, 1)

            def final_var(i, s):
                dve.wait_ge(fstats_ready, i * (STREAMS * NT) + (s + 1) * NT)
                nc.vector.memset(fvar[:], 1e-5)
                for t in range(NT):
                    op = nc.vector.bn_aggr(fmv[:, t, :], fstats[:, t, :])
                op.then_inc(fmean_ready, 1)
                dve.wait_ge(fmean_ready, i * STREAMS + s + 1)
                nc.vector.tensor_tensor(fvar[:], fvar[:], fmv[:, :, 1], ALU.add).then_inc(fvar_ready, 1)

            def final_offset(i, s):
                dve.wait_ge(frstd_ready, i * STREAMS + s + 1)
                nc.vector.scalar_tensor_tensor(foffset[s][:], fmv[:, :, 0], -1.0, frstd[s][:], ALU.mult, ALU.mult)\
                    .then_inc(foffset_ready, 1)

            def final_normalise(i, s):
                dve.wait_ge(foffset_ready, i * STREAMS + s + 1)
                for t in range(NT // 2, NT):
                    nc.vector.tensor_scalar(z[s][:, t, 0:H], z[s][:, t, 0:H], frstd[s][:, t:t + 1], foffset[s][:, t:t + 1],
                                            ALU.mult, ALU.add).then_inc(last_ready, 1)

            def one_pass(i, last):
                for unit in range(UNITS):
                    more = not (last and unit == UNITS - 1)
                    layer, s = divmod(unit, STREAMS)
                    variances(i, unit)
                    if not more:
                        for k in range(KO):
                            next_turn_lo(k)
                    deviations(i, unit)
                    if more:
                        for j in range(1, QB):
                            query_lo(i, unit + 1, j)
                            if layer == 1 and j > 2:
                                gain_and_shift(i, s, j - 3)
                        if layer == 1:
                            gain_and_shift(i, s, NT - 1)
                        up_to_contexts(i, unit + 1, last, s if layer == 1 else None)
                    else:
                        for t in range(NT):
                            gain_and_shift(i, s, t)
                        add_residual(i, s)
                        for t in range(NT):
                            final_stats(i, s, t)
                        final_var(i, s)
                        final_offset(i, s)
                        final_normalise(i, s)

            def up_to_contexts(i, unit, last, s):
                more = not (last and unit == UNITS - 1)
                turn_next = more and layer_of(unit + 1) == 1
                if turn_next:
                    turn_lo(i, unit + 1, 0)
                biased_value(i, unit, 0)
                if turn_next:
                    turn_lo(i, unit + 1, 1)
                if s is not None:
                    add_residual(i, s)
                if turn_next:
                    turn_lo(i, unit + 1, 2)
                mask_scores(i, unit)
                biased_value(i, unit, 1)
                probabilities(i, unit)
                biased_value(i, unit, 2)
                probabilities_lo(i, unit)
                biased_value(i, unit, 3, uses=1 if more else 2)
                if s is not None:
                    for t in range(NT - 1):
                        final_stats(i, s, t)
                if more:
                    query_lo(i, unit + 1, 0)
                context_stats(i, unit, 0)
                if s is not None:
                    final_stats(i, s, NT - 1)
                context_stats(i, unit, 1)
                if s is not None:
                    final_var(i, s)
                context_stats(i, unit, 2)
                context_stats(i, unit, 3)
                if s is not None:
                    final_offset(i, s)

            for k in range(KO):
                first_x_lo(k)
            weight_lo(0)
            weight_lo(1)
            query_lo(0, 0, 0)
            weight_lo(2)
            for j in range(1, QB):
                query_lo(0, 0, j)
            dve.wait_ge(bias_in, 16 * 5)
            up_to_contexts(0, 0, False, None)
            with dve.Fori(0, PASSES - 1) as i:
                one_pass(i, False)
            one_pass(PASSES - 1, True)


def softmax_layers(nc, sh, x1, adj_t, w_nbr_t, table, out):
    H, KO, HC = sh.H, sh.KO, sh.HC
    const, w_hi, w_lo, x_in, a_tr = sh.const, sh.w_hi, sh.w_lo, sh.x_in, sh.a_tr
    bias, gain_f, shift_f, gain, shift = sh.bias, sh.gain_f, sh.shift_f, sh.gain, sh.shift
    x_loaded, adj_loaded = sh.x_loaded, sh.adj_loaded
    ht, z, ht_full, turn, score_ps, stored = sh.ht, sh.z, sh.ht_full, sh.turn, sh.score_ps, sh.stored
    ht_hi, ht_lo = ([h[:, :, half, :] for h in sh.ht] for half in range(2))
    turned, turn_read, ht_ready, score_full = sh.turned, sh.turn_read, sh.ht_ready, sh.score_full
    pick_row = sh.pick_row
    LAYERS = w_nbr_t[0].shape[0]
    PASSES = x1.shape[0] // (TOK * STREAMS)
    SCALE = float(H) ** -0.5
    SIDES = 3
    VB = NT * SIDES
    WN = VB + NT
    RING = 4
    GT = 3
    LAST_GT = 1
    VF = 4
    assert LAYERS == 2 and WN * UNITS % RING == 0 and UNITS * KO % 2 == 0

    x_v = x1.rearrange("(i s t p) h -> i s p t h", s=STREAMS, t=NT, p=P)
    out_v = out.rearrange("a n h -> (a n) h").rearrange("(i s t p) h -> i s p t h", s=STREAMS, t=NT, p=P)
    adj_t_v = adj_t.rearrange("(i s t b) r c -> i s b r t c", s=STREAMS, t=NT, b=2)

    with ExitStack() as ctx:
        def sb(name, shape, dt=F32):
            return ctx.enter_context(nc.sbuf_tensor("s_" + name, shape, dt))

        def sem(name):
            return ctx.enter_context(nc.semaphore("s_" + name))

        power = sb("power", [P, NT])
        x_res = [sb(f"x_res{s}", [P, NT, H]) for s in range(STREAMS)]
        v_hi = sb("v_hi", [P, NT, 2, HC], F32R)
        v_lo = sb("v_lo", [P, NT, 2, HC], F32R)
        v_full = sb("v_full", [P, VF, H])
        v_own = sb("v_own", [P, NT, H])
        row_max = sb("row_max", [P, NT], F32R)
        exp_bias = sb("exp_bias", [P, NT])
        exp_sum = sb("exp_sum", [P, NT])
        neg_max = sb("neg_max", [NT, P], F32R)
        score = sb("score", [P, NT, P])
        shifted_score = sb("shifted_score", [P, NT, P])
        part = sb("part", [P, NT, P])
        expo = sb("expo", [P, NT, P])
        prob = [sb(f"prob{n}", [P, NT, P]) for n in range(2)]
        prob_hi = [sb(f"prob_hi{n}", [P, NT, P], F32R) for n in range(2)]
        prob_lo = [sb(f"prob_lo{n}", [P, NT, P], F32R) for n in range(2)]
        own = sb("own", [P, NT])
        stats = sb("stats", [P, NT, 6])
        mv = sb("mv", [P, NT, 2])
        total = sb("total", [P, NT])
        var = sb("var", [P, NT])
        rstd = sb("rstd", [P, NT])
        fmv = sb("fmv", [P, NT, 2])
        offset = sb("offset", [P, NT])
        foffset = [sb(f"foffset{s}", [P, NT]) for s in range(STREAMS)]
        fvar = sb("fvar", [P, NT])
        frstd = [sb(f"frstd{s}", [P, NT]) for s in range(STREAMS)]

        work = [ctx.enter_context(nc.psum_tensor(f"s_work{n}", [P, 512], F32)) for n in range(RING)]
        max_ps = turn[0][0:NT, 0:P]

        eye = const[:, C_EYE:C_EYE + P]

        def over_tiles(c):
            return const[:, c:c + P].unsqueeze(1).to_broadcast([P, NT, P])

        stage_in = [sem(f"stage_in{n}") for n in range(SIDES)]
        upper_split, split = sem("upper_split"), sem("split")
        x_copied = [sem(f"x_copied{s}") for s in range(STREAMS)]
        power_set = sem("power_set")
        work_full, work_free = sem("work_full"), sem("work_free")
        max_ready, max_turned = sem("max_ready"), sem("max_turned")
        neg_ready, shifted, exp_ready, sums_ready = sem("neg_ready"), sem("shifted"), sem("exp_ready"), sem("sums_ready")
        prob_ready, prob_hi_ready, prob_lo_ready = sem("prob_ready"), sem("prob_hi_ready"), sem("prob_lo_ready")
        diag_ready, own_ready = sem("diag_ready"), sem("own_ready")
        v_hi_ready, v_lo_ready, bias_ready = sem("v_hi_ready"), sem("v_lo_ready"), sem("bias_ready")
        stats_ready, mean_ready, total_ready, var_ready, rstd_ready, z_ready = (
            sem("stats_ready"), sem("mean_ready"), sem("total_ready"), sem("var_ready"), sem("rstd_ready"), sem("z_ready"))
        offset_ready, foffset_ready = sem("offset_ready"), sem("foffset_ready")
        normed, gained, scaled, summed, fstats_ready = sem("normed"), sem("gained"), sem("scaled"), sem("summed"), sem("fstats_ready")
        fmean_ready, fvar_ready, frstd_ready, out_ready = sem("fmean_ready"), sem("fvar_ready"), sem("frstd_ready"), sem("out_ready")
        last_ready = sem("last_ready")
        squared, part_copied, joined = sem("squared"), sem("part_copied"), sem("joined")
        total_begun, own_gained, own_scaled = sem("total_begun"), sem("own_gained"), sem("own_scaled")

        def value_job(j):
            return divmod(j, SIDES)

        before = [16 * (PASSES + 1 + s) for s in range(STREAMS)]

        def freed(i, unit, j):
            return nth(i, unit, WN, j) + RING

        stage = [b[:, 0:KO, 0:H] for b in (x_res[0], x_res[1], z[1])]

        block = ctx.enter_context(nc.Block())

        @block.sync
        def _(sp):
            def load_x(i, s):
                sp.dma_start(x_in[s][:], x_v[i, s]).then_inc(x_loaded[s], 16)

            def load_adj(i, s):
                for b in range(2):
                    h = slice(b * 64, b * 64 + 64)
                    sp.dma_start(a_tr[s][h, :, h], adj_t_v[i, s, b]).then_inc(adj_loaded[s], 16)

            for s in range(STREAMS):
                sp.wait_ge(stored[s], before[s])
            for n in range(SIDES):
                sp.dma_start(stage[n], w_nbr_t[n][1].rearrange("(k p) o -> p k o", p=P)).then_inc(stage_in[n], 16)
            sp.wait_ge(split, SIDES)

            def one_pass(i, last):
                for s in range(STREAMS):
                    sp.wait_ge(x_loaded[s], 16 * (i + 1))
                    wait(sp, summed, i * (STREAMS * NT) + (s + 1 - STREAMS) * NT)
                    sp.dma_start(x_res[s][:], x_in[s][:]).then_inc(x_copied[s], 16)
                    if not last:
                        sp.wait_ge(turned, nth(i, s, KO, KO - 1))
                        sp.wait_ge(x_copied[s], 16 * (i + 1))
                        load_x(i + 1, s)
                for s in range(STREAMS):
                    if not last:
                        sp.wait_ge(own_ready, nth(i, 2 + s, 1, 0))
                        load_adj(i + 1, s)
                    if last and s == STREAMS - 1:
                        half = NT // 2
                        sp.wait_ge(out_ready, i * (STREAMS * NT) + NT * s + half)
                        sp.dma_start(out_v[i, s][:, 0:half], z[s][:, 0:half, 0:H]).then_inc(stored[s], 16)
                        sp.wait_ge(last_ready, half)
                        sp.dma_start(out_v[i, s][:, half:], z[s][:, half:, 0:H]).then_inc(stored[s], 16)
                    else:
                        sp.wait_ge(out_ready, i * (STREAMS * NT) + NT * (s + 1))
                        sp.dma_start(out_v[i, s], z[s][:, :, 0:H]).then_inc(stored[s], 16)

            one_pass(0, False)
            with sp.Fori(1, PASSES - 1) as i:
                one_pass(i, False)
            one_pass(PASSES - 1, True)
            for s in range(STREAMS):
                sp.wait_ge(stored[s], before[s] + 16 * (PASSES + s))

        @block.tensor
        def _(pe):
            def turn_block(i, unit, k):
                layer, s = divmod(unit % UNITS, STREAMS)
                src = x_in[s] if layer == 0 else z[s]
                if layer == 0:
                    pe.wait_ge(x_loaded[s], i * 16 + 16 * (unit // UNITS + 1))
                else:
                    pe.wait_ge(z_ready, i * (STREAMS * NT) + NT * (s + 1))
                wait(pe, turn_read, nth(i, unit, KO, k - 2))
                bank = turn[(unit * KO + k) % 2]
                for t in range(NT):
                    mm = pe.transpose(bank[:, t * P:(t + 1) * P], src[:, t, k * P:(k + 1) * P], eye)
                mm.then_inc(turned, 1)

            def work_bank(i, unit, j):
                pe.wait_ge(work_free, freed(i, unit, j - RING))
                return work[(unit * WN + j) % RING]

            def scores(i, unit):
                pe.wait_ge(ht_ready, nth(i, unit, KO, KO - 1))
                pe.wait_ge(joined, nth(i, unit, 2, -1))
                symmetric_scores(pe, sh, unit % STREAMS)

            def turn_max(i, unit):
                pe.wait_ge(max_ready, nth(i, unit, 1, 0))
                pe.transpose(max_ps, row_max[:].bitcast(F32), eye).then_inc(max_turned, 1)

            def subtract_max(i, unit):
                pe.wait_ge(neg_ready, nth(i, unit, 1, 0))
                for t in range(NT):
                    mm = pe.matmul(score_ps[:, t, 0, :], pick_row[:, t, :], neg_max[:], start=False,
                                   stop=(t == NT - 1), skip_group_check=True)
                mm.then_inc(shifted, 1)

            def values(i, unit, j):
                layer, s = divmod(unit, STREAMS)
                t, side = value_job(j)
                if layer == 1:
                    pe.wait_ge(split, side + 1)
                bank = work_bank(i, unit, j)
                pairs = [(h[s][:, k, t * P:(t + 1) * P], w[:, layer, side, k, :])
                         for k in range(KO) for h, w in three_products(ht_hi, ht_lo, w_hi, w_lo)]
                for n, (h, w) in enumerate(pairs):
                    mm = pe.matmul(bank[:, 0:H], h, w, start=(n == 0), stop=(n == len(pairs) - 1))
                mm.then_inc(work_full, 1)

            def contexts(i, unit):
                pe.wait_ge(prob_lo_ready, nth(i, unit, 2, 1))
                for t in range(NT):
                    pe.wait_ge(v_lo_ready, nth(i, unit, 2 * NT, 2 * t + 1))
                    bank = work_bank(i, unit, VB + t)
                    pairs = [(p[n][:, t, :], v[:, t, n, :])
                             for n in range(2) for p, v in three_products(prob_hi, prob_lo, v_hi, v_lo)]
                    for n, (p, v) in enumerate(pairs):
                        mm = pe.matmul(bank[:, 0:HC], p, v, start=(n == 0), stop=(n == len(pairs) - 1))
                    mm.then_inc(work_full, 1)

            def one_pass(i, last):
                for unit in range(UNITS):
                    more = not (last and unit == UNITS - 1)
                    values(i, unit, 0)
                    turn_max(i, unit)
                    values(i, unit, 1)
                    values(i, unit, 2)
                    subtract_max(i, unit)
                    values(i, unit, 3)
                    for j in range(4, 7):
                        values(i, unit, j)
                    if more:
                        turn_block(i, unit + 1, 0)
                        turn_block(i, unit + 1, 1)
                    values(i, unit, 7)
                    values(i, unit, 8)
                    if more:
                        turn_block(i, unit + 1, 2)
                    for j in range(9, VB):
                        values(i, unit, j)
                    if more:
                        scores(i, unit + 1)
                    contexts(i, unit)

            with pe.Fori(0, PASSES - 1) as i:
                one_pass(i, False)
            one_pass(PASSES - 1, True)

        @block.scalar
        def _(act):
            def weight_hi(n):
                act.wait_ge(stage_in[n], 16)
                nc.scalar.activation(w_hi[:, 1, n], stage[n], ACT.Copy).then_inc(upper_split, 1)

            def turn_out(i, unit, k):
                layer, s = divmod(unit % UNITS, STREAMS)
                act.wait_ge(turned, nth(i, unit, KO, k))
                wait(act, ht_ready, nth(i, unit, KO, k - KO))
                bank = turn[(unit * KO + k) % 2]
                for out_ in (ht_full[:, k, :], ht_hi[s][:, k, :]):
                    if layer == 0:
                        op = nc.scalar.activation(out_, bank[:], ACT.Copy)
                    else:
                        op = nc.scalar.activation(out_, bank[:], ACT.Relu, bias=shift_f[:, k:k + 1],
                                                  scale=gain_f[:, k:k + 1])
                op.then_inc(turn_read, 1)

            def copy_part(i, unit):
                act.wait_ge(score_full, nth(i, unit, 1, 0))
                nc.scalar.activation(part[:], score_ps[:, :, 1, :], ACT.Copy).then_inc(part_copied, 1)

            def negate_max(i, unit):
                act.wait_ge(max_turned, nth(i, unit, 1, 0))
                nc.scalar.activation(neg_max[:], max_ps, ACT.Copy, scale=-1.0).then_inc(neg_ready, 1)

            def exponential_sums(i, unit):
                act.wait_ge(bias_ready, nth(i, unit, 1, 0))
                for t in range(NT):
                    op = nc.scalar.activation(score[:, t, :], score[:, t, :], ACT.Exp, scale=SCALE,
                                              bias=exp_bias[:, t:t + 1], accum_out=exp_sum[:, t:t + 1])
                op.then_inc(sums_ready, 1)

            def exponentials(i, unit):
                act.wait_ge(joined, nth(i, unit, 2, 1))
                nc.scalar.activation(expo[:], shifted_score[:], ACT.Exp, scale=SCALE).then_inc(exp_ready, 1)

            def probabilities_hi(i, unit):
                for n in range(2):
                    act.wait_ge(prob_ready, nth(i, unit, 2, n))
                    nc.scalar.activation(prob_hi[n][:], prob[n][:], ACT.Copy).then_inc(prob_hi_ready, 1)

            def values_hi(i, unit, t):
                for n in range(2):
                    act.wait_ge(work_free, freed(i, unit, t * SIDES + n))
                    nc.scalar.activation(v_hi[:, t, n, 0:H], v_full[:, (2 * t + n) % VF, :], ACT.Copy)\
                        .then_inc(v_hi_ready, 1)

            def final_normalise(i, s, tiles=NT):
                act.wait_ge(foffset_ready, i * STREAMS + s + 1)
                for t in range(tiles):
                    nc.scalar.activation(z[s][:, t, 0:H], z[s][:, t, 0:H], ACT.Identity, scale=frstd[s][:, t:t + 1],
                                         bias=foffset[s][:, t:t + 1]).then_inc(out_ready, 1)

            def normalise(i, unit, more):
                layer, s = divmod(unit, STREAMS)
                act.wait_ge(offset_ready, nth(i, unit, 1, 0))
                for t in range(NT if layer == 0 else GT if more else LAST_GT):
                    nc.scalar.activation(z[s][:, t, 0:H], z[s][:, t, 0:H], ACT.Identity, scale=rstd[:, t:t + 1],
                                         bias=offset[:, t:t + 1]).then_inc((z_ready, normed)[layer], 1)

            def first_half(i, unit):
                negate_max(i, unit)
                values_hi(i, unit, 0)
                exponentials(i, unit)

            def second_half(i, unit, more):
                values_hi(i, unit, 1)
                probabilities_hi(i, unit)
                if more:
                    turn_out(i, unit + 1, 0)
                    turn_out(i, unit + 1, 1)
                values_hi(i, unit, 2)
                if more:
                    turn_out(i, unit + 1, 2)
                exponential_sums(i, unit)
                values_hi(i, unit, 3)
                if more:
                    copy_part(i, unit + 1)

            def one_pass(i, last):
                for unit in range(UNITS):
                    more = not (last and unit == UNITS - 1)
                    if more:
                        first_half(i, unit + 1)
                    normalise(i, unit, more)
                    if more:
                        second_half(i, unit + 1, not (last and unit == UNITS - 2))
                    if unit >= STREAMS:
                        final_normalise(i, unit - STREAMS, tiles=NT if more else NT // 2)

            copy_part(0, 0)
            first_half(0, 0)
            for n in range(SIDES):
                weight_hi(n)
            second_half(0, 0, True)
            with act.Fori(0, PASSES - 1) as i:
                one_pass(i, False)
            one_pass(PASSES - 1, True)

        @block.gpsimd
        def _(pool):
            def weight_lo(n):
                pool.wait_ge(upper_split, n + 1)
                nc.gpsimd.tensor_tensor(w_lo[:, 1, n], stage[n], w_hi[:, 1, n].bitcast(F32), ALU.subtract)\
                    .then_inc(split, 1)

            def values_lo(i, unit, t):
                for n in range(2):
                    pool.wait_ge(v_hi_ready, nth(i, unit, 2 * NT, 2 * t + n))
                    nc.gpsimd.tensor_tensor(v_lo[:, t, n, 0:H], v_full[:, (2 * t + n) % VF, :],
                                            v_hi[:, t, n, 0:H].bitcast(F32), ALU.subtract).then_inc(v_lo_ready, 1)

            def diagonal(i, unit):
                pool.wait_ge(prob_ready, nth(i, unit, 2, 1))
                nc.gpsimd.tensor_tensor(expo[:], expo[:], over_tiles(C_EYE), ALU.mult).then_inc(diag_ready, 1)

            def roots(i, unit):
                pool.wait_ge(var_ready, nth(i, unit, 1, 0))
                nc.gpsimd.tensor_tensor(rstd[:], var[:], power[:], ALU.pow).then_inc(rstd_ready, 1)

            def final_roots(i, s):
                pool.wait_ge(fvar_ready, i * STREAMS + s + 1)
                nc.gpsimd.tensor_tensor(frstd[s][:], fvar[:], power[:], ALU.pow).then_inc(frstd_ready, 1)

            def gain_and_shift(i, s, t):
                done = i * (STREAMS * GT) + s * GT + t + 1
                pool.wait_ge(normed, done)
                nc.gpsimd.tensor_tensor(z[s][:, t, 0:H], z[s][:, t, 0:H], gain[:], ALU.mult).then_inc(gained, 1)
                pool.wait_ge(gained, done)
                nc.gpsimd.tensor_tensor(z[s][:, t, 0:H], z[s][:, t, 0:H], shift[:], ALU.add).then_inc(scaled, 1)

            def one_pass(i, last):
                for unit in range(UNITS):
                    layer, s = divmod(unit, STREAMS)
                    more = not (last and unit == UNITS - 1)
                    if more:
                        values_lo(i, unit + 1, 0)
                    if layer == 1:
                        for t in range(GT // 2 if more else LAST_GT):
                            gain_and_shift(i, s, t)
                    if more:
                        values_lo(i, unit + 1, 1)
                    if layer == 1 and more:
                        for t in range(GT // 2, GT):
                            gain_and_shift(i, s, t)
                    if more:
                        diagonal(i, unit + 1)
                        values_lo(i, unit + 1, 2)
                        values_lo(i, unit + 1, 3)
                    if layer == 1:
                        final_roots(i, s)
                    if more:
                        roots(i, unit + 1)

            nc.gpsimd.memset(v_hi[:, :, :, H:HC].bitcast(F32), 1.0)
            nc.gpsimd.memset(v_lo[:, :, :, H:HC].bitcast(F32), 0.0)
            nc.gpsimd.memset(power[:], -0.5).then_inc(power_set, 1)
            pool.wait_ge(power_set, 1)
            values_lo(0, 0, 0)
            for n in range(SIDES):
                weight_lo(n)
            values_lo(0, 0, 1)
            diagonal(0, 0)
            values_lo(0, 0, 2)
            values_lo(0, 0, 3)
            roots(0, 0)
            with pool.Fori(0, PASSES - 1) as i:
                one_pass(i, False)
            one_pass(PASSES - 1, True)

        @block.vector
        def _(dve):
            def turn_lo(i, unit, k):
                s = unit % STREAMS
                dve.wait_ge(turn_read, nth(i, unit, KO, k))
                nc.vector.tensor_tensor(ht_lo[s][:, k, :], ht_full[:, k, :], ht_hi[s][:, k, :].bitcast(F32),
                                        ALU.subtract).then_inc(ht_ready, 1)

            def join(i, unit, n):
                nc.vector.tensor_tensor((score, shifted_score)[n][:], score_ps[:, :, 0, :], part[:], ALU.add)\
                    .then_inc(joined, 1)

            def maximum(i, unit):
                dve.wait_ge(part_copied, nth(i, unit, 1, 0))
                join(i, unit, 0)
                dve.wait_ge(joined, nth(i, unit, 2, 0))
                nc.vector.tensor_reduce(row_max[:], score[:], AX.X, ALU.max).then_inc(max_ready, 1)
                dve.wait_ge(max_ready, nth(i, unit, 1, 0))
                nc.vector.tensor_scalar(exp_bias[:], row_max[:].bitcast(F32), -SCALE, None, ALU.mult)\
                    .then_inc(bias_ready, 1)

            def biased_value(i, unit, j):
                layer = unit % UNITS // STREAMS
                t, side = value_job(j)
                dve.wait_ge(work_full, nth(i, unit, WN, j))
                if side < 2:
                    if 2 * t >= VF:
                        dve.wait_ge(v_lo_ready, nth(i, unit, 2 * NT, 2 * t + side - VF))
                    dst = v_full[:, (2 * t + side) % VF, :]
                else:
                    dst = v_own[:, t, :]
                nc.vector.tensor_tensor(dst, work[(unit * WN + j) % RING][:, 0:H], bias[:, side, layer, :],
                                        ALU.add).then_inc(work_free, 1)

            def probabilities(i, unit):
                s = unit % STREAMS
                dve.wait_ge(exp_ready, nth(i, unit, 1, 0))
                if unit % UNITS < STREAMS:
                    dve.wait_ge(adj_loaded[s], 32 * (i + unit // UNITS + 1))
                nc.vector.tensor_tensor(expo[:], expo[:], a_tr[s][:], ALU.mult).then_inc(squared, 1)
                dve.wait_ge(squared, nth(i, unit, 1, 0))
                for n, c in enumerate((C_LT, C_GT)):
                    nc.vector.tensor_tensor(prob[n][:], expo[:], over_tiles(c), ALU.mult).then_inc(prob_ready, 1)

            def own_probability(i, unit):
                dve.wait_ge(diag_ready, nth(i, unit, 1, 0))
                nc.vector.tensor_reduce(own[:], expo[:], AX.X, ALU.add).then_inc(own_ready, 1)

            def probabilities_lo(i, unit):
                for n in range(2):
                    dve.wait_ge(prob_hi_ready, nth(i, unit, 2, n))
                    nc.vector.tensor_tensor(prob_lo[n][:], prob[n][:], prob_hi[n][:].bitcast(F32), ALU.subtract)\
                        .then_inc(prob_lo_ready, 1)

            def contexts_out(i, unit, tiles):
                layer, s = divmod(unit % UNITS, STREAMS)
                if tiles[0] == 0:
                    if layer == 0:
                        dve.wait_ge(stored[s], before[s] + 16 * (i + unit // UNITS))
                    dve.wait_ge(own_ready, nth(i, unit, 1, 0))
                    nc.vector.scalar_tensor_tensor(total[:], exp_sum[:], 1e-10, own[:], ALU.mult, ALU.add)\
                        .then_inc(total_begun, 1)
                    dve.wait_ge(total_begun, nth(i, unit, 1, 0))
                for t in tiles:
                    j = VB + t
                    bank = work[(unit * WN + j) % RING]
                    dve.wait_ge(work_full, nth(i, unit, WN, j))
                    nc.vector.tensor_tensor(total[:, t:t + 1], total[:, t:t + 1], bank[:, H:H + 1], ALU.add)
                    nc.vector.scalar_tensor_tensor(z[s][:, t, 0:H], v_own[:, t, :], own[:, t:t + 1], bank[:, 0:H],
                                                   ALU.mult, ALU.add).then_inc(work_free, 1)
                    dve.wait_ge(work_free, freed(i, unit, j))
                    nc.vector.bn_stats(stats[:, t, :], z[s][:, t, 0:H]).then_inc(stats_ready, 1)

            def variances(i, unit):
                layer, s = divmod(unit, STREAMS)
                dve.wait_ge(stats_ready, nth(i, unit, NT, NT - 1))
                nc.vector.scalar_tensor_tensor(total[:], total[:], 1e-12, total[:], ALU.mult, ALU.mult)\
                    .then_inc(total_ready, 1)
                for t in range(NT):
                    op = nc.vector.bn_aggr(mv[:, t, :], stats[:, t, :])
                op.then_inc(mean_ready, 1)
                dve.wait_ge(total_ready, nth(i, unit, 1, 0))
                dve.wait_ge(mean_ready, nth(i, unit, 1, 0))
                nc.vector.tensor_tensor(var[:], mv[:, :, 1], total[:], ALU.add).then_inc(var_ready, 1)

            def deviations(i, unit):
                dve.wait_ge(rstd_ready, nth(i, unit, 1, 0))
                nc.vector.scalar_tensor_tensor(offset[:], mv[:, :, 0], -1.0, rstd[:], ALU.mult, ALU.mult)\
                    .then_inc(offset_ready, 1)

            def gain_and_shift(i, s, first=GT):
                for t in range(first, NT):
                    nc.vector.scalar_tensor_tensor(z[s][:, t, 0:H], z[s][:, t, 0:H], mv[:, t, 0:1], gain[:],
                                                   ALU.subtract, ALU.mult).then_inc(own_gained, 1)
                for t in range(first, NT):
                    dve.wait_ge(own_gained, (i * STREAMS + s) * (NT - GT) + t - first + 1)
                    nc.vector.scalar_tensor_tensor(z[s][:, t, 0:H], z[s][:, t, 0:H], rstd[:, t:t + 1], shift[:],
                                                   ALU.mult, ALU.add).then_inc(own_scaled, 1)

            def add_residual(i, s, first=GT):
                dve.wait_ge(x_copied[s], 16 * (i + 1))
                for t in range(NT):
                    if t < first:
                        dve.wait_ge(scaled, (i * STREAMS + s) * GT + t + 1)
                    else:
                        dve.wait_ge(own_scaled, (i * STREAMS + s) * (NT - GT) + t - first + 1)
                    nc.vector.scalar_tensor_tensor(z[s][:, t, 0:H], z[s][:, t, 0:H], 0.0, x_res[s][:, t, :],
                                                   ALU.max, ALU.add).then_inc(summed, 1)

            def final_stats(i, s):
                for t in range(NT):
                    dve.wait_ge(summed, i * (STREAMS * NT) + s * NT + t + 1)
                    nc.vector.bn_stats(stats[:, t, :], z[s][:, t, 0:H]).then_inc(fstats_ready, 1)

            def final_var(i, s):
                dve.wait_ge(fstats_ready, i * (STREAMS * NT) + (s + 1) * NT)
                nc.vector.memset(fvar[:], 1e-5)
                for t in range(NT):
                    op = nc.vector.bn_aggr(fmv[:, t, :], stats[:, t, :])
                op.then_inc(fmean_ready, 1)
                dve.wait_ge(fmean_ready, i * STREAMS + s + 1)
                nc.vector.tensor_tensor(fvar[:], fvar[:], fmv[:, :, 1], ALU.add).then_inc(fvar_ready, 1)

            def final_offset(i, s):
                dve.wait_ge(frstd_ready, i * STREAMS + s + 1)
                nc.vector.scalar_tensor_tensor(foffset[s][:], fmv[:, :, 0], -1.0, frstd[s][:], ALU.mult, ALU.mult)\
                    .then_inc(foffset_ready, 1)

            def final_normalise(i, s):
                dve.wait_ge(foffset_ready, i * STREAMS + s + 1)
                for t in range(NT // 2, NT):
                    nc.vector.tensor_scalar(z[s][:, t, 0:H], z[s][:, t, 0:H], frstd[s][:, t:t + 1], foffset[s][:, t:t + 1],
                                            ALU.mult, ALU.add).then_inc(last_ready, 1)

            def up_to_contexts(i, unit, last, s):
                more = not (last and unit == UNITS - 1)
                dve.wait_ge(shifted, nth(i, unit, 1, 0))
                join(i, unit, 1)
                biased_value(i, unit, 3)
                biased_value(i, unit, 4)
                probabilities(i, unit)
                if s is not None:
                    gain_and_shift(i, s)
                biased_value(i, unit, 5)
                biased_value(i, unit, 6)
                if more:
                    turn_lo(i, unit + 1, 0)
                probabilities_lo(i, unit)
                if more:
                    turn_lo(i, unit + 1, 1)
                biased_value(i, unit, 7)
                biased_value(i, unit, 8)
                if more:
                    turn_lo(i, unit + 1, 2)
                if s is not None:
                    add_residual(i, s)
                biased_value(i, unit, 9)
                biased_value(i, unit, 10)
                if s is not None:
                    final_stats(i, s)
                    final_var(i, s)
                own_probability(i, unit)
                biased_value(i, unit, 11)
                dve.wait_ge(sums_ready, nth(i, unit, 1, 0))
                contexts_out(i, unit, (0,))
                if more:
                    maximum(i, unit + 1)
                    if s is not None:
                        final_offset(i, s)
                contexts_out(i, unit, range(1, NT))
                if s is not None and not more:
                    final_offset(i, s)

            def one_pass(i, last):
                for unit in range(UNITS):
                    layer, s = divmod(unit, STREAMS)
                    variances(i, unit)
                    if not (last and unit == UNITS - 1):
                        for j in range(SIDES):
                            biased_value(i, unit + 1, j)
                    deviations(i, unit)
                    if not (last and unit == UNITS - 1):
                        up_to_contexts(i, unit + 1, last, s if layer == 1 else None)
                    else:
                        gain_and_shift(i, s, LAST_GT)
                        add_residual(i, s, LAST_GT)
                        final_stats(i, s)
                        final_var(i, s)
                        final_offset(i, s)
                        final_normalise(i, s)

            nc.vector.memset(own[:], 0.0).then_inc(work_free, RING)
            maximum(0, 0)
            for j in range(SIDES):
                biased_value(0, 0, j)
            up_to_contexts(0, 0, False, None)
            with dve.Fori(0, PASSES - 1) as i:
                one_pass(i, False)
            one_pass(PASSES - 1, True)


def resnorm_graph_blocks(nc, x, x_t, adj, adj_t, w, table, out):
    B, S, H = x.shape
    assert S == P // 2 and H % P == 0 and B * S % (TOK * STREAMS) == 0
    x1 = nc.dram_tensor("x1", (B * S, H), F32).ap()
    second = ([w["L1_gnn_Wl"], w["L1_gnn_Wr"], w["L1_gnn_Ws"]], [w["L1_gnn_bl"], w["L1_gnn_br"], w["L1_gnn_bs"]],
              w["L1_gnn_ln_w"], w["L1_gnn_ln_b"])
    with ExitStack() as ctx:
        sh = Shared(nc, ctx, H, w["L0_gnn_W_left"].shape[0])
        gated_layers(nc, sh, x, x_t, adj, adj_t, w["L0_gnn_W_left"], w["L0_gnn_W_right"], w["L0_gnn_W_lin"],
                     w["L0_gnn_b_lin"], w["L0_gnn_ln_a"], w["L0_gnn_ln_b"], table, x1, *second)
        softmax_layers(nc, sh, x1, adj_t, second[0], table, out)


_TURNED = ["L0_gnn_W_lin", "L1_gnn_Wl", "L1_gnn_Wr", "L1_gnn_Ws"]
_STRAIGHT = ["L0_gnn_W_left", "L0_gnn_W_right", "L0_gnn_b_lin", "L0_gnn_ln_a", "L0_gnn_ln_b",
             "L1_gnn_bl", "L1_gnn_bs", "L1_gnn_br", "L1_gnn_ln_w", "L1_gnn_ln_b"]


def kernel(**inputs):
    import numpy as _np
    import concourse.bacc as _bacc
    from concourse import mybir as _mybir
    from concourse.bass_utils import run_bass_kernel_spmd as _run

    host = {n: _np.ascontiguousarray(inputs[n]) for n in ["x", "adj"] + _STRAIGHT}
    host["adj_t"] = _np.ascontiguousarray(_np.transpose(_np.asarray(inputs["adj"]), (0, 2, 1)))
    for n in _TURNED:
        host[n] = _np.ascontiguousarray(_np.transpose(_np.asarray(inputs[n]), (0, 2, 1)))
    host["x_t"] = _np.ascontiguousarray(host["x"].reshape(-1, host["x"].shape[2]).T)
    host["table"] = constants_table()

    nc = _bacc.Bacc("TRN2", target_bir_lowering=False, num_devices=1)
    ap = {n: nc.dram_tensor(f"in_{n}", a.shape, _mybir.dt.from_np(a.dtype), kind="ExternalInput").ap()
          for n, a in host.items()}
    out = nc.dram_tensor("out_0", host["x"].shape, F32, kind="ExternalOutput").ap()
    resnorm_graph_blocks(nc, ap["x"], ap["x_t"], ap["adj"], ap["adj_t"], ap, ap["table"], out)
    r = _run(nc, [{f"in_{n}": a for n, a in host.items()}], core_ids=[0])
    return r.results[0]["out_0"]
```
